# Optimizing a Trainium2 kernel written in Bass

```python
import numpy as np
import jax
import jax.numpy as jnp

def _softmax(x, axis=-1):
    return jax.nn.softmax(x, axis=axis)
def _gelu(x):
    return jax.nn.gelu(x, approximate=True)
def _silu(x):
    return jax.nn.silu(x)
def _sigmoid(x):
    return jax.nn.sigmoid(x)
def _layernorm(x, axis=-1, eps=1e-5):
    m = jnp.mean(x, axis=axis, keepdims=True)
    v = jnp.var(x, axis=axis, keepdims=True)
    return (x - m) / jnp.sqrt(v + eps)
def _scatter_add(tgt, idx, src, axis=0):
    return tgt.at[idx].add(src)
def _segment_sum(src, seg, n):
    return jax.ops.segment_sum(src, seg, n)

kernel_name = 'mk_conv_preact_d4_conv_nhwc1024_f3d105'

def setup_inputs(seed: int = 0):
    np.random.seed(seed)
    _w = jnp.asarray
    def _rec_inputs():
        import jax
        import jax.numpy as jnp
        _gk = jax.random.key(seed)
        x = -0.000929 + 1 * jax.random.normal(jax.random.fold_in(_gk, 1), (4, 16, 16, 1024), jnp.float32)
        return x
    x = _rec_inputs()
    def _L0_conv_setup():
        import jax, jax.numpy as jnp
        import numpy as np
        BN_EPS = 0.001

        def _bn(x, gamma, beta, mean, var):
            return (x - mean) * (gamma * jax.lax.rsqrt(var + BN_EPS)) + beta

        def _rel_pos_idx(n):
            ii, jj = np.meshgrid(np.arange(n), np.arange(n), indexing='ij')
            pos = np.stack([ii.reshape(-1), jj.reshape(-1)], axis=-1)
            rel = pos[None, :, :] - pos[:, None, :] + (n - 1)
            return jnp.asarray(rel, dtype=jnp.int32)
        key = jax.random.key(seed)
        ks = jax.random.split(key, 13)
        b, hh, ww, c = (4, 16, 16, 1024)
        heads, dim_k, dim_u, dim_out = (4, 256, 1, 1024)
        dim_v = dim_out // heads
        n = hh
        rel_len = 2 * n - 1
        inp = {'x': jax.random.normal(ks[0], (b, hh, ww, c), jnp.float32), 'Wq': jax.random.normal(ks[1], (c, dim_k * heads), jnp.float32) * 0.02, 'Wk': jax.random.normal(ks[2], (c, dim_k * dim_u), jnp.float32) * 0.02, 'Wv': jax.random.normal(ks[3], (c, dim_v * dim_u), jnp.float32) * 0.02, 'q_gamma': jax.random.normal(ks[4], (dim_k * heads,), jnp.float32), 'q_beta': jax.random.normal(ks[5], (dim_k * heads,), jnp.float32), 'q_mean': jax.random.normal(ks[6], (dim_k * heads,), jnp.float32), 'q_var': jax.random.uniform(ks[7], (dim_k * heads,), jnp.float32, 0.5, 1.5), 'v_gamma': jax.random.normal(ks[8], (dim_v * dim_u,), jnp.float32), 'v_beta': jax.random.normal(ks[9], (dim_v * dim_u,), jnp.float32), 'v_mean': jax.random.normal(ks[10], (dim_v * dim_u,), jnp.float32), 'v_var': jax.random.uniform(ks[11], (dim_v * dim_u,), jnp.float32, 0.5, 1.5), 'rel_pos_emb': jax.random.normal(ks[12], (rel_len, rel_len, dim_k, dim_u), jnp.float32) * 0.05}
        return inp
    _L0_conv_all = _L0_conv_setup()
    _L0_conv_in = {k: v for k, v in _L0_conv_all.items() if k in ('Wq', 'Wk', 'Wv', 'q_gamma', 'q_beta', 'q_mean', 'q_var', 'v_gamma', 'v_beta', 'v_mean', 'v_var', 'rel_pos_emb', )}
    del _L0_conv_all

    def _L1_conv_setup():
        import jax, jax.numpy as jnp
        import numpy as np
        EMBED_DIM = 1024
        NUM_HEADS = 16
        LB_HEADS = 8
        LA_HEADS = 8
        HEAD_DIM = EMBED_DIM // NUM_HEADS

        def _masked_attention(xf, Wq, Wk, Wv, lookahead):
            q = jnp.einsum('bnd,hed->bhne', xf, Wq)
            k = jnp.einsum('bnd,hed->bhne', xf, Wk)
            v = jnp.einsum('bnd,hed->bhne', xf, Wv)
            scale = 1.0 / jnp.sqrt(jnp.asarray(q.shape[-1], q.dtype))
            s = jnp.einsum('bhqe,bhke->bhqk', q, k) * scale
            n = s.shape[-1]
            i = jnp.arange(n)
            mask = i[:, None] <= i[None, :] if lookahead else i[:, None] >= i[None, :]
            s = jnp.where(mask, s, jnp.finfo(s.dtype).min)
            p = jax.nn.softmax(s, axis=-1)
            return jnp.einsum('bhqk,bhke->bhqe', p, v)
        key = jax.random.key(seed)
        ks = jax.random.split(key, 8)
        B, T, F, D = (2, 16, 128, EMBED_DIM)

        def xavier(k, shape):
            fan_out, fan_in = (shape[-2], shape[-1])
            lim = float(np.sqrt(6.0 / (fan_in + fan_out)))
            return jax.random.uniform(k, shape, jnp.float32, -lim, lim)
        return {'x': jax.random.normal(ks[0], (B, T, F, D), jnp.float32), 'Wq_lb': xavier(ks[1], (LB_HEADS, HEAD_DIM, D)), 'Wk_lb': xavier(ks[2], (LB_HEADS, HEAD_DIM, D)), 'Wv_lb': xavier(ks[3], (LB_HEADS, HEAD_DIM, D)), 'Wq_la': xavier(ks[4], (LA_HEADS, HEAD_DIM, D)), 'Wk_la': xavier(ks[5], (LA_HEADS, HEAD_DIM, D)), 'Wv_la': xavier(ks[6], (LA_HEADS, HEAD_DIM, D)), 'Wo': xavier(ks[7], (D, D))}
    _L1_conv_all = _L1_conv_setup()
    _L1_conv_in = {k: v for k, v in _L1_conv_all.items() if k in ('Wq_lb', 'Wk_lb', 'Wv_lb', 'Wq_la', 'Wk_la', 'Wv_la', 'Wo', )}
    del _L1_conv_all

    def _L2_conv_setup():
        import jax, jax.numpy as jnp
        import numpy as np
        NUM_HEADS = 16
        key = jax.random.key(seed)
        ks = jax.random.split(key, 7)
        B, H, W, C = (4, 56, 28, 1024)
        hd = C // NUM_HEADS
        return {'hidden_states': jax.random.normal(ks[0], (B, H, W, C), jnp.float32), 'qkv_w': jax.random.normal(ks[1], (C, 3 * C), jnp.float32) * 0.02, 'qkv_b': jax.random.normal(ks[2], (3 * C,), jnp.float32) * 0.02, 'proj_w': jax.random.normal(ks[3], (C, C), jnp.float32) * 0.02, 'proj_b': jax.random.normal(ks[4], (C,), jnp.float32) * 0.02, 'rel_pos_h': jax.random.normal(ks[5], (2 * H - 1, hd), jnp.float32) * 0.02, 'rel_pos_w': jax.random.normal(ks[6], (2 * W - 1, hd), jnp.float32) * 0.02}
    _L2_conv_all = _L2_conv_setup()
    _L2_conv_in = {k: v for k, v in _L2_conv_all.items() if k in ('qkv_w', 'qkv_b', 'proj_w', 'proj_b', 'rel_pos_h', 'rel_pos_w', )}
    del _L2_conv_all

    def _L3_conv_setup():
        import jax, jax.numpy as jnp
        import numpy as np
        from jax import lax
        INP_MODES = (4, 8, 8, 4)
        OUT_MODES = (4, 8, 8, 4)
        RANKS = (1, 8, 8, 8, 1)
        WINDOW = (3, 3)

        def tt_conv(x, filters, cores, bias):
            B, H, W, C = x.shape
            r0 = filters.shape[3]
            tmp = x.transpose(0, 3, 1, 2).reshape(B * C, H, W, 1)
            tmp = lax.conv_general_dilated(tmp, filters, window_strides=(1, 1), padding='SAME', dimension_numbers=('NHWC', 'HWIO', 'NHWC'))
            h, w = (tmp.shape[1], tmp.shape[2])
            tmp = tmp.reshape(B, C, h, w, r0).transpose(4, 1, 0, 2, 3)
            for i in range(len(cores)):
                tmp = tmp.reshape(RANKS[i] * INP_MODES[i], -1)
                tmp = cores[i] @ tmp
                tmp = tmp.reshape(OUT_MODES[i], -1).T
            M = int(np.prod(OUT_MODES))
            out = tmp.reshape(-1, h, w, M) + bias
            return jax.nn.relu(out)
        key = jax.random.key(seed)
        ks = jax.random.split(key, 7)
        d = {}
        d['x'] = jax.random.normal(ks[0], (16, 32, 32, 1024), jnp.float32)
        d['filters'] = jax.random.normal(ks[1], (WINDOW[0], WINDOW[1], 1, RANKS[0]), jnp.float32) * (1.0 / 3.0)
        for i in range(4):
            shp = (OUT_MODES[i] * RANKS[i + 1], RANKS[i] * INP_MODES[i])
            d[f'core{i}'] = jax.random.normal(ks[2 + i], shp, jnp.float32) * (1.0 / np.sqrt(shp[1]).astype(np.float32))
        d['bias'] = jnp.zeros((int(np.prod(OUT_MODES)),), jnp.float32)
        return d
    _L3_conv_all = _L3_conv_setup()
    _L3_conv_in = {k: v for k, v in _L3_conv_all.items() if k in ('filters', 'core0', 'core1', 'core2', 'core3', 'bias', )}
    del _L3_conv_all

    return {
        "x": x,
        "L0_conv_Wq": _L0_conv_in["Wq"],
        "L0_conv_Wk": _L0_conv_in["Wk"],
        "L0_conv_Wv": _L0_conv_in["Wv"],
        "L0_conv_q_gamma": _L0_conv_in["q_gamma"],
        "L0_conv_q_beta": _L0_conv_in["q_beta"],
        "L0_conv_q_mean": _L0_conv_in["q_mean"],
        "L0_conv_q_var": _L0_conv_in["q_var"],
        "L0_conv_v_gamma": _L0_conv_in["v_gamma"],
        "L0_conv_v_beta": _L0_conv_in["v_beta"],
        "L0_conv_v_mean": _L0_conv_in["v_mean"],
        "L0_conv_v_var": _L0_conv_in["v_var"],
        "L0_conv_rel_pos_emb": _L0_conv_in["rel_pos_emb"],
        "L1_conv_Wq_lb": _L1_conv_in["Wq_lb"],
        "L1_conv_Wk_lb": _L1_conv_in["Wk_lb"],
        "L1_conv_Wv_lb": _L1_conv_in["Wv_lb"],
        "L1_conv_Wq_la": _L1_conv_in["Wq_la"],
        "L1_conv_Wk_la": _L1_conv_in["Wk_la"],
        "L1_conv_Wv_la": _L1_conv_in["Wv_la"],
        "L1_conv_Wo": _L1_conv_in["Wo"],
        "L2_conv_qkv_w": _L2_conv_in["qkv_w"],
        "L2_conv_qkv_b": _L2_conv_in["qkv_b"],
        "L2_conv_proj_w": _L2_conv_in["proj_w"],
        "L2_conv_proj_b": _L2_conv_in["proj_b"],
        "L2_conv_rel_pos_h": _L2_conv_in["rel_pos_h"],
        "L2_conv_rel_pos_w": _L2_conv_in["rel_pos_w"],
        "L3_conv_filters": _L3_conv_in["filters"],
        "L3_conv_core0": _L3_conv_in["core0"],
        "L3_conv_core1": _L3_conv_in["core1"],
        "L3_conv_core2": _L3_conv_in["core2"],
        "L3_conv_core3": _L3_conv_in["core3"],
        "L3_conv_bias": _L3_conv_in["bias"],
    }

def reference(x, L0_conv_Wq, L0_conv_Wk, L0_conv_Wv, L0_conv_q_gamma, L0_conv_q_beta, L0_conv_q_mean, L0_conv_q_var, L0_conv_v_gamma, L0_conv_v_beta, L0_conv_v_mean, L0_conv_v_var, L0_conv_rel_pos_emb, L1_conv_Wq_lb, L1_conv_Wk_lb, L1_conv_Wv_lb, L1_conv_Wq_la, L1_conv_Wk_la, L1_conv_Wv_la, L1_conv_Wo, L2_conv_qkv_w, L2_conv_qkv_b, L2_conv_proj_w, L2_conv_proj_b, L2_conv_rel_pos_h, L2_conv_rel_pos_w, L3_conv_filters, L3_conv_core0, L3_conv_core1, L3_conv_core2, L3_conv_core3, L3_conv_bias):
    import jax
    import jax.numpy as jnp
    def _L0_conv_ref(x, Wq, Wk, Wv, q_gamma, q_beta, q_mean, q_var, v_gamma, v_beta, v_mean, v_var, rel_pos_emb):
        import jax, jax.numpy as jnp
        import numpy as np
        BN_EPS = 0.001

        def _bn(x, gamma, beta, mean, var):
            return (x - mean) * (gamma * jax.lax.rsqrt(var + BN_EPS)) + beta

        def _rel_pos_idx(n):
            ii, jj = np.meshgrid(np.arange(n), np.arange(n), indexing='ij')
            pos = np.stack([ii.reshape(-1), jj.reshape(-1)], axis=-1)
            rel = pos[None, :, :] - pos[:, None, :] + (n - 1)
            return jnp.asarray(rel, dtype=jnp.int32)
        b, hh, ww, c = x.shape
        heads, dim_u = (4, 1)
        dim_k = rel_pos_emb.shape[2]
        dim_v = Wv.shape[1] // dim_u
        m = hh * ww
        q = jnp.einsum('bhwc,cd->bhwd', x, Wq)
        k = jnp.einsum('bhwc,cd->bhwd', x, Wk)
        v = jnp.einsum('bhwc,cd->bhwd', x, Wv)
        q = _bn(q, q_gamma, q_beta, q_mean, q_var)
        v = _bn(v, v_gamma, v_beta, v_mean, v_var)
        q = q.reshape(b, heads, dim_v, m)
        k = k.reshape(b, dim_u, dim_v, m)
        v = v.reshape(b, dim_u, dim_v, m)
        k = jax.nn.softmax(k, axis=-1)
        Lc = jnp.einsum('bukm,buvm->bkv', k, v)
        Yc = jnp.einsum('bhkn,bkv->bnhv', q, Lc)
        rel_pos = _rel_pos_idx(hh)
        rel = rel_pos_emb[rel_pos[..., 0], rel_pos[..., 1]]
        Lp = jnp.einsum('nmku,buvm->bnkv', rel, v)
        Yp = jnp.einsum('bhkn,bnkv->bnhv', q, Lp)
        Y = Yc + Yp
        return Y.reshape(b, hh, ww, heads * dim_v)

    def _L1_conv_ref(x, Wq_lb, Wk_lb, Wv_lb, Wq_la, Wk_la, Wv_la, Wo):
        import jax, jax.numpy as jnp
        import numpy as np
        EMBED_DIM = 1024
        NUM_HEADS = 16
        LB_HEADS = 8
        LA_HEADS = 8
        HEAD_DIM = EMBED_DIM // NUM_HEADS

        def _masked_attention(xf, Wq, Wk, Wv, lookahead):
            q = jnp.einsum('bnd,hed->bhne', xf, Wq)
            k = jnp.einsum('bnd,hed->bhne', xf, Wk)
            v = jnp.einsum('bnd,hed->bhne', xf, Wv)
            scale = 1.0 / jnp.sqrt(jnp.asarray(q.shape[-1], q.dtype))
            s = jnp.einsum('bhqe,bhke->bhqk', q, k) * scale
            n = s.shape[-1]
            i = jnp.arange(n)
            mask = i[:, None] <= i[None, :] if lookahead else i[:, None] >= i[None, :]
            s = jnp.where(mask, s, jnp.finfo(s.dtype).min)
            p = jax.nn.softmax(s, axis=-1)
            return jnp.einsum('bhqk,bhke->bhqe', p, v)
        B, T, F, D = x.shape
        xf = x.reshape(B, T * F, D)
        o_lb = _masked_attention(xf, Wq_lb, Wk_lb, Wv_lb, lookahead=False)
        o_la = _masked_attention(xf, Wq_la, Wk_la, Wv_la, lookahead=True)
        o = jnp.concatenate([o_lb, o_la], axis=1)
        o = o.reshape(B, T * F, D)
        out = jnp.einsum('bnd,od->bno', o, Wo)
        return out.reshape(B, T, F, D)

    def _L2_conv_ref(hidden_states, qkv_w, qkv_b, proj_w, proj_b, rel_pos_h, rel_pos_w):
        import jax, jax.numpy as jnp
        import numpy as np
        NUM_HEADS = 16
        B, H, W, C = hidden_states.shape
        nH = NUM_HEADS
        hd = C // nH
        scale = hd ** (-0.5)
        qkv = hidden_states @ qkv_w + qkv_b
        qkv = qkv.reshape(B, H * W, 3, nH, hd).transpose(2, 0, 3, 1, 4)
        qkv = qkv.reshape(3, B * nH, H * W, hd)
        q, k, v = (qkv[0], qkv[1], qkv[2])
        attn = jnp.einsum('bqc,bkc->bqk', q * scale, k)
        coords_h = jnp.arange(H)[:, None] - jnp.arange(H)[None, :] + (H - 1)
        coords_w = jnp.arange(W)[:, None] - jnp.arange(W)[None, :] + (W - 1)
        Rh = rel_pos_h[coords_h]
        Rw = rel_pos_w[coords_w]
        rq = q.reshape(B * nH, H, W, hd)
        rel_h = jnp.einsum('bhwc,hkc->bhwk', rq, Rh)
        rel_w = jnp.einsum('bhwc,wkc->bhwk', rq, Rw)
        attn = attn.reshape(B * nH, H, W, H, W)
        attn = attn + rel_h[:, :, :, :, None] + rel_w[:, :, :, None, :]
        attn = attn.reshape(B * nH, H * W, H * W)
        attn = jax.nn.softmax(attn, axis=-1)
        out = attn @ v
        out = out.reshape(B, nH, H, W, hd).transpose(0, 2, 3, 1, 4).reshape(B, H, W, C)
        return out @ proj_w + proj_b

    def _L3_conv_ref(x, filters, core0, core1, core2, core3, bias):
        import jax, jax.numpy as jnp
        import numpy as np
        from jax import lax
        INP_MODES = (4, 8, 8, 4)
        OUT_MODES = (4, 8, 8, 4)
        RANKS = (1, 8, 8, 8, 1)
        WINDOW = (3, 3)

        def tt_conv(x, filters, cores, bias):
            B, H, W, C = x.shape
            r0 = filters.shape[3]
            tmp = x.transpose(0, 3, 1, 2).reshape(B * C, H, W, 1)
            tmp = lax.conv_general_dilated(tmp, filters, window_strides=(1, 1), padding='SAME', dimension_numbers=('NHWC', 'HWIO', 'NHWC'))
            h, w = (tmp.shape[1], tmp.shape[2])
            tmp = tmp.reshape(B, C, h, w, r0).transpose(4, 1, 0, 2, 3)
            for i in range(len(cores)):
                tmp = tmp.reshape(RANKS[i] * INP_MODES[i], -1)
                tmp = cores[i] @ tmp
                tmp = tmp.reshape(OUT_MODES[i], -1).T
            M = int(np.prod(OUT_MODES))
            out = tmp.reshape(-1, h, w, M) + bias
            return jax.nn.relu(out)
        return tt_conv(x, filters, [core0, core1, core2, core3], bias)

    def _gn(v, G=32, eps=1e-5):
        B_, H_, W_, C_ = v.shape
        g = v.reshape(B_, H_, W_, G, C_ // G)
        m = jnp.mean(g, axis=(1, 2, 4), keepdims=True)
        s = jnp.var(g, axis=(1, 2, 4), keepdims=True)
        return ((g - m) / jnp.sqrt(s + eps)).reshape(v.shape)

    def _ln_c(v, eps=1e-6):
        m = jnp.mean(v, axis=-1, keepdims=True)
        s = jnp.var(v, axis=-1, keepdims=True)
        return (v - m) / jnp.sqrt(s + eps)

    def _ln_t(v, eps=1e-5):
        m = jnp.mean(v, axis=-1, keepdims=True)
        s = jnp.var(v, axis=-1, keepdims=True)
        return (v - m) / jnp.sqrt(s + eps)

    def _to_tokens(v):
        B_, H_, W_, C_ = v.shape
        return v.reshape(B_, H_ * W_, C_)
    def _from_tokens(t, like):
        return t.reshape(like.shape)

    x = x + _L0_conv_ref(_gn(x), L0_conv_Wq, L0_conv_Wk, L0_conv_Wv, L0_conv_q_gamma, L0_conv_q_beta, L0_conv_q_mean, L0_conv_q_var, L0_conv_v_gamma, L0_conv_v_beta, L0_conv_v_mean, L0_conv_v_var, L0_conv_rel_pos_emb)
    x = x + _L1_conv_ref(_gn(x), L1_conv_Wq_lb, L1_conv_Wk_lb, L1_conv_Wv_lb, L1_conv_Wq_la, L1_conv_Wk_la, L1_conv_Wv_la, L1_conv_Wo)
    x = x + _L2_conv_ref(_gn(x), L2_conv_qkv_w, L2_conv_qkv_b, L2_conv_proj_w, L2_conv_proj_b, L2_conv_rel_pos_h, L2_conv_rel_pos_w)
    x = x + _L3_conv_ref(_gn(x), L3_conv_filters, L3_conv_core0, L3_conv_core1, L3_conv_core2, L3_conv_core3, L3_conv_bias)
    return x


_drawn_inputs = setup_inputs


def setup_inputs(seed=0):
    import zlib

    import numpy as np

    out = dict(_drawn_inputs(seed))
    spreads = {'L3_conv_bias': (0.0, 2.0)}
    factors = {'L2_conv_qkv_w': 8.0,
     'L2_conv_qkv_b': 8.0,
     'L2_conv_proj_w': 8.0,
     'L2_conv_proj_b': 200.0,
     'L2_conv_rel_pos_h': 8.0,
     'L2_conv_rel_pos_w': 8.0,
     'L3_conv_filters': 4.037}
    for name, (base, spread) in spreads.items():
        noise = np.random.default_rng([zlib.crc32(name.encode()), seed]).standard_normal(out[name].shape)
        drawn = base * np.exp(spread * noise) if base else spread * noise
        out[name] = jnp.asarray(drawn.astype(out[name].dtype))
    for name, factor in factors.items():
        out[name] = (out[name] * factor).astype(out[name].dtype)
    return out
```

```python
from contextlib import ExitStack

import numpy as np
import concourse.bass as bass
from concourse import mybir

F32 = mybir.dt.float32
F32R = mybir.dt.float32r
BF16 = mybir.dt.bfloat16
ALU = mybir.AluOpType
ACT = mybir.ActivationFunctionType
AX = mybir.AxisListType.X

P = 128
B = 4
SIDE = 16
N = SIDE * SIDE
T = B * N
C = 1024
CK = C // P
HALF = 512
PAIRS = 8
UNITS = 8
HEADS0 = 4
GROUP = 32
GN_EPS = 1e-5
BN_EPS = 1e-3
OUT_MODES = (4, 8, 8, 4)
RANK = 8
DY = 23
KROWS = 112

HB0 = 2 * 12
HB1 = 2 + 4 * 6 + 16 + 3 * 6 + 4 + 16
HB2 = 2 + 4 * 6 + 8 + 3 * 6 + 4 + 8
HB_TOTAL = HB0 + HB1 + HB2


class Count:

    def __init__(self, sem):
        self.sem, self.n = sem, 0

    def up(self, ins, k=1):
        self.n += k
        ins.then_inc(self.sem, k)
        return self.n


def build(nc, A, out):
    outer = ExitStack()
    with outer:
        names = [0]

        def sem(name):
            names[0] += 1
            return outer.enter_context(nc.semaphore(f"{name}_{names[0]}"))

        def sb(ctx, name, shape, dt=F32):
            names[0] += 1
            return ctx.enter_context(nc.sbuf_tensor(f"{name}_{names[0]}", shape, dt))

        PS = outer.enter_context(nc.psum_tensor("PS", [P, 8, HALF], F32))
        xT = sb(outer, "xT", [P, CK, T])
        ident = sb(outer, "ident", [P, P])
        gmat = sb(outer, "gmat", [P, P])
        identb = sb(outer, "identb", [P, P], BF16)
        maskb = sb(outer, "maskb", [P, 2, P], BF16)
        bn = sb(outer, "bn", [P, 40])
        bias = sb(outer, "bias", [P, 40])
        bst = sb(outer, "bst", [P, CK * B, 6])
        mv = sb(outer, "mv", [P, CK * B, 2])
        st2 = sb(outer, "st2", [P, 64])
        gn = sb(outer, "gn", [P, 6, 32])
        neghalf = sb(outer, "neghalf", [P, 32])
        ttA = sb(outer, "ttA", [32, 256])
        ttB = sb(outer, "ttB", [32, 1024])
        weights = outer.enter_context(ExitStack())
        w_raw = sb(weights, "w_raw", [P, 2, HALF])
        w_hi = sb(weights, "w_hi", [P, 2, HALF], F32R)
        w_lo = sb(weights, "w_lo", [P, 2, HALF], F32R)
        zeros = sb(weights, "zeros", [P, HALF])

        w_landed = [sem("w_landed0"), sem("w_landed1")]
        w_hi_done = sem("w_hi_done")
        w_ready = sem("w_ready")
        w_used = sem("w_used")
        consts_in = sem("consts_in")
        x_in = [sem(f"x_in{c}") for c in range(CK)]

        def w_load(sp, n, s, waits):
            if waits:
                sp.wait_ge(w_ready, n - 1)
            src = A["w"][n] if isinstance(n, int) else A["w"][bass.ds(n, 1)].rearrange("a p n -> p (a n)")
            sp.dma_start(w_raw[:, s, :], src).then_inc(w_landed[s], 16)

        def w_loads(sp, n0, n1):
            if n0 == 0:
                for s in range(2):
                    w_load(sp, s, s, False)
                n0 = 2
            with sp.Fori(n0 // 2, n1 // 2) as i:
                for s in range(2):
                    w_load(sp, 2 * i + s, s, True)

        def w_split(pool, i, s, waits):
            n = 2 * i + s
            pool.wait_ge(w_landed[s], 16 * i + 16)
            if waits:
                pool.wait_ge(w_used, n - 1)
            pool.tensor_tensor(w_hi[:, s, :], w_raw[:, s, :], zeros[:, :], ALU.add).then_inc(w_hi_done, 1)
            pool.wait_ge(w_hi_done, n + 1)
            pool.tensor_tensor(w_lo[:, s, :], w_raw[:, s, :], w_hi[:, s, :].bitcast(F32),
                               ALU.subtract).then_inc(w_ready, 1)

        def w_splits(pool, n0, n1):
            if n0 == 0:
                for s in range(2):
                    w_split(pool, 0, s, False)
                n0 = 2
            with pool.Fori(n0 // 2, n1 // 2) as i:
                for s in range(2):
                    w_split(pool, i, s, True)

        def chunk_product(n, slot, cc, c, rhs_hi, rhs_lo, banks, first, last, cols=HALF):
            if cc == 0:
                nc.tensor.wait_ge(w_ready, n + 1)
            w = slice(cc * P, cc * P + P)
            for k, (wt, x) in enumerate(((w_hi, rhs_hi), (w_hi, rhs_lo), (w_lo, rhs_hi))):
                for h, bank in enumerate(banks):
                    m = nc.tensor.matmul(PS[:, bank, 0:cols], wt[:, slot, w], x[:, c, h * HALF:h * HALF + cols],
                                         start=first and k == 0, stop=last and k == 2)
            if cc == 3:
                m.then_inc(w_used, 1)
            return m

        def block_product(n, rhs_hi, rhs_lo, banks, ready=None):
            for c in range(CK):
                if ready:
                    ready(c)
                m = chunk_product(n + c // 4, (c // 4) % 2, c % 4, c, rhs_hi, rhs_lo, banks, c == 0, c == CK - 1)
            return m

        class Norm:

            def __init__(self):
                self.stats = sem("gn_stats")
                self.aggr = sem("gn_aggr")
                self.step = sem("gn_step")
                self.grouped = sem("gn_grouped")
                self.rstd = sem("gn_rstd")
                self.y = sem("gn_y")
                self.hi = sem("xh_ready")
                self.lo = sem("xl_ready")

            def chunk_stats(self, c):
                for b in range(B):
                    src = xT[:, bass.ds(c, 1), b * N:(b + 1) * N].rearrange("p a n -> p (a n)")
                    dst = bst[:, bass.ds(c * B + b, 1), :].rearrange("p a n -> p (a n)")
                    last = nc.vector.bn_stats(dst, src)
                last.then_inc(self.stats, 1)

            def aggregate(self, c0=0, c1=CK):
                nc.vector.wait_ge(self.stats, c1)
                for k in range(c0 * B, c1 * B):
                    last = nc.vector.bn_aggr(mv[:, k, :], bst[:, k, :])
                last.then_inc(self.aggr, 1)

            def on_vector(self, xh, xl, ytmp, between=None):
                v = nc.vector
                step = Count(self.step)
                v.wait_ge(self.aggr, 1)
                v.tensor_copy(st2[:, 0:32], mv[:, :, 0])
                step.up(v.tensor_tensor(gn[:, 0, :], mv[:, :, 0], mv[:, :, 0], ALU.mult))
                v.wait_ge(self.step, step.n)
                step.up(v.tensor_tensor(st2[:, 32:64], mv[:, :, 1], gn[:, 0, :], ALU.add))
                v.wait_ge(self.grouped, 1)
                step.up(v.tensor_copy(gn[:, 1, :], PS[:, 6, 0:32]))
                v.wait_ge(self.step, step.n)
                step.up(v.tensor_tensor(gn[:, 2, :], gn[:, 1, :], gn[:, 1, :], ALU.mult))
                v.wait_ge(self.step, step.n)
                step.up(v.tensor_tensor(gn[:, 3, :], PS[:, 6, 32:64], gn[:, 2, :], ALU.subtract))
                v.wait_ge(self.step, step.n)
                step.up(v.tensor_scalar(gn[:, 3, :], gn[:, 3, :], 0.0, GN_EPS, ALU.max, ALU.add))
                v.wait_ge(self.rstd, 1)
                step.up(v.scalar_tensor_tensor(gn[:, 5, :], gn[:, 1, :], -1.0, gn[:, 4, :], ALU.mult, ALU.mult))
                v.wait_ge(self.step, step.n)
                for c in range(CK):
                    if between:
                        between(c)
                    if c >= 2:
                        v.wait_ge(self.hi, c - 1)
                        v.wait_ge(self.lo, c - 1)
                    for b in range(B):
                        k = c * B + b
                        last = v.tensor_scalar(ytmp[:, c % 2, b * N:(b + 1) * N], xT[:, c, b * N:(b + 1) * N],
                                               gn[:, 4, k:k + 1], gn[:, 5, k:k + 1], ALU.mult, ALU.add)
                    last.then_inc(self.y, 1)
                    if c >= 1:
                        self.rest(c - 1, xh, xl, ytmp)
                self.rest(CK - 1, xh, xl, ytmp)

            def rest(self, c, xh, xl, ytmp):
                nc.vector.wait_ge(self.y, c + 1)
                nc.vector.wait_ge(self.hi, c + 1)
                nc.vector.tensor_tensor(xl[:, c, :], ytmp[:, c % 2, :], xh[:, c, :].bitcast(F32),
                                        ALU.subtract).then_inc(self.lo, 1)

            def on_scalar(self, xh, ytmp, between=None):
                for c in range(CK):
                    if between:
                        between(c)
                    nc.scalar.wait_ge(self.y, c + 1)
                    nc.scalar.activation(xh[:, c, :], ytmp[:, c % 2, :], ACT.Copy).then_inc(self.hi, 1)

            def on_tensor(self):
                nc.tensor.wait_ge(self.step, 2)
                nc.tensor.matmul(PS[:, 6, 0:64], gmat[:, :], st2[:, :], start=True, stop=True)\
                    .then_inc(self.grouped, 1)

            def on_gpsimd(self):
                nc.gpsimd.wait_ge(self.step, 6)
                nc.gpsimd.tensor_tensor(gn[:, 4, :], gn[:, 3, :], neghalf[:, :], ALU.pow).then_inc(self.rstd, 1)

            def ready(self, c):
                nc.tensor.wait_ge(self.hi, c + 1)
                nc.tensor.wait_ge(self.lo, c + 1)

        norms = [Norm() for _ in range(4)]

        layer0(nc, A, outer, locals())
        layer12(nc, A, outer, locals(), 1)
        layer12(nc, A, outer, locals(), 2)
        weights.close()
        layer3(nc, A, out, outer, locals())


def layer0(nc, A, outer, g):
    PS, xT, zeros, ident, gmat, identb, maskb = (g[x] for x in ("PS", "xT", "zeros", "ident", "gmat", "identb", "maskb"))
    bn, bias, neghalf, ttA, ttB = (g[x] for x in ("bn", "bias", "neghalf", "ttA", "ttB"))
    sem, sb, norms, consts_in, x_in = (g[x] for x in ("sem", "sb", "norms", "consts_in", "x_in"))
    block_product, w_used = g["block_product"], g["w_used"]
    norm = norms[0]
    with ExitStack() as keep:
        Qs = sb(keep, "Qs", [P, 2, B * HEADS0 * N])
        VT = sb(keep, "VT", [P, 2, T])
        ks = sb(keep, "ks", [P, B, 2, N])

        with ExitStack() as ctx:
            xh = sb(ctx, "xh", [P, CK, T], F32R)
            xl = sb(ctx, "xl", [P, CK, T], F32R)
            ytmp = sb(ctx, "ytmp", [P, 2, T])
            qT = sb(ctx, "qT", [P, 2, T])
            KT = sb(ctx, "KT", [P, 2, T])
            bns = sb(ctx, "bns", [P, 4, 10])
            kmax = sb(ctx, "kmax", [P, B, 2])
            ksum = sb(ctx, "ksum", [P, B, 2])
            krec = sb(ctx, "krec", [P, B, 2])
            maskf = sb(ctx, "maskf", [P, 2, P])
            memset_done = sem("memset_done")
            bn_step = sem("bn_step")
            bn_pow = sem("bn_pow")
            vk_evac = sem("vk_evac")
            q_evac = sem("q_evac")
            q_tr = sem("q_tr")
            q_placed = sem("q_placed")
            k_tr = sem("k_tr")
            k_max = sem("k_max")
            k_exp = sem("k_exp")
            k_rec = sem("k_rec")
            k_soft = sem("k_soft")

            with nc.Block() as block:
                @block.sync
                def _(sp):
                    for c in range(0, CK, 2):
                        sp.dma_start(xT[:, c, :], A["x"][c]).then_inc(x_in[c], 16)
                    g["w_loads"](sp, 0, HB0 + 2)

                @block.gpsimd
                def _(pool):
                    nc.gpsimd.memset(zeros[:, :], 0.0).then_inc(memset_done, 1)
                    nc.gpsimd.memset(neghalf[:, :], -0.5).then_inc(memset_done, 1)
                    pool.wait_ge(memset_done, 2)
                    for i in range(1):
                        for s in range(2):
                            g["w_split"](pool, i, s, False)
                    pool.wait_ge(bn_step, 1)
                    nc.gpsimd.tensor_tensor(bns[:, 1, :], bns[:, 0, :], neghalf[:, 0:10], ALU.pow).then_inc(bn_pow, 1)
                    norm.on_gpsimd()
                    g["w_splits"](pool, 2, HB0 + 2)

                @block.vector
                def _(dve):
                    dve.wait_ge(consts_in, 16 * 5)
                    nc.vector.tensor_copy(identb[:, :], ident[:, :]).then_inc(q_placed, 1)
                    nc.vector.tensor_copy(maskb[:, :, :], maskf[:, :, :])
                    nc.vector.tensor_scalar(bns[:, 0, :], bn[:, 30:40], BN_EPS, None, ALU.add).then_inc(bn_step, 1)
                    for c in range(CK):
                        dve.wait_ge(x_in[c], 16)
                        norm.chunk_stats(c)
                    norm.aggregate()
                    dve.wait_ge(bn_pow, 1)
                    nc.vector.tensor_tensor(bns[:, 2, :], bns[:, 1, :], bn[:, 0:10], ALU.mult).then_inc(bn_step, 1)
                    dve.wait_ge(bn_step, 2)
                    nc.vector.tensor_tensor(bns[:, 3, :], bn[:, 20:30], bns[:, 2, :], ALU.mult).then_inc(bn_step, 1)
                    dve.wait_ge(bn_step, 3)
                    nc.vector.tensor_tensor(bns[:, 3, :], bn[:, 10:20], bns[:, 3, :], ALU.subtract).then_inc(bn_step, 1)
                    norm.on_vector(xh, xl, ytmp)

                    def soft_k(b):
                        dve.wait_ge(k_tr, b + 1)
                        nc.vector.tensor_reduce(kmax[:, b, :], PS[:, 6 + b % 2, :].rearrange("p (j m) -> p j m", j=2),
                                                AX, ALU.max, negate=True).then_inc(k_max, 1)
                        dve.wait_ge(k_exp, b + 1)
                        nc.vector.reciprocal(krec[:, b, :], ksum[:, b, :]).then_inc(k_rec, 1)
                        dve.wait_ge(k_rec, b + 1)
                        for jp in range(2):
                            last = nc.vector.tensor_scalar(ks[:, b, jp, :], ks[:, b, jp, :], krec[:, b, jp:jp + 1],
                                                           None, ALU.mult)
                        last.then_inc(k_soft, 1)

                    for b in range(2):
                        soft_k(b)
                    with dve.Fori(0, 2) as jp:
                        for k in range(4):
                            j2, ph = k // 2, k % 2
                            dve.wait_ge(q_tr, 4 * jp + k + 1)
                            for bank in range(2):
                                for h2 in range(2):
                                    src = PS[64 * h2:64 * h2 + 64, 4 + bank, :].rearrange("p (c y x) -> p c y x", c=4, x=SIDE)
                                    dst = Qs[64 * j2:64 * j2 + 64, bass.ds(jp, 1), :]\
                                        .rearrange("p a (x y g h) -> p (a g) y x h", x=SIDE, y=SIDE, h=2)[
                                            :, 4 * bank:4 * bank + 4, 8 * ph:8 * ph + 8, :, h2]
                                    last = nc.vector.tensor_copy(dst, src)
                            last.then_inc(q_placed, 1)
                    for b in range(2, B):
                        soft_k(b)

                @block.scalar
                def _(act):
                    for c in range(1, CK, 2):
                        act.dma_start(xT[:, c, :], A["x"][c]).then_inc(x_in[c], 16)
                    act.dma_start(ident[:, :], A["ident"]).then_inc(consts_in, 16)
                    act.dma_start(gmat[:, :], A["gmat"]).then_inc(consts_in, 16)
                    act.dma_start(maskf[:, :, :], A["mask"].rearrange("a p n -> p a n")).then_inc(consts_in, 16)
                    act.dma_start(bn[:, :], A["bn"]).then_inc(consts_in, 16)
                    act.dma_start(bias[:, :], A["bias"]).then_inc(consts_in, 16)
                    norm.on_scalar(xh, ytmp)
                    act.wait_ge(bn_step, 4)
                    for i, (dst, at) in enumerate(((VT[:, 0, :], 0), (VT[:, 1, :], 2), (KT[:, 0, :], 0), (KT[:, 1, :], 2))):
                        act.wait_ge(w_used, 2 * i + 2)
                        src = PS[:, at:at + 2, :].rearrange("p a n -> p (a n)")
                        if i < 2:
                            ins = nc.scalar.activation(dst, src, ACT.Identity, bias=bns[:, 3, 8 + i:9 + i],
                                                       scale=bns[:, 2, 8 + i:9 + i])
                        else:
                            dst = dst.rearrange("p (b j t) -> p b t j", b=B, j=4)
                            src = src.rearrange("p (b t j) -> p b t j", b=B, j=4)
                            ins = nc.scalar.activation(dst, src, ACT.Copy)
                        ins.then_inc(vk_evac, 1)

                    def exp_k(b):
                        act.wait_ge(k_max, b + 1)
                        for jp in range(2):
                            last = nc.scalar.activation(ks[:, b, jp, :], PS[:, 6 + b % 2, jp * N:jp * N + N], ACT.Exp,
                                                        bias=kmax[:, b, jp:jp + 1], accum_out=ksum[:, b, jp:jp + 1])
                        last.then_inc(k_exp, 1)

                    for b in range(2):
                        exp_k(b)
                    with act.Fori(0, 2) as jp:
                        for k in range(4):
                            n = 4 * jp + k
                            at = 2 * (k % 2)
                            act.wait_ge(w_used, 2 * n + 10)
                            nc.scalar.activation(qT[:, k % 2, :], PS[:, at:at + 2, :].rearrange("p a n -> p (a n)"),
                                                 ACT.Identity, bias=bns[:, 3, bass.ds(n, 1)],
                                                 scale=bns[:, 2, bass.ds(n, 1)]).then_inc(q_evac, 1)
                    for b in range(2, B):
                        exp_k(b)

                @block.tensor
                def _(pe):
                    norm.on_tensor()
                    for i in range(4):
                        if i >= 2:
                            pe.wait_ge(vk_evac, i - 1)
                        block_product(2 * i, xh, xl, (2 * (i % 2), 2 * (i % 2) + 1),
                                      norm.ready if i == 0 else None)

                    def transpose_k(b):
                        for jp in range(2):
                            for mc in range(2):
                                src = KT[:, mc, b * N + jp * P:b * N + jp * P + P]
                                m = nc.tensor.transpose(PS[:, 6 + b % 2, jp * N + mc * P:jp * N + mc * P + P], src, ident[:, :])
                        m.then_inc(k_tr, 1)

                    def transpose_q(n, k):
                        pe.wait_ge(q_evac, n + 1)
                        pe.wait_ge(q_placed, n + 1)
                        for tt in range(8):
                            m = nc.tensor.transpose(PS[:, 4 + tt // 4, (tt % 4) * P:(tt % 4) * P + P],
                                                    qT[:, k % 2, tt * P:tt * P + P], ident[:, :])
                        m.then_inc(q_tr, 1)

                    pe.wait_ge(vk_evac, 4)
                    for b in range(2):
                        transpose_k(b)
                    with pe.Fori(0, 2) as jp:
                        for k in range(4):
                            n = 4 * jp + k
                            if k >= 2:
                                pe.wait_ge(q_evac, n - 1)
                            block_product(8 + 2 * n, xh, xl, (2 * (k % 2), 2 * (k % 2) + 1))
                            if k >= 1:
                                transpose_q(n - 1, k - 1)
                        transpose_q(4 * jp + 3, 3)
                    pe.wait_ge(k_exp, 2)
                    for b in range(2, B):
                        transpose_k(b)

        with ExitStack() as ctx:
            AT = sb(ctx, "AT", [P, 2, B * HEADS0 * N])
            ET = sb(ctx, "ET", [P, 2, 961])
            G = sb(ctx, "G", [P, 2, 8, DY * SIDE])
            A2 = sb(ctx, "A2", [P, 4, 8, N])
            c0 = sb(ctx, "c0", [32, 8, 4, 4])
            c1 = sb(ctx, "c1", [32, 8, 2, 8])
            c2 = sb(ctx, "c2", [32, 8, 8, 8])
            c3 = sb(ctx, "c3", [32, 8, 4, 4])
            tA = sb(ctx, "tA", [32, 256])
            tB = sb(ctx, "tB", [32, 1024])
            et_in = sem("et_in")
            cores_in = sem("cores_in")
            mul_done = sem("mul_done")
            add_done = sem("add_done")
            shifted = [sem(f"shifted{u}") for u in range(4)]
            pe_group = sem("pe_group")
            act_evac = sem("act_evac")
            dve_evac = sem("dve_evac")
            x_sum = sem("x_sum")

            groups = []
            for u in range(4):
                for xi in range(8):
                    groups.append(("G", (u, xi), "act" if xi % 2 else "dve"))
            for b in range(B):
                for mc in range(2):
                    for nh in range(2):
                        groups.append(("K", (b, mc, nh), "act" if nh else "dve"))
            for u in range(4):
                for xg in range(2):
                    for mc in range(2):
                        groups.append(("A", (u, xg, mc), "dve"))
            for b in range(B):
                for vt in range(2):
                    for nh in range(2):
                        groups.append(("Y", (b, vt, nh), "dve"))
            seen = {"act": 0, "dve": 0}
            evac_at = []
            for _, _, e in groups:
                seen[e] += 1
                evac_at.append((e, seen[e]))
            evac_sem = {"act": act_evac, "dve": dve_evac}

            def evacuated(eng, i):
                e, k = evac_at[i]
                eng.wait_ge(evac_sem[e], k)

            def a_view(mc, u, xg):
                yg, x0 = u // 2, 8 * (u % 2) + 4 * xg
                v = AT[:, mc, :].rearrange("p (g y x) -> p x y g", y=SIDE, x=SIDE)
                return v[:, x0:x0 + 4, 8 * yg:8 * yg + 8, :]

            def read_out(eng, name):
                for i, (kind, d, e) in enumerate(groups):
                    if e != name:
                        continue
                    bank = PS[:, i % 8, :]
                    eng.wait_ge(pe_group, i + 1)
                    if kind == "G":
                        u, xi = d
                        if u >= 2:
                            eng.wait_ge(shifted[u - 2], 128)
                        dst, src = G[:, u % 2, xi, :], bank[:, 0:DY * SIDE]
                    elif kind == "K":
                        b, mc, nh = d
                        dst = AT[:, mc, b * C:b * C + C].rearrange("p (h y x) -> p x y h", y=SIDE, x=SIDE)[
                            :, 8 * nh:8 * nh + 8, :, :]
                        src = bank.rearrange("p (x y h) -> p x y h", x=8, y=SIDE)
                    if kind in "GK":
                        ins = nc.scalar.activation(dst, src, ACT.Copy) if name == "act" else nc.vector.tensor_copy(dst, src)
                    elif kind == "A":
                        u, xg, mc = d
                        if (u, xg, mc) == (0, 0, 0):
                            eng.wait_ge(act_evac, 24)
                            eng.wait_ge(dve_evac, 24)
                        v = a_view(mc, u, xg)
                        ins = nc.vector.tensor_tensor(v, bank.rearrange("p (x y g) -> p x y g", x=4, y=8), v, ALU.add)
                    else:
                        b, vt, nh = d
                        v = xT[:, :, b * N:(b + 1) * N].rearrange("p (h v) n -> p v h n", v=2)[:, vt, 2 * nh:2 * nh + 2, :]
                        ins = nc.vector.tensor_tensor(v, bank.rearrange("p (h n) -> p h n", h=2), v, ALU.add)
                    ins.then_inc(evac_sem[name], 1)

            def shift(eng, u, ys):
                for i in range(8 * u, 8 * u + 8):
                    evacuated(eng, i)
                for y in ys:
                    rows = slice(16 * y, 16 * y + 16)
                    eng.dma_start(A2[rows, u, :, :], G[rows, u % 2, :, (7 - y) * SIDE:(7 - y) * SIDE + N])\
                        .then_inc(shifted[u], 16)

            with nc.Block() as block:
                @block.sync
                def _(sp):
                    sp.dma_start(ET[:, :, :], A["emb"]).then_inc(et_in, 16)
                    sp.dma_start(c0[:, :, :, :].rearrange("p a b c -> p (a b c)"), A["c0"].partition_broadcast(32)).then_inc(cores_in, 16)
                    sp.dma_start(c3[:, :, :, :].rearrange("p a b c -> p (a b c)"), A["c3"].partition_broadcast(32)).then_inc(cores_in, 16)
                    sp.dma_start(c1[:, :, :, :].rearrange("p a b c -> p (a b c)"), A["c1"]).then_inc(cores_in, 16)
                    for r in range(4):
                        sp.dma_start(c2[r:32:4, :, :, :].rearrange("p a b c -> p (a b c)"), A["c2"]).then_inc(cores_in, 16)
                    for u in range(4):
                        shift(sp, u, range(8))

                @block.gpsimd
                def _(pool):
                    pool.wait_ge(cores_in, 16 * 7)
                    muls, adds = Count(mul_done), Count(add_done)
                    for r in range(RANK):
                        to = tA if r else ttA
                        if r:
                            pool.wait_ge(add_done, adds.n)
                        for a in range(4):
                            o = to[:, 64 * a:64 * a + 64].rearrange("p (h o q) -> p h o q", h=2, o=4)
                            i0 = c0[:, r, a, :].rearrange("p (h o q) -> p h o q", h=1, q=1).broadcast_to([32, 2, 4, 8])
                            i1 = c1[:, r, :, :].rearrange("p h (o q) -> p h o q", o=1).broadcast_to([32, 2, 4, 8])
                            last = nc.gpsimd.tensor_tensor(o, i0, i1, ALU.mult)
                        muls.up(last)
                        pool.wait_ge(mul_done, muls.n)
                        if r:
                            adds.up(nc.gpsimd.tensor_tensor(ttA[:, :], ttA[:, :], tA[:, :], ALU.add))
                    for r in range(RANK):
                        to = tB if r else ttB
                        if r:
                            pool.wait_ge(add_done, adds.n)
                        for o2 in range(8):
                            o = to[:, 128 * o2:128 * o2 + 128].rearrange("p (o c q) -> p o c q", o=4, c=8)
                            i0 = c2[:, r, o2, :].rearrange("p (o c q) -> p o c q", o=1, q=1).broadcast_to([32, 4, 8, 4])
                            i1 = c3[:, r, :, :].rearrange("p o (c q) -> p o c q", c=1).broadcast_to([32, 4, 8, 4])
                            last = nc.gpsimd.tensor_tensor(o, i0, i1, ALU.mult)
                        muls.up(last)
                        pool.wait_ge(mul_done, muls.n)
                        if r:
                            adds.up(nc.gpsimd.tensor_tensor(ttB[:, :], ttB[:, :], tB[:, :], ALU.add))

                @block.scalar
                def _(act):
                    read_out(act, "act")

                @block.vector
                def _(dve):
                    read_out(dve, "dve")
                    dve.wait_ge(dve_evac, seen["dve"])
                    for c in range(CK):
                        norms[1].chunk_stats(c)
                    norms[1].aggregate()

                @block.tensor
                def _(pe):
                    pe.wait_ge(et_in, 16)
                    for i, (kind, d, _) in enumerate(groups):
                        bank = PS[:, i % 8, :]
                        if i >= 8:
                            evacuated(pe, i - 8)
                        if kind == "G":
                            u, xi = d
                            yg, x = u // 2, 8 * (u % 2) + xi
                            d0 = (1 - yg) * 8
                            for jp in range(2):
                                lhs = Qs[:, jp, x * N + yg * P:x * N + yg * P + P]
                                rhs = ET[:, jp, :].rearrange("p (a b) -> p a b", a=31)[:, d0:d0 + DY, 15 - x:31 - x]
                                m = nc.tensor.matmul(bank[:, 0:DY * SIDE], lhs, rhs, start=jp == 0, stop=jp == 1)
                        elif kind == "K":
                            b, mc, nh = d
                            for jp in range(2):
                                rhs = Qs[:, jp, :].rearrange("p (x y g) -> p x y g", x=SIDE, y=SIDE)[
                                    :, 8 * nh:8 * nh + 8, :, HEADS0 * b:HEADS0 * b + HEADS0]
                                m = nc.tensor.matmul(bank, ks[:, b, jp, mc * P:mc * P + P], rhs,
                                                     start=jp == 0, stop=jp == 1)
                        elif kind == "A":
                            u, xg, mc = d
                            if xg == 0 and mc == 0:
                                pe.wait_ge(shifted[u], 128)
                            for xi in range(4):
                                m = nc.tensor.transpose(bank[:, xi * P:xi * P + P], A2[:, u, 4 * xg + xi, mc * P:mc * P + P], ident[:, :])
                        else:
                            b, vt, nh = d
                            if (b, vt, nh) == (0, 0, 0):
                                pe.wait_ge(dve_evac, 24 + 16)
                            for mc in range(2):
                                m = nc.tensor.matmul(bank, VT[:, mc, b * N + vt * P:b * N + vt * P + P],
                                                     AT[:, mc, b * C + nh * HALF:b * C + nh * HALF + HALF],
                                                     start=mc == 0, stop=mc == 1)
                        m.then_inc(pe_group, 1)


def layer12(nc, A, outer, g, layer):
    PS, xT, ident, identb, maskb, bias = (g[x] for x in ("PS", "xT", "ident", "identb", "maskb", "bias"))
    sem, sb, norms, w_used = (g[x] for x in ("sem", "sb", "norms", "w_used"))
    chunk_product, block_product = g["chunk_product"], g["block_product"]
    norm = norms[layer]
    masked = layer == 1
    n0 = HB0 if masked else HB0 + HB1
    per_pass = 16 if masked else 8
    n1 = n0 + (HB1 if masked else HB2)
    PJ, S, PT, O = (0, 1), 2, 4, 6
    SCALE = 64 ** -0.5

    def q_block(j, second):
        return 6 * j + (n0 + 2 + (per_pass if second else 0))

    def spans(ahead):
        if not masked:
            return ((0, N), (0, N))
        return ((0, N), (P, N)) if ahead else ((0, P), (0, N))

    def tiles(ahead):
        at, r = 0, []
        for kt in range(2):
            for qt in range(2):
                lo, hi = spans(ahead)[qt]
                if lo <= kt * P < hi:
                    r.append((kt, qt, at))
                    at += P
        return r

    with ExitStack() as ctx:
        xh = sb(ctx, "xh", [P, CK, T], F32R)
        xl = sb(ctx, "xl", [P, CK, T], F32R)
        ytmp = sb(ctx, "ytmp", [P, 2, T])
        o_shape = [P, CK, HALF] if masked else [P, PAIRS // 2, T]
        oh = sb(ctx, "oh", o_shape, F32R)
        ol = sb(ctx, "ol", o_shape, F32R)
        vT = sb(ctx, "vT", [P, T])
        v = sb(ctx, "v", [P, CK, P])
        prob = sb(ctx, "prob", [P, 2, 2, N])
        probT = sb(ctx, "probT", [P, 2, HALF])
        nmax = sb(ctx, "nmax", [P, 2, 2])
        psum_ = sb(ctx, "psum", [P, 2, 2])
        prec = sb(ctx, "prec", [P, 2, 2])
        if masked:
            q = sb(ctx, "q", [P, T])
            k = sb(ctx, "k", [P, T])
        else:
            qp = sb(ctx, "qp", [P, T])
            q = sb(ctx, "qa", [KROWS, 2, T])
            k = sb(ctx, "ka", [KROWS, 2, T])
            rel = sb(ctx, "rel", [P, 2, 64])
            kb = sb(ctx, "kb", [P, PAIRS])

        v_evac = sem("v_evac")
        v_tr = sem("v_tr")
        v_ready = sem("v_ready")
        q_evac = sem("q_evac")
        qa_evac = sem("qa_evac")
        k_evac = sem("k_evac")
        relh_done = sem("relh_done")
        relw_done = sem("relw_done")
        relh_evac = sem("relh_evac")
        relw_evac = sem("relw_evac")
        s_done = sem("s_done")
        p_max = sem("p_max")
        p_exp = sem("p_exp")
        p_rec = sem("p_rec")
        p_norm = sem("p_norm")
        t_done = sem("t_done")
        t_evac = sem("t_evac")
        o_done = sem("o_done")
        o_hi = sem("o_hi")
        o_ready = sem("o_ready")
        sum_done = sem("sum_done")
        tables_in = sem("tables_in")
        kb_ready = sem("kb_ready")

        def pairs(eng, step, out_pass):
            with eng.Fori(0, PAIRS // 2) as j:
                step(j, False, True)
            out_pass(0)
            with eng.Fori(PAIRS // 2, PAIRS - 1) as j:
                step(j, True, True)
            step(PAIRS - 1, True, False)
            out_pass(1)

        def pass_block(half):
            return n0 + 2 + 24 if half == 0 else n1 - per_pass

        with nc.Block() as block:
            @block.sync
            def _(sp):
                if not masked:
                    sp.dma_start(rel[:, :, :], A["rel"].rearrange("a p n -> p a n")).then_inc(tables_in, 16)
                    for hh in range(2):
                        sp.dma_start(k[64:KROWS, hh, :], A["hot"]).then_inc(tables_in, 16)
                g["w_loads"](sp, n0 + 2, min(n1 + 2, HB_TOTAL))

            @block.gpsimd
            def _(pool):
                norm.on_gpsimd()
                g["w_splits"](pool, n0 + 2, min(n1 + 2, HB_TOTAL))

            @block.scalar
            def _(act):
                norm.on_scalar(xh, ytmp)

                def step(j, ahead, more):
                    n = q_block(j, ahead)
                    both = PS[:, 0:2, :].rearrange("p a n -> p (a n)")
                    act.wait_ge(w_used, n + 2)
                    if masked:
                        nc.scalar.activation(q[:, :], both, ACT.Copy).then_inc(q_evac, 1)
                    else:
                        nc.scalar.activation(qp[:, :], both, ACT.Identity, bias=bias[:, bass.ds(j, 1)])\
                            .then_inc(q_evac, 1)
                    act.wait_ge(w_used, n + 4)
                    both = PS[:, S:S + 2, :].rearrange("p a n -> p (a n)")
                    if masked:
                        nc.scalar.activation(k[:, :], both, ACT.Copy, scale=SCALE).then_inc(k_evac, 1)
                    else:
                        for hh in range(2):
                            rows = slice(64 * hh, 64 * hh + 64)
                            last = nc.scalar.activation(k[0:64, hh, :], PS[rows, S:S + 2, :].rearrange("p a n -> p (a n)"),
                                                        ACT.Identity, bias=kb[rows, bass.ds(j, 1)], scale=SCALE)
                        last.then_inc(k_evac, 1)
                        act.wait_ge(relh_done, j + 1)
                        for bank in range(2):
                            for hh in range(2):
                                src = PS[32 * hh:32 * hh + SIDE, O + bank, :].rearrange("p (h b w) -> p h b w", h=8, b=B)
                                dst = q[64:64 + SIDE, hh, :].rearrange("p (b h w) -> p h b w", b=B, h=SIDE)[
                                    :, 8 * bank:8 * bank + 8, :, :]
                                last = nc.scalar.activation(dst, src, ACT.Copy)
                        last.then_inc(relh_evac, 1)

                    def evac_t(u):
                        act.wait_ge(t_done, 8 * j + u + 1)
                        w = P * len(tiles(ahead))
                        nc.scalar.activation(probT[:, u % 2, 0:w], PS[:, PT + u % 2, 0:w], ACT.Copy).then_inc(t_evac, 1)

                    for u in range(UNITS):
                        act.wait_ge(p_max, 8 * j + u + 1)
                        for qt, (lo, hi) in enumerate(spans(ahead)):
                            last = nc.scalar.activation(prob[:, u % 2, qt, lo:hi], PS[:, S + u % 2, qt * N + lo:qt * N + hi],
                                                        ACT.Exp, bias=nmax[:, u % 2, qt:qt + 1],
                                                        accum_out=psum_[:, u % 2, qt:qt + 1])
                        last.then_inc(p_exp, 1)
                        if u:
                            evac_t(u - 1)
                    evac_t(UNITS - 1)

                pairs(act, step, lambda half: None)

            @block.vector
            def _(dve):
                nc.vector.memset(nmax[:, :, :], 0.0).then_inc(sum_done, 2)
                nc.vector.memset(psum_[:, :, :], 0.0).then_inc(o_ready, 1)
                if not masked:
                    nc.vector.memset(q[64:96, :, :], 0.0)
                    nc.vector.tensor_scalar(kb[:, :], bias[:, 8:16], SCALE, None, ALU.mult).then_inc(kb_ready, 1)
                norm.on_vector(xh, xl, ytmp)

                def evac_v(j, n):
                    dve.wait_ge(w_used, n + 2)
                    both = PS[:, 0:2, :].rearrange("p a n -> p (a n)")
                    if masked:
                        ins = nc.vector.tensor_copy(vT[:, :], both)
                    else:
                        ins = nc.vector.tensor_scalar(vT[:, :], both, bias[:, bass.ds(j + 16, 1)], None, ALU.add)
                    ins.then_inc(v_evac, 1)

                def evac_o(j, half, grp):
                    dve.wait_ge(o_done, 2 * j + grp + 1)
                    jl = j - half * (PAIRS // 2)
                    src = PS[:, O + grp, :]
                    if masked:
                        src = src.rearrange("p (b r c) -> p b r c", b=2, c=CK)
                        hi, lo = (t[:, :, :].rearrange("p c (b j r) -> p b j r c", b=B, j=4)[
                            :, 2 * grp:2 * grp + 2, bass.ds(jl, 1), :, :].rearrange("p b j r c -> p b (j r) c") for t in (oh, ol))
                    else:
                        hi, lo = (t[:, bass.ds(jl, 1), HALF * grp:HALF * grp + HALF].rearrange("p a n -> p (a n)") for t in (oh, ol))
                    nc.vector.tensor_copy(hi, src).then_inc(o_hi, 1)
                    dve.wait_ge(o_hi, 2 * j + grp + 1)
                    nc.vector.tensor_tensor(lo, src, hi.bitcast(F32), ALU.subtract).then_inc(o_ready, 1)

                def step(j, ahead, more):
                    n = q_block(j, ahead)
                    if not masked:
                        dve.wait_ge(q_evac, j + 1)
                        for hh in range(2):
                            rows = slice(64 * hh, 64 * hh + 64)
                            last = nc.vector.tensor_scalar(q[0:64, hh, :], PS[rows, 0:2, :].rearrange("p a n -> p (a n)"),
                                                           bias[rows, bass.ds(j, 1)], None, ALU.add)
                        last.then_inc(qa_evac, 1)
                    dve.wait_ge(v_tr, j + 1)
                    nc.vector.tensor_copy(v[:, :, :].rearrange("p a n -> p (a n)"),
                                          PS[:, PT:PT + 2, :].rearrange("p a n -> p (a n)")).then_inc(v_ready, 1)
                    if not masked:
                        dve.wait_ge(relw_done, j + 1)
                        for bank in range(2):
                            for hh in range(2):
                                src = PS[32 * hh:32 * hh + SIDE, PT + bank, :].rearrange("p (w b h) -> p w b h", w=8, b=B)
                                dst = q[96:96 + SIDE, hh, :].rearrange("p (b h w) -> p w b h", b=B, h=SIDE)[
                                    :, 8 * bank:8 * bank + 8, :, :]
                                last = nc.vector.tensor_copy(dst, src)
                        last.then_inc(relw_evac, 1)
                    for u in range(UNITS):
                        unit = 8 * j + u + 1
                        dve.wait_ge(s_done, unit)
                        if masked:
                            for qt, (lo, hi) in enumerate(spans(ahead)):
                                last = nc.vector.tensor_reduce(nmax[:, u % 2, qt:qt + 1], PS[:, S + u % 2, qt * N + lo:qt * N + hi],
                                                               AX, ALU.max, negate=True)
                        else:
                            last = nc.vector.tensor_reduce(nmax[:, u % 2, :], PS[:, S + u % 2, :].rearrange("p (a n) -> p a n", a=2),
                                                           AX, ALU.max, negate=True)
                        last.then_inc(p_max, 1)
                        dve.wait_ge(p_exp, unit)
                        nc.vector.reciprocal(prec[:, u % 2, :], psum_[:, u % 2, :]).then_inc(p_rec, 1)
                        dve.wait_ge(p_rec, unit)
                        for qt, (lo, hi) in enumerate(spans(ahead)):
                            last = nc.vector.tensor_scalar(prob[:, u % 2, qt, lo:hi], prob[:, u % 2, qt, lo:hi],
                                                           prec[:, u % 2, qt:qt + 1], None, ALU.mult)
                        last.then_inc(p_norm, 1)
                        if u == 5:
                            evac_o(j, int(ahead), 0)
                    if more:
                        evac_v(j + 1, n + 4)
                    evac_o(j, int(ahead), 1)

                def out_pass(half):
                    base = 2 + CK * half
                    n = pass_block(half)
                    with dve.Fori(0, CK // 2) as i:
                        for s in range(2):
                            o = 2 * i + s
                            x = xT[:, bass.ds(o, 1), :]
                            if masked:
                                dve.wait_ge(w_used, n + 2 * o + 2)
                                x = x.rearrange("p a (b r) -> p (a b) r", b=B)[:, :, half * P:half * P + P]
                                nc.vector.tensor_tensor(x, PS[:, s, :].rearrange("p (b r) -> p b r", b=B), x, ALU.add)\
                                    .then_inc(sum_done, 1)
                            else:
                                dve.wait_ge(w_used, n + o + 1)
                                x = x.rearrange("p a n -> p (a n)")
                                src = PS[:, 2 * s:2 * s + 2, :].rearrange("p a n -> p (a n)")
                                if half:
                                    ins = nc.vector.scalar_tensor_tensor(x, src, bias[:, bass.ds(o + 24, 1)], x, ALU.add, ALU.add)
                                else:
                                    ins = nc.vector.tensor_tensor(x, src, x, ALU.add)
                                ins.then_inc(sum_done, 1)
                            if half:
                                dve.wait_ge(sum_done, base + o + 1)
                                norms[layer + 1].chunk_stats(o)
                    if half:
                        norms[layer + 1].aggregate()

                evac_v(0, n0)
                pairs(dve, step, out_pass)

            @block.tensor
            def _(pe):
                norm.on_tensor()
                block_product(n0, xh, xl, PJ, norm.ready)
                if not masked:
                    pe.wait_ge(tables_in, 48)

                def scores(j, u, ahead):
                    b, hh = u // 2, u % 2
                    for qt, (lo, hi) in enumerate(spans(ahead)):
                        at = qt * N
                        if masked:
                            rows = slice(64 * hh, 64 * hh + 64)
                            lhs, rhs = q[rows, b * N + qt * P:b * N + qt * P + P], k[rows, b * N + lo:b * N + hi]
                        else:
                            lhs, rhs = q[:, hh, b * N + qt * P:b * N + qt * P + P], k[:, hh, b * N:b * N + N]
                        m = nc.tensor.matmul(PS[:, S + u % 2, at + lo:at + hi], lhs, rhs, start=True, stop=not masked)
                        if masked:
                            m = nc.tensor.matmul(PS[:, S + u % 2, at + qt * P:at + qt * P + P], identb[:, :],
                                                 maskb[:, int(ahead), :], start=False, stop=True)
                    m.then_inc(s_done, 1)

                def transposed(j, u, ahead):
                    pe.wait_ge(p_norm, 8 * j + u + 1)
                    for kt, qt, at in tiles(ahead):
                        m = nc.tensor.transpose(PS[:, PT + u % 2, at:at + P], prob[:, u % 2, qt, kt * P:kt * P + P], ident[:, :])
                    m.then_inc(t_done, 1)

                def outputs(j, u, ahead):
                    b, hh = u // 2, u % 2
                    pe.wait_ge(t_evac, 8 * j + u + 1)
                    bank = O + u // 4
                    if not masked:
                        for kt in range(2):
                            m = nc.tensor.matmul(PS[64 * hh:64 * hh + 64, bank, (b % 2) * N:(b % 2) * N + N],
                                                 v[:, 2 * b + kt, 64 * hh:64 * hh + 64], probT[:, u % 2, kt * N:kt * N + N],
                                                 start=kt == 0, stop=kt == 1)
                    else:
                        col = (u % 4) * P
                        whole, part = (1, 0) if ahead else (0, 1)
                        w_at, p_at, p_col = (P, 0, 0) if ahead else (0, N, 64)
                        for r in range(2):
                            rows = slice(64 * r, 64 * r + 64)
                            nc.tensor.matmul(PS[rows, bank, col:col + P], v[:, 2 * b + whole, 64 * hh:64 * hh + 64],
                                             probT[:, u % 2, w_at + r:w_at + N:2], start=True, stop=False)
                            m = nc.tensor.matmul(PS[rows, bank, col + p_col:col + p_col + 64],
                                                 v[:, 2 * b + part, 64 * hh:64 * hh + 64],
                                                 probT[:, u % 2, p_at + r:p_at + P:2], start=False, stop=True)
                    if u % 4 == 3:
                        m.then_inc(o_done, 1)

                def step(j, ahead, more):
                    n = q_block(j, ahead)
                    pe.wait_ge(v_evac, j + 1)
                    block_product(n, xh, xl, PJ)
                    for tt in range(CK):
                        m = nc.tensor.transpose(PS[:, PT + tt // 4, (tt % 4) * P:(tt % 4) * P + P],
                                                vT[:, tt * P:tt * P + P], ident[:, :])
                    m.then_inc(v_tr, 1)
                    block_product(n + 2, xh, xl, (S, S + 1))
                    pe.wait_ge(q_evac, j + 1)
                    if not masked:
                        pe.wait_ge(qa_evac, j + 1)
                        pe.wait_ge(o_ready, 2 * j + 1)
                        for h in range(SIDE):
                            m = nc.tensor.matmul(PS[0:48, O + h // 8, (h % 8) * 64:(h % 8) * 64 + 64],
                                                 rel[:, 0, 15 - h:63 - h],
                                                 qp[:, :].rearrange("p (b h w) -> p h b w", b=B, h=SIDE)[:, h, :, :],
                                                 start=True, stop=True)
                        m.then_inc(relh_done, 1)
                        pe.wait_ge(v_ready, j + 1)
                        for w in range(SIDE):
                            m = nc.tensor.matmul(PS[0:48, PT + w // 8, (w % 8) * 64:(w % 8) * 64 + 64],
                                                 rel[:, 1, 15 - w:63 - w],
                                                 qp[:, :].rearrange("p (b h w) -> p w b h", b=B, h=SIDE)[:, w, :, :],
                                                 start=True, stop=True)
                        m.then_inc(relw_done, 1)
                    pe.wait_ge(k_evac, j + 1)
                    if not masked:
                        if more:
                            chunk_product(n + 4, 0, 0, 0, xh, xl, PJ, True, False)
                        pe.wait_ge(relh_evac, j + 1)
                        pe.wait_ge(relw_evac, j + 1)
                    for u in range(UNITS):
                        scores(j, u, ahead)
                        if more and (masked or u):
                            chunk_product(n + 4 + u // 4, u // 4, u % 4, u, xh, xl, PJ, u == 0, u == UNITS - 1)
                        if u >= 1:
                            if u == 1:
                                pe.wait_ge(v_ready, j + 1)
                            transposed(j, u - 1, ahead)
                        if u >= 2:
                            outputs(j, u - 2, ahead)
                    transposed(j, UNITS - 1, ahead)
                    outputs(j, UNITS - 2, ahead)
                    outputs(j, UNITS - 1, ahead)

                def out_pass(half):
                    pe.wait_ge(o_ready, 8 * half + 9)
                    if half == 0:
                        pe.wait_ge(v_evac, PAIRS // 2 + 1)
                    n = pass_block(half)
                    with pe.Fori(0, CK // 2) as i:
                        for s in range(2):
                            o = 2 * i + s
                            pe.wait_ge(sum_done, CK * half + o + 1)
                            if masked:
                                block_product(n + 2 * o, oh, ol, (s,))
                            else:
                                for c in range(4):
                                    chunk_product(n + o, s, c, c, oh, ol, (2 * s, 2 * s + 1), c == 0, c == 3)
                    if half == 0:
                        pe.wait_ge(sum_done, 2 + CK)

                pairs(pe, step, out_pass)


def layer3(nc, A, out, outer, g):
    PS, xT, bias, ttA, ttB = (g[x] for x in ("PS", "xT", "bias", "ttA", "ttB"))
    sem, sb, norms = (g[x] for x in ("sem", "sb", "norms"))
    norm = norms[3]
    O23, O01 = 32, 32
    QUART = 8
    with ExitStack() as ctx:
        xh = sb(ctx, "xh", [P, CK, T], F32R)
        xl = sb(ctx, "xl", [P, CK, T], F32R)
        ytmp = sb(ctx, "ytmp", [P, 2, T])
        Mh = sb(ctx, "Mh", [P, CK, C], F32R)
        Ml = sb(ctx, "Ml", [P, CK, C], F32R)
        BD = sb(ctx, "BD", [32, 2, QUART, P])
        U = sb(ctx, "U", [P, 2, 2, C])
        K = sb(ctx, "K", [P, 2, N])
        kt = sb(ctx, "kt", [P, 2, N])
        kx = sb(ctx, "kx", [P, 3, SIDE])
        kxt = sb(ctx, "kxt", [P, 3, SIDE])
        taps = sb(ctx, "taps", [P, 9])
        near_x = sb(ctx, "near_x", [P, 3, SIDE])
        near_y = sb(ctx, "near_y", [P, 3, 2, SIDE])
        r2c = sb(ctx, "r2c", [32, 4])
        act_out = ytmp[:, :, 0:2 * N].rearrange("p a (s n) -> p a s n", s=2)
        consts3 = sem("consts3")
        bd_ready = sem("bd_ready")
        m_done = sem("m_done")
        m_hi = sem("m_hi")
        m_lo = sem("m_lo")
        k_step = sem("k_step")
        k_ready = sem("k_ready")
        u_done = sem("u_done")
        u_act = sem("u_act")
        u_dve = sem("u_dve")
        f_done = sem("f_done")
        relu_done = sem("relu_done")
        x_final = sem("x_final")
        stored = sem("stored")

        with nc.Block() as block:
            @block.sync
            def _(sp):
                sp.dma_start(r2c[:, :], A["r2c"]).then_inc(consts3, 16)
                sp.dma_start(taps[:, :], A["taps"].partition_broadcast(P)).then_inc(consts3, 16)
                sp.dma_start(near_x[:, :, :].rearrange("p a b -> p (a b)"), A["near_x"]).then_inc(consts3, 16)
                sp.dma_start(near_y[:, :, :, :].rearrange("p a b c -> p (a b c)"), A["near_y"]).then_inc(consts3, 16)
                for b in range(B):
                    sp.wait_ge(x_final, 4 * b + 4)
                    sp.dma_start(out.rearrange("c p t -> p c t")[:, :, b * N:(b + 1) * N],
                                 xT[:, :, b * N:(b + 1) * N]).then_inc(stored, 16)
                sp.wait_ge(stored, 16 * B)

            @block.gpsimd
            def _(pool):
                pool.wait_ge(consts3, 64)

                def masked_factor(i):
                    if i >= 2:
                        pool.wait_ge(m_done, 4 * (i - 1))
                    o = BD[:, i % 2, :, :].rearrange("p o (a c) -> p o a c", a=4)
                    fac = ttB[:, i * 256:i * 256 + 256].rearrange("p (o a c) -> p o a c", o=QUART, a=1)\
                        .broadcast_to([32, QUART, 4, 32])
                    msk = r2c[:, :].rearrange("p (o a c) -> p o a c", o=1, c=1).broadcast_to([32, QUART, 4, 32])
                    nc.gpsimd.tensor_tensor(o, fac, msk, ALU.mult).then_inc(bd_ready, 1)

                masked_factor(0)
                masked_factor(1)
                norm.on_gpsimd()
                for i in range(2, 4):
                    masked_factor(i)
                step = Count(k_step)
                for dx in range(3):
                    to = kxt if dx else kx
                    t = taps[:, :].rearrange("p (a b c) -> p a b c", a=3, c=1)[:, :, dx, :].broadcast_to([P, 3, SIDE])
                    m = near_x[:, dx:dx + 1, :].broadcast_to([P, 3, SIDE])
                    step.up(nc.gpsimd.tensor_tensor(to[:, :, :], t, m, ALU.mult))
                    pool.wait_ge(k_step, step.n)
                    if dx:
                        step.up(nc.gpsimd.tensor_tensor(kx[:, :, :], kx[:, :, :], kxt[:, :, :], ALU.add))
                        pool.wait_ge(k_step, step.n)
                for dy in range(3):
                    to = (kt if dy else K)[:, :, :].rearrange("p t (y x) -> p t y x", y=SIDE)
                    a = near_y[:, dy, :, :].rearrange("p t (y x) -> p t y x", x=1).broadcast_to([P, 2, SIDE, SIDE])
                    b = kx[:, dy, :].rearrange("p (t y x) -> p t y x", t=1, y=1).broadcast_to([P, 2, SIDE, SIDE])
                    step.up(nc.gpsimd.tensor_tensor(to, a, b, ALU.mult))
                    pool.wait_ge(k_step, step.n)
                    if dy:
                        ins = nc.gpsimd.tensor_tensor(K[:, :, :], K[:, :, :], kt[:, :, :], ALU.add)
                        if dy == 2:
                            ins.then_inc(k_ready, 1)
                        else:
                            step.up(ins)
                            pool.wait_ge(k_step, step.n)

            def m_views(i):
                src = PS[:, i % 4, :].rearrange("p (b k a) -> p b k a", b=2, k=CK)
                return src, *(t[:, :, :].rearrange("p k (a b) -> p b k a", b=O23)[:, 2 * i:2 * i + 2, :, :] for t in (Mh, Ml))

            @block.scalar
            def _(act):
                def head_of_m(c):
                    for i in range(2 * c, 2 * c + 2):
                        act.wait_ge(m_done, i + 1)
                        src, hi, _ = m_views(i)
                        nc.scalar.activation(hi, src, ACT.Copy).then_inc(m_hi, 1)

                norm.on_scalar(xh, ytmp, head_of_m)

                def relu(b):
                    for op in range(4):
                        i = 4 * b + op
                        act.wait_ge(f_done, i + 1)
                        if i >= 2:
                            act.wait_ge(x_final, i - 1)
                        for s in range(2):
                            o = 2 * op + s
                            last = nc.scalar.activation(act_out[:, i % 2, s, :], PS[:, 4 + i % 4, s * N:s * N + N],
                                                        ACT.Relu, bias=bias[:, 32 + o:33 + o])
                        last.then_inc(relu_done, 1)

                for b in range(B):
                    for tt in range(2):
                        act.wait_ge(u_done, 4 * b + 2 * tt + 1)
                        nc.scalar.activation(U[:, b % 2, tt, 0:HALF], PS[:, 2 * tt, :], ACT.Copy).then_inc(u_act, 1)
                    if b:
                        relu(b - 1)
                relu(B - 1)

            @block.vector
            def _(dve):
                def rest_of_m(c):
                    for i in range(2 * c, 2 * c + 2):
                        dve.wait_ge(m_hi, i + 1)
                        src, hi, lo = m_views(i)
                        nc.vector.tensor_tensor(lo, src, hi.bitcast(F32), ALU.subtract).then_inc(m_lo, 1)

                norm.on_vector(xh, xl, ytmp, rest_of_m)

                def add(b):
                    for op in range(4):
                        i = 4 * b + op
                        dve.wait_ge(relu_done, i + 1)
                        x = xT[:, 2 * op:2 * op + 2, b * N:(b + 1) * N]
                        nc.vector.tensor_tensor(x, act_out[:, i % 2, :, :], x, ALU.add).then_inc(x_final, 1)

                for b in range(B):
                    for tt in range(2):
                        dve.wait_ge(u_done, 4 * b + 2 * tt + 2)
                        nc.vector.tensor_copy(U[:, b % 2, tt, HALF:C], PS[:, 2 * tt + 1, :]).then_inc(u_dve, 1)
                    if b:
                        add(b - 1)
                add(B - 1)

            @block.tensor
            def _(pe):
                norm.on_tensor()
                for i in range(16):
                    if i % 4 == 0:
                        pe.wait_ge(bd_ready, i // 4 + 1)
                    if i >= 4:
                        pe.wait_ge(m_lo, i - 3)
                    for s in range(2):
                        m = nc.tensor.matmul(PS[:, i % 4, s * 256:s * 256 + 256], BD[:, (i // 4) % 2, (2 * i + s) % QUART, :],
                                             ttA[:, :], start=True, stop=True)
                    m.then_inc(m_done, 1)
                pe.wait_ge(m_lo, 16)

                def channel_product(b):
                    for tt in range(2):
                        for oh in range(2):
                            bank = 2 * tt + oh
                            if b:
                                pe.wait_ge(u_dve if oh else u_act, 2 * b - 1 + tt)
                            cols = slice((2 * b + tt) * P, (2 * b + tt) * P + P)
                            for c in range(CK):
                                if b == tt == oh == 0:
                                    norm.ready(c)
                                for k, (x, w) in enumerate(((xh, Mh), (xh, Ml), (xl, Mh))):
                                    m = nc.tensor.matmul(PS[:, bank, :], x[:, c, cols], w[:, c, oh * HALF:oh * HALF + HALF],
                                                         start=c == 0 and k == 0, stop=c == CK - 1 and k == 2)
                            m.then_inc(u_done, 1)

                def convolution(b):
                    for op in range(4):
                        i = 4 * b + op
                        if op == 0:
                            if b == 0:
                                pe.wait_ge(k_ready, 1)
                            pe.wait_ge(u_act, 2 * b + 2)
                            pe.wait_ge(u_dve, 2 * b + 2)
                        if i >= 4:
                            pe.wait_ge(relu_done, i - 3)
                        for s in range(2):
                            o = 2 * op + s
                            for tt in range(2):
                                m = nc.tensor.matmul(PS[:, 4 + i % 4, s * N:s * N + N], U[:, b % 2, tt, o * P:o * P + P],
                                                     K[:, tt, :], start=tt == 0, stop=tt == 1)
                        m.then_inc(f_done, 1)

                for b in range(B):
                    channel_product(b)
                    if b:
                        convolution(b - 1)
                convolution(B - 1)


def lay_out(v):
    def f(name):
        return np.asarray(v[name])

    def chunks(a):
        return a.T.reshape(CK, P, -1)

    def cols(a):
        return a.reshape(-1, P).T

    def block(w, d):
        return w[:, d:d + P].reshape(2, 4, P, P).transpose(0, 2, 1, 3).reshape(2, P, HALF)

    def rows(w):
        return w.reshape(-1, C).T

    s0 = [block(f("L0_conv_Wv"), P * i) for i in range(2)] + [block(f("L0_conv_Wk"), P * i) for i in range(2)]
    s0 += [block(f("L0_conv_Wq"), P * i) for i in range(8)]

    def heads(q, k, w, out_blocks):
        s = [block(w, 0)]
        for j in range(PAIRS):
            s += [block(q, P * j), block(k, P * j)]
            if j + 1 < PAIRS:
                s.append(block(w, P * (j + 1)))
            if j in (PAIRS // 2 - 1, PAIRS - 1):
                s += out_blocks(j // (PAIRS // 2))
        return s

    q1, k1, v1 = (np.concatenate([rows(f(f"L1_conv_W{x}_lb")), rows(f(f"L1_conv_W{x}_la"))], axis=1) for x in "qkv")
    wo = f("L1_conv_Wo").T
    s1 = heads(q1, k1, v1, lambda half: [block(wo, P * o) for o in range(CK)])
    q2, k2, v2 = np.split(f("L2_conv_qkv_w"), 3, axis=1)
    wp = f("L2_conv_proj_w")
    s2 = heads(q2, k2, v2, lambda half: [block(wp, P * o)[half:half + 1] for o in range(CK)])

    emb = f("L0_conv_rel_pos_emb")[..., 0].reshape(961, 64, 2, 2)
    rel = np.zeros((2, P, 64), np.float32)
    for i, name in enumerate(("L2_conv_rel_pos_h", "L2_conv_rel_pos_w")):
        table = f(name)[30::-1].T
        rel[i, 0:64, 0:31] = table
        rel[i, 64:128, 32:63] = table
    t = np.arange(N)
    hot = np.zeros((48, T), np.float32)
    hot[0:16] = np.tile(np.arange(16)[:, None] == t // SIDE, (1, B))
    hot[32:48] = np.tile(np.arange(16)[:, None] == t % SIDE, (1, B))
    i, j = np.arange(P)[:, None], np.arange(P)[None, :]
    mask = np.zeros((2, P, P), np.float32)
    mask[0][j > i] = -1e30
    mask[1][j < i] = -1e30
    c1 = f("L3_conv_core1").reshape(8, 8, 8, 2, 4)
    c2 = f("L3_conv_core2").reshape(8, 8, 8, 8)
    x = np.arange(P) % SIDE
    y = np.arange(P)[:, None] // SIDE + np.array([0, P // SIDE])
    d3 = np.arange(3)
    near_x = (x[:, None, None] - np.arange(16)[None, None] == d3[None, :, None] - 1).astype(np.float32)
    near_y = (y[:, None, :, None] - np.arange(16) == d3[None, :, None, None] - 1).astype(np.float32)
    bn = [np.concatenate([cols(f(f"L0_conv_q_{x}")), cols(f(f"L0_conv_v_{x}"))], axis=1)
          for x in ("gamma", "beta", "mean", "var")]
    return {
        "x": chunks(f("x").reshape(T, C)),
        "w": np.concatenate(s0 + s1 + s2),
        "ident": np.eye(P, dtype=np.float32),
        "gmat": np.kron(np.eye(P // GROUP), np.full((GROUP, GROUP), 1.0 / GROUP)).astype(np.float32),
        "mask": mask,
        "bn": np.concatenate(bn, axis=1),
        "bias": np.concatenate([cols(f("L2_conv_qkv_b")), cols(f("L2_conv_proj_b")), cols(f("L3_conv_bias"))], axis=1),
        "emb": emb.transpose(3, 1, 2, 0).reshape(P, 2, 961),
        "rel": rel,
        "hot": hot,
        "c0": f("L3_conv_core0").reshape(4, 8, 4).transpose(1, 2, 0).reshape(P),
        "c1": c1.transpose(1, 4, 2, 3, 0).reshape(32, P),
        "c2": c2.transpose(2, 1, 0, 3).reshape(8, HALF),
        "c3": f("L3_conv_core3").reshape(4, 8, 4).transpose(1, 0, 2).reshape(P),
        "taps": f("L3_conv_filters").reshape(9),
        "near_x": near_x.reshape(P, 48),
        "near_y": near_y.reshape(P, 96),
        "r2c": (np.arange(32)[:, None] % 4 == np.arange(4)[None]).astype(np.float32),
    }


def kernel(**inputs):
    import concourse.bacc as _bacc
    from concourse.bass_utils import run_bass_kernel_spmd as _run

    nc = _bacc.Bacc("TRN2", target_bir_lowering=False, num_devices=1)
    arrays, args = {}, {}
    for name, a in lay_out(inputs).items():
        a = np.ascontiguousarray(a)
        arrays[f"in_{name}"] = a
        args[name] = nc.dram_tensor(f"in_{name}", a.shape, mybir.dt.from_np(a.dtype), kind="ExternalInput").ap()
    out = nc.dram_tensor("out_x", (CK, P, T), F32, kind="ExternalOutput").ap()
    build(nc, args, out)
    r = _run(nc, [arrays], core_ids=[0])
    return np.ascontiguousarray(r.results[0]["out_x"].reshape(C, T).T).reshape(B, SIDE, SIDE, C)
```

```python
from contextlib import ExitStack

import numpy as np
import concourse.bass as bass
from concourse import mybir

F32 = mybir.dt.float32
F32R = mybir.dt.float32r
BF16 = mybir.dt.bfloat16
ALU = mybir.AluOpType
ACT = mybir.ActivationFunctionType
AX = mybir.AxisListType.X

P = 128
B = 4
SIDE = 16
N = SIDE * SIDE
T = B * N
C = 1024
CK = C // P
HALF = 512
PAIRS = 8
UNITS = 8
HEADS0 = 4
GROUP = 32
GN_EPS = 1e-5
BN_EPS = 1e-3
OUT_MODES = (4, 8, 8, 4)
RANK = 8
DY = 23
KROWS = 112

HB0 = 2 * 12
HB1 = 2 + 4 * 6 + 16 + 3 * 6 + 4 + 16
HB2 = 2 + 4 * 6 + 8 + 3 * 6 + 4 + 8
HB_TOTAL = HB0 + HB1 + HB2


class Count:

    def __init__(self, sem):
        self.sem, self.n = sem, 0

    def up(self, ins, k=1):
        self.n += k
        ins.then_inc(self.sem, k)
        return self.n


def build(nc, A, out):
    outer = ExitStack()
    with outer:
        names = [0]

        def sem(name):
            names[0] += 1
            return outer.enter_context(nc.semaphore(f"{name}_{names[0]}"))

        def sb(ctx, name, shape, dt=F32):
            names[0] += 1
            return ctx.enter_context(nc.sbuf_tensor(f"{name}_{names[0]}", shape, dt))

        PS = outer.enter_context(nc.psum_tensor("PS", [P, 8, HALF], F32))
        xT = sb(outer, "xT", [P, CK, T])
        ident = sb(outer, "ident", [P, P])
        gmat = sb(outer, "gmat", [P, P])
        identb = sb(outer, "identb", [P, P], BF16)
        maskb = sb(outer, "maskb", [P, 2, P], BF16)
        bn = sb(outer, "bn", [P, 40])
        bias = sb(outer, "bias", [P, 40])
        bst = sb(outer, "bst", [P, CK * B, 6])
        mv = sb(outer, "mv", [P, CK * B, 2])
        sq = sb(outer, "sq", [P, CK * B])
        gn = sb(outer, "gn", [CK * B, 4, P // GROUP])
        gn_row = sb(outer, "gn_row", [CK * B, 2, P])
        coef = sb(outer, "coef", [P, 2, CK * B])
        neghalf = sb(outer, "neghalf", [P, 32])
        ttA = sb(outer, "ttA", [32, 256])
        ttB = sb(outer, "ttB", [32, 1024])
        weights = outer.enter_context(ExitStack())
        w_raw = sb(weights, "w_raw", [P, 2, HALF])
        w_hi = sb(weights, "w_hi", [P, 2, HALF], F32R)
        w_lo = sb(weights, "w_lo", [P, 2, HALF], F32R)
        zeros = sb(weights, "zeros", [P, HALF])

        w_landed = [sem("w_landed0"), sem("w_landed1")]
        w_hi_done = sem("w_hi_done")
        w_ready = sem("w_ready")
        w_used = sem("w_used")
        consts_in = sem("consts_in")
        x_in = [sem(f"x_in{c}") for c in range(CK)]

        def w_load(sp, n, s, waits):
            if waits:
                sp.wait_ge(w_ready, n - 1)
            src = A["w"][n] if isinstance(n, int) else A["w"][bass.ds(n, 1)].rearrange("a p n -> p (a n)")
            sp.dma_start(w_raw[:, s, :], src).then_inc(w_landed[s], 16)

        def w_loads(sp, n0, n1):
            with sp.Fori(n0 // 2, n1 // 2) as i:
                for s in range(2):
                    w_load(sp, 2 * i + s, s, True)

        def w_split(pool, i, s, waits):
            n = 2 * i + s
            pool.wait_ge(w_landed[s], 16 * i + 16)
            if waits:
                pool.wait_ge(w_used, n - 1)
            pool.tensor_tensor(w_hi[:, s, :], w_raw[:, s, :], zeros[:, :], ALU.add).then_inc(w_hi_done, 1)
            pool.wait_ge(w_hi_done, n + 1)
            pool.tensor_tensor(w_lo[:, s, :], w_raw[:, s, :], w_hi[:, s, :].bitcast(F32),
                               ALU.subtract).then_inc(w_ready, 1)

        def w_splits(pool, n0, n1):
            with pool.Fori(n0 // 2, n1 // 2) as i:
                for s in range(2):
                    w_split(pool, i, s, True)

        def chunk_product(n, slot, cc, c, rhs_hi, rhs_lo, banks, first, last, ready=None, used=True):
            if cc == 0:
                nc.tensor.wait_ge(w_ready, n + 1)
            w = slice(cc * P, cc * P + P)
            for k, (wt, x) in enumerate(((w_hi, rhs_hi), (w_lo, rhs_hi), (w_hi, rhs_lo))):
                if ready and k != 1:
                    ready(c, k == 2)
                for h, bank in enumerate(banks):
                    m = nc.tensor.matmul(PS[:, bank, :], wt[:, slot, w], x[:, c, h * HALF:h * HALF + HALF],
                                         start=first and k == 0, stop=last and k == 2)
            if cc == 3 and used:
                m.then_inc(w_used, 1)
            return m

        def block_product(n, rhs_hi, rhs_lo, banks, chunks=range(CK), used=True):
            for c in chunks:
                m = chunk_product(n + c // 4, c // 4, c % 4, c, rhs_hi, rhs_lo, banks, c == 0, c == CK - 1, used=used)
            return m

        def block_pair(n, rhs_hi, rhs_lo, banks_a, banks_b, ready, before):
            for c in range(CK):
                before(c)
                slots = ((0, banks_a), (1, banks_b))
                for slot, banks in slots:
                    chunk_product(n + slot + 2 * (c // 4), slot, c % 4, c, rhs_hi, rhs_lo, banks, c == 0, c == CK - 1,
                                  ready=None if slot else ready)

        class Norm:

            def __init__(self, batches):
                self.batches = batches
                self.stats = sem("gn_stats")
                self.aggr = sem("gn_aggr")
                self.step = sem("gn_step")
                self.grouped = sem("gn_grouped")
                self.rstd = sem("gn_rstd")
                self.rows = sem("gn_rows")
                self.turned = sem("gn_turned")
                self.coef = sem("gn_coef")
                self.y_dve = sem("gn_y_dve")
                self.y_act = sem("gn_y_act")
                self.hi = sem("xh_ready")
                self.lo = sem("xl_ready")
                self.steps = Count(self.step)

            def chunk_stats(self, c, images=range(B)):
                for b in images:
                    src = xT[:, bass.ds(c, 1), b * N:(b + 1) * N].rearrange("p a n -> p (a n)")
                    dst = bst[:, bass.ds(c * B + b, 1), :].rearrange("p a n -> p (a n)")
                    last = nc.vector.bn_stats(dst, src)
                return last

            def aggregate(self, chunks, stats):
                nc.vector.wait_ge(self.stats, stats)
                for c in chunks:
                    for k in range(c * B, c * B + B):
                        last = nc.vector.bn_aggr(mv[:, k, :], bst[:, k, :])
                last.then_inc(self.aggr, len(chunks))

            def size(self, i):
                c0, c1 = self.batches[i]
                return (c1 - c0) * B, slice(c0 * B, c1 * B)

            def squares(self, i):
                n, ks = self.size(i)
                nc.vector.wait_ge(self.aggr, self.batches[i][1])
                self.steps.up(nc.vector.tensor_tensor(sq[:, ks], mv[:, ks, 0], mv[:, ks, 0], ALU.mult))

            def variances(self, i):
                v, steps = nc.vector, self.steps
                n, ks = self.size(i)
                v.wait_ge(self.grouped, i + 1)
                steps.up(v.tensor_copy(gn[0:n, 0, :], PS[0:n, 6, 0:4]))
                v.wait_ge(self.step, steps.n)
                steps.up(v.tensor_tensor(gn[0:n, 1, :], gn[0:n, 0, :], gn[0:n, 0, :], ALU.mult))
                v.wait_ge(self.step, steps.n)
                steps.up(v.tensor_tensor(gn[0:n, 2, :], PS[0:n, 6, 4:8], gn[0:n, 1, :], ALU.subtract))
                v.wait_ge(self.step, steps.n)
                steps.up(v.tensor_scalar(gn[0:n, 2, :], gn[0:n, 2, :], 0.0, GN_EPS, ALU.max, ALU.add))

            def to_rows(self, i):
                n, ks = self.size(i)
                nc.vector.wait_ge(self.rstd, i + 1)
                mean, rstd = (gn[0:n, k, :].rearrange("p (g q) -> p g q", q=1).broadcast_to([n, 4, GROUP]) for k in (0, 3))
                nc.vector.tensor_copy(gn_row[0:n, 0, :].rearrange("p (g q) -> p g q", g=4), rstd)
                nc.vector.scalar_tensor_tensor(gn_row[0:n, 1, :].rearrange("p (g q) -> p g q", g=4), mean, -1.0, rstd,
                                               ALU.mult, ALU.mult).then_inc(self.rows, 1)

            def coefficients(self, i):
                n, ks = self.size(i)
                nc.vector.wait_ge(self.turned, i + 1)
                nc.vector.tensor_copy(coef[:, :, ks], PS[:, 6, 8:8 + 2 * n].rearrange("p (a k) -> p a k", a=2))\
                    .then_inc(self.coef, 1)

            def y(self, eng, c, images, ytmp, done):
                i = next(i for i, (c0, c1) in enumerate(self.batches) if c0 <= c < c1)
                eng.wait_ge(self.coef, i + 1)
                if c >= 2:
                    eng.wait_ge(self.hi, c - 1)
                    eng.wait_ge(self.lo, c - 1)
                for b in images:
                    k = c * B + b
                    dst, src = ytmp[:, c % 2, b * N:(b + 1) * N], xT[:, c, b * N:(b + 1) * N]
                    scale, shift = coef[:, 0, k:k + 1], coef[:, 1, k:k + 1]
                    if eng is nc.scalar:
                        last = nc.scalar.activation(dst, src, ACT.Identity, bias=shift, scale=scale)
                    else:
                        last = nc.vector.tensor_scalar(dst, src, scale, shift, ALU.mult, ALU.add)
                last.then_inc(done, 1)

            def on_vector(self, xh, xl, ytmp, after, flush=()):
                for c in range(CK):
                    self.y(nc.vector, c, (0, 1), ytmp, self.y_dve)
                    if c and c - 1 not in flush:
                        self.rest(c - 1, xh, xl, ytmp)
                    if c in flush or c == CK - 1:
                        self.rest(c, xh, xl, ytmp)
                    after(c)

            def rest(self, c, xh, xl, ytmp):
                nc.vector.wait_ge(self.y_dve, c + 1)
                nc.vector.wait_ge(self.hi, c + 1)
                nc.vector.tensor_tensor(xl[:, c, :], ytmp[:, c % 2, :], xh[:, c, :].bitcast(F32),
                                        ALU.subtract).then_inc(self.lo, 1)

            def head(self, c, xh, ytmp):
                nc.scalar.wait_ge(self.y_dve, c + 1)
                nc.scalar.wait_ge(self.y_act, c + 1)
                nc.scalar.activation(xh[:, c, :], ytmp[:, c % 2, :], ACT.Copy).then_inc(self.hi, 1)

            def on_scalar(self, xh, ytmp):
                for c0, c1 in self.batches:
                    for c in range(c0, c1):
                        self.y(nc.scalar, c, (2, 3), ytmp, self.y_act)
                        if c > c0:
                            self.head(c - 1, xh, ytmp)
                    self.head(c1 - 1, xh, ytmp)

            def averages(self, i):
                n, ks = self.size(i)
                groups = gmat[:, 0:P:GROUP]
                nc.tensor.wait_ge(self.step, 5 * i + 1)
                nc.tensor.matmul(PS[0:n, 6, 0:4], mv[:, ks, 0], groups, start=True, stop=True)
                nc.tensor.matmul(PS[0:n, 6, 4:8], mv[:, ks, 1], groups, start=True, stop=False)
                nc.tensor.matmul(PS[0:n, 6, 4:8], sq[:, ks], groups, start=False, stop=True).then_inc(self.grouped, 1)

            def turn(self, i):
                n, ks = self.size(i)
                nc.tensor.wait_ge(self.rows, i + 1)
                for a in range(2):
                    m = nc.tensor.transpose(PS[:, 6, 8 + a * n:8 + a * n + n], gn_row[0:n, a, :], ident[0:n, 0:n])
                m.then_inc(self.turned, 1)

            def power(self, i):
                n, ks = self.size(i)
                nc.gpsimd.wait_ge(self.step, 5 * i + 5)
                nc.gpsimd.tensor_tensor(gn[0:n, 3, :], gn[0:n, 2, :], neghalf[0:n, 0:4], ALU.pow).then_inc(self.rstd, 1)

            def ready(self, c, lo):
                if lo:
                    nc.tensor.wait_ge(self.lo, c + 1)
                else:
                    nc.tensor.wait_ge(self.hi, c + 1)

        norms = [Norm(((0, 4), (4, 8))), Norm(((0, 4), (4, 8))), Norm(((0, 6), (6, 8))), Norm(((0, 6), (6, 8)))]

        layer0(nc, A, outer, locals())
        layer12(nc, A, outer, locals(), 1)
        layer12(nc, A, outer, locals(), 2)
        weights.close()
        layer3(nc, A, out, outer, locals())


def layer0(nc, A, outer, g):
    PS, xT, zeros, ident, gmat, identb, maskb = (g[x] for x in ("PS", "xT", "zeros", "ident", "gmat", "identb", "maskb"))
    bn, bias, neghalf, ttA, ttB = (g[x] for x in ("bn", "bias", "neghalf", "ttA", "ttB"))
    sem, sb, norms, consts_in, x_in = (g[x] for x in ("sem", "sb", "norms", "consts_in", "x_in"))
    block_product, block_pair, w_used = g["block_product"], g["block_pair"], g["w_used"]
    norm = norms[0]
    with ExitStack() as keep:
        Qs = sb(keep, "Qs", [P, 2, B * HEADS0 * N])
        VT = sb(keep, "VT", [P, 2, T])
        ks = sb(keep, "ks", [P, B, 2, N])

        ET = sb(keep, "ET", [P, 2, 961])
        et_in = sem("et_in")

        with ExitStack() as ctx:
            xh = sb(ctx, "xh", [P, CK, T], F32R)
            xl = sb(ctx, "xl", [P, CK, T], F32R)
            ytmp = sb(ctx, "ytmp", [P, 2, T])
            qT = sb(ctx, "qT", [P, 2, T])
            KT = sb(ctx, "KT", [P, 2, T])
            bns = sb(ctx, "bns", [P, 4, 10])
            kmax = sb(ctx, "kmax", [P, B, 2])
            ksum = sb(ctx, "ksum", [P, B, 2])
            krec = sb(ctx, "krec", [P, B, 2])
            maskf = sb(ctx, "maskf", [P, 2, P])
            memset_done = sem("memset_done")
            gn_consts = sem("gn_consts")
            bn_step = sem("bn_step")
            bn_pow = sem("bn_pow")
            vk_evac = sem("vk_evac")
            q_evac = sem("q_evac")
            q_tr = sem("q_tr")
            q_placed = sem("q_placed")
            k_tr = sem("k_tr")
            k_max = sem("k_max")
            k_exp = sem("k_exp")
            k_rec = sem("k_rec")
            k_soft = sem("k_soft")

            with nc.Block() as block:
                @block.sync
                def _(sp):
                    for c in (0, 2):
                        sp.dma_start(xT[:, c, :], A["x"][c]).then_inc(x_in[c], 16)
                    for s in range(2):
                        g["w_load"](sp, s, s, False)
                    for c in (4, 6):
                        sp.dma_start(xT[:, c, :], A["x"][c]).then_inc(x_in[c], 16)
                    g["w_loads"](sp, 2, HB0 + 2)

                @block.gpsimd
                def _(pool):
                    nc.gpsimd.memset(zeros[:, :], 0.0).then_inc(memset_done, 1)
                    nc.gpsimd.memset(neghalf[:, :], -0.5).then_inc(memset_done, 1)
                    pool.wait_ge(memset_done, 2)
                    for s in range(2):
                        g["w_split"](pool, 0, s, False)
                    norm.power(0)
                    pool.wait_ge(bn_step, 1)
                    nc.gpsimd.tensor_tensor(bns[:, 1, :], bns[:, 0, :], neghalf[:, 0:10], ALU.pow).then_inc(bn_pow, 1)
                    norm.power(1)
                    g["w_splits"](pool, 2, HB0 + 2)

                @block.vector
                def _(dve):
                    def stats(c):
                        dve.wait_ge(x_in[c], 16)
                        norm.chunk_stats(c).then_inc(norm.stats, 1)

                    def after(c):
                        if c == 0:
                            dve.wait_ge(consts_in, 16 * 3)
                            dve.wait_ge(gn_consts, 16 * 2)
                            nc.vector.tensor_copy(identb[:, :], ident[:, :]).then_inc(q_placed, 1)
                            nc.vector.tensor_copy(maskb[:, :, :], maskf[:, :, :])
                            nc.vector.tensor_scalar(bns[:, 0, :], bn[:, 30:40], BN_EPS, None, ALU.add).then_inc(bn_step, 1)
                        if c < 4:
                            stats(c + 4)
                        if c == 3:
                            norm.aggregate(range(4, CK), CK)
                            norm.squares(1)
                            norm.variances(1)
                            norm.to_rows(1)
                            norm.coefficients(1)
                        if c == 4:
                            dve.wait_ge(bn_pow, 1)
                            nc.vector.tensor_tensor(bns[:, 2, :], bns[:, 1, :], bn[:, 0:10], ALU.mult).then_inc(bn_step, 1)
                        if c == 5:
                            dve.wait_ge(bn_step, 2)
                            nc.vector.tensor_tensor(bns[:, 3, :], bn[:, 20:30], bns[:, 2, :], ALU.mult).then_inc(bn_step, 1)
                        if c == 6:
                            dve.wait_ge(bn_step, 3)
                            nc.vector.tensor_tensor(bns[:, 3, :], bn[:, 10:20], bns[:, 3, :], ALU.subtract).then_inc(bn_step, 1)

                    for c in range(4):
                        stats(c)
                    norm.aggregate(range(4), 4)
                    norm.squares(0)
                    norm.variances(0)
                    norm.to_rows(0)
                    norm.coefficients(0)
                    norm.on_vector(xh, xl, ytmp, after, flush=(3,))

                    def soft_k(b):
                        dve.wait_ge(k_tr, b + 1)
                        nc.vector.tensor_reduce(kmax[:, b, :], PS[:, 6 + b % 2, :].rearrange("p (j m) -> p j m", j=2),
                                                AX, ALU.max, negate=True).then_inc(k_max, 1)
                        dve.wait_ge(k_exp, b + 1)
                        nc.vector.reciprocal(krec[:, b, :], ksum[:, b, :]).then_inc(k_rec, 1)
                        dve.wait_ge(k_rec, b + 1)
                        for jp in range(2):
                            last = nc.vector.tensor_scalar(ks[:, b, jp, :], ks[:, b, jp, :], krec[:, b, jp:jp + 1],
                                                           None, ALU.mult)
                        last.then_inc(k_soft, 1)

                    def place_q(jp):
                        for k in range(4):
                            j2, ph = k // 2, k % 2
                            dve.wait_ge(q_tr, 4 * jp + k + 1)
                            for bank in range(2):
                                for h2 in range(2):
                                    src = PS[64 * h2:64 * h2 + 64, 4 + bank, :].rearrange("p (c y x) -> p c y x", c=4, x=SIDE)
                                    dst = Qs[64 * j2:64 * j2 + 64, bass.ds(jp, 1), :]\
                                        .rearrange("p a (x y g h) -> p (a g) y x h", x=SIDE, y=SIDE, h=2)[
                                            :, 4 * bank:4 * bank + 4, 8 * ph:8 * ph + 8, :, h2]
                                    last = nc.vector.tensor_copy(dst, src)
                            last.then_inc(q_placed, 1)

                    for jp in range(2):
                        for b in (2 * jp, 2 * jp + 1):
                            soft_k(b)
                        place_q(jp)

                @block.scalar
                def _(act):
                    for c in (1, 3):
                        act.dma_start(xT[:, c, :], A["x"][c]).then_inc(x_in[c], 16)
                    act.dma_start(ident[:, :], A["ident"]).then_inc(gn_consts, 16)
                    act.dma_start(gmat[:, :], A["gmat"]).then_inc(gn_consts, 16)
                    for c in (5, 7):
                        act.dma_start(xT[:, c, :], A["x"][c]).then_inc(x_in[c], 16)
                    act.dma_start(maskf[:, :, :], A["mask"].rearrange("a p n -> p a n")).then_inc(consts_in, 16)
                    act.dma_start(bn[:, :], A["bn"]).then_inc(consts_in, 16)
                    act.dma_start(bias[:, :], A["bias"]).then_inc(consts_in, 16)
                    act.dma_start(ET[:, :, :], A["emb"]).then_inc(et_in, 16)
                    norm.on_scalar(xh, ytmp)
                    act.wait_ge(bn_step, 4)
                    for i, (dst, at) in enumerate(((VT[:, 0, :], 0), (VT[:, 1, :], 2), (KT[:, 0, :], 0), (KT[:, 1, :], 2))):
                        act.wait_ge(w_used, (3, 4, 6, 8)[i])
                        src = PS[:, at:at + 2, :].rearrange("p a n -> p (a n)")
                        if i < 2:
                            ins = nc.scalar.activation(dst, src, ACT.Identity, bias=bns[:, 3, 8 + i:9 + i],
                                                       scale=bns[:, 2, 8 + i:9 + i])
                        else:
                            dst = dst.rearrange("p (b j t) -> p b t j", b=B, j=4)
                            src = src.rearrange("p (b t j) -> p b t j", b=B, j=4)
                            ins = nc.scalar.activation(dst, src, ACT.Copy)
                        ins.then_inc(vk_evac, 1)

                    def exp_k(b):
                        act.wait_ge(k_max, b + 1)
                        for jp in range(2):
                            last = nc.scalar.activation(ks[:, b, jp, :], PS[:, 6 + b % 2, jp * N:jp * N + N], ACT.Exp,
                                                        bias=kmax[:, b, jp:jp + 1], accum_out=ksum[:, b, jp:jp + 1])
                        last.then_inc(k_exp, 1)

                    def evac_q(jp):
                        for k in range(4):
                            n = 4 * jp + k
                            at = 2 * (k % 2)
                            act.wait_ge(w_used, 2 * n + 10)
                            nc.scalar.activation(qT[:, k % 2, :], PS[:, at:at + 2, :].rearrange("p a n -> p (a n)"),
                                                 ACT.Identity, bias=bns[:, 3, bass.ds(n, 1)],
                                                 scale=bns[:, 2, bass.ds(n, 1)]).then_inc(q_evac, 1)

                    for jp in range(2):
                        for b in (2 * jp, 2 * jp + 1):
                            exp_k(b)
                        evac_q(jp)

                @block.tensor
                def _(pe):
                    def before(c):
                        if c == 4:
                            norm.averages(1)
                            norm.turn(1)

                    pe.wait_ge(gn_consts, 16 * 2)
                    norm.averages(0)
                    norm.turn(0)
                    block_pair(0, xh, xl, (0, 1), (2, 3), norm.ready, before)
                    for i in range(2, 4):
                        pe.wait_ge(vk_evac, i - 1)
                        block_product(2 * i, xh, xl, (2 * (i % 2), 2 * (i % 2) + 1))

                    def transpose_k(b):
                        for jp in range(2):
                            for mc in range(2):
                                src = KT[:, mc, b * N + jp * P:b * N + jp * P + P]
                                m = nc.tensor.transpose(PS[:, 6 + b % 2, jp * N + mc * P:jp * N + mc * P + P], src, ident[:, :])
                        m.then_inc(k_tr, 1)

                    def transpose_q(n, k):
                        pe.wait_ge(q_evac, n + 1)
                        pe.wait_ge(q_placed, n + 1)
                        for tt in range(8):
                            m = nc.tensor.transpose(PS[:, 4 + tt // 4, (tt % 4) * P:(tt % 4) * P + P],
                                                    qT[:, k % 2, tt * P:tt * P + P], ident[:, :])
                        m.then_inc(q_tr, 1)

                    pe.wait_ge(vk_evac, 4)
                    for jp in range(2):
                        if jp:
                            pe.wait_ge(k_exp, 2)
                        for b in (2 * jp, 2 * jp + 1):
                            transpose_k(b)
                        for k in range(4):
                            n = 4 * jp + k
                            if n >= 2:
                                pe.wait_ge(q_evac, n - 1)
                            block_product(8 + 2 * n, xh, xl, (2 * (k % 2), 2 * (k % 2) + 1))
                            if n >= 1:
                                transpose_q(n - 1, (k - 1) % 4)
                    transpose_q(7, 3)

        with ExitStack() as ctx:
            AT = sb(ctx, "AT", [P, 2, B * HEADS0 * N])
            G = sb(ctx, "G", [P, 2, 8, DY * SIDE])
            A2 = sb(ctx, "A2", [P, 4, 8, N])
            c0 = sb(ctx, "c0", [32, 8, 4, 4])
            c1 = sb(ctx, "c1", [32, 8, 2, 8])
            c2 = sb(ctx, "c2", [32, 8, 8, 8])
            c3 = sb(ctx, "c3", [32, 8, 4, 4])
            tA = sb(ctx, "tA", [32, 256])
            tB = sb(ctx, "tB", [32, 1024])
            cores_in = sem("cores_in")
            mul_done = sem("mul_done")
            add_done = sem("add_done")
            shifted = [sem(f"shifted{u}") for u in range(4)]
            pe_group = sem("pe_group")
            act_evac = sem("act_evac")
            dve_evac = sem("dve_evac")
            x_sum = sem("x_sum")

            groups = []
            for u in range(4):
                for xi in range(8):
                    groups.append(("G", (u, xi), "act" if xi % 2 else "dve"))
            for b in range(B):
                for mc in range(2):
                    for nh in range(2):
                        groups.append(("K", (b, mc, nh), "act" if nh else "dve"))
            for u in range(4):
                for xg in range(2):
                    for mc in range(2):
                        groups.append(("A", (u, xg, mc), "dve"))
            for nh in range(2):
                for vt in range(2):
                    for b in range(B):
                        groups.append(("Y", (b, vt, nh), "dve"))
            seen = {"act": 0, "dve": 0}
            evac_at = []
            for _, _, e in groups:
                seen[e] += 1
                evac_at.append((e, seen[e]))
            bank_of = [i % 8 if kind != "Y" else (0, 1, 2, 3, 4, 5, 7)[i % 7] for i, (kind, _, _) in enumerate(groups)]
            before_it = [max((k for k in range(i) if bank_of[k] == bank_of[i]), default=None) for i in range(len(groups))]
            evac_sem = {"act": act_evac, "dve": dve_evac}

            def evacuated(eng, i):
                e, k = evac_at[i]
                eng.wait_ge(evac_sem[e], k)

            def a_view(mc, u, xg):
                yg, x0 = u // 2, 8 * (u % 2) + 4 * xg
                v = AT[:, mc, :].rearrange("p (g y x) -> p x y g", y=SIDE, x=SIDE)
                return v[:, x0:x0 + 4, 8 * yg:8 * yg + 8, :]

            def next_stats(eng, i):
                b, vt, nh = groups[i][1]
                evacuated(eng, i)
                chunks = (4 * nh + vt, 4 * nh + 2 + vt)
                for c in chunks:
                    norms[1].chunk_stats(c, (b,)).then_inc(norms[1].stats, 1)
                if b == B - 1:
                    norms[1].aggregate(chunks, 8 * (2 * nh + vt + 1))
                k = i - (len(groups) - 16)
                if k == 7:
                    norms[1].squares(0)
                if k == 9:
                    norms[1].variances(0)
                if k == 10:
                    norms[1].to_rows(0)
                if k == 12:
                    norms[1].coefficients(0)

            def read_out(eng, name):
                for i, (kind, d, e) in enumerate(groups):
                    if e != name:
                        continue
                    bank = PS[:, bank_of[i], :]
                    eng.wait_ge(pe_group, i + 1)
                    if kind == "G":
                        u, xi = d
                        if u >= 2:
                            eng.wait_ge(shifted[u - 2], 128)
                        dst, src = G[:, u % 2, xi, :], bank[:, 0:DY * SIDE]
                    elif kind == "K":
                        b, mc, nh = d
                        dst = AT[:, mc, b * C:b * C + C].rearrange("p (h y x) -> p x y h", y=SIDE, x=SIDE)[
                            :, 8 * nh:8 * nh + 8, :, :]
                        src = bank.rearrange("p (x y h) -> p x y h", x=8, y=SIDE)
                    if kind in "GK":
                        ins = nc.scalar.activation(dst, src, ACT.Copy) if name == "act" else nc.vector.tensor_copy(dst, src)
                    elif kind == "A":
                        u, xg, mc = d
                        if (u, xg, mc) == (0, 0, 0):
                            eng.wait_ge(act_evac, 24)
                            eng.wait_ge(dve_evac, 24)
                        v = a_view(mc, u, xg)
                        ins = nc.vector.tensor_tensor(v, bank.rearrange("p (x y g) -> p x y g", x=4, y=8), v, ALU.add)
                    else:
                        b, vt, nh = d
                        v = xT[:, :, b * N:(b + 1) * N].rearrange("p (h v) n -> p v h n", v=2)[:, vt, 2 * nh:2 * nh + 2, :]
                        ins = nc.vector.tensor_tensor(v, bank.rearrange("p (h n) -> p h n", h=2), v, ALU.add)
                    ins.then_inc(evac_sem[name], 1)
                    if kind == "Y" and d != (0, 0, 0):
                        next_stats(eng, i - 1)

            def shift(eng, u, ys):
                for i in range(8 * u, 8 * u + 8):
                    evacuated(eng, i)
                for y in ys:
                    rows = slice(16 * y, 16 * y + 16)
                    eng.dma_start(A2[rows, u, :, :], G[rows, u % 2, :, (7 - y) * SIDE:(7 - y) * SIDE + N])\
                        .then_inc(shifted[u], 16)

            with nc.Block() as block:
                @block.sync
                def _(sp):
                    sp.dma_start(c0[:, :, :, :].rearrange("p a b c -> p (a b c)"), A["c0"].partition_broadcast(32)).then_inc(cores_in, 16)
                    sp.dma_start(c3[:, :, :, :].rearrange("p a b c -> p (a b c)"), A["c3"].partition_broadcast(32)).then_inc(cores_in, 16)
                    sp.dma_start(c1[:, :, :, :].rearrange("p a b c -> p (a b c)"), A["c1"]).then_inc(cores_in, 16)
                    for r in range(4):
                        sp.dma_start(c2[r:32:4, :, :, :].rearrange("p a b c -> p (a b c)"), A["c2"]).then_inc(cores_in, 16)
                    for u in range(4):
                        shift(sp, u, range(8))

                @block.gpsimd
                def _(pool):
                    pool.wait_ge(cores_in, 16 * 7)
                    muls, adds = Count(mul_done), Count(add_done)
                    for r in range(RANK):
                        to = tA if r else ttA
                        if r:
                            pool.wait_ge(add_done, adds.n)
                        for a in range(4):
                            o = to[:, 64 * a:64 * a + 64].rearrange("p (h o q) -> p h o q", h=2, o=4)
                            i0 = c0[:, r, a, :].rearrange("p (h o q) -> p h o q", h=1, q=1).broadcast_to([32, 2, 4, 8])
                            i1 = c1[:, r, :, :].rearrange("p h (o q) -> p h o q", o=1).broadcast_to([32, 2, 4, 8])
                            last = nc.gpsimd.tensor_tensor(o, i0, i1, ALU.mult)
                        muls.up(last)
                        pool.wait_ge(mul_done, muls.n)
                        if r:
                            adds.up(nc.gpsimd.tensor_tensor(ttA[:, :], ttA[:, :], tA[:, :], ALU.add))
                    for r in range(RANK):
                        to = tB if r else ttB
                        if r:
                            pool.wait_ge(add_done, adds.n)
                        for o2 in range(8):
                            o = to[:, 128 * o2:128 * o2 + 128].rearrange("p (o c q) -> p o c q", o=4, c=8)
                            i0 = c2[:, r, o2, :].rearrange("p (o c q) -> p o c q", o=1, q=1).broadcast_to([32, 4, 8, 4])
                            i1 = c3[:, r, :, :].rearrange("p o (c q) -> p o c q", c=1).broadcast_to([32, 4, 8, 4])
                            last = nc.gpsimd.tensor_tensor(o, i0, i1, ALU.mult)
                        muls.up(last)
                        pool.wait_ge(mul_done, muls.n)
                        if r:
                            adds.up(nc.gpsimd.tensor_tensor(ttB[:, :], ttB[:, :], tB[:, :], ALU.add))
                    norms[1].power(0)

                @block.scalar
                def _(act):
                    read_out(act, "act")

                @block.vector
                def _(dve):
                    read_out(dve, "dve")
                    evacuated(dve, len(groups) - 1)

                @block.tensor
                def _(pe):
                    pe.wait_ge(et_in, 16)
                    for i, (kind, d, _) in enumerate(groups):
                        bank = PS[:, bank_of[i], :]
                        if before_it[i] is not None:
                            evacuated(pe, before_it[i])
                        if kind == "G":
                            u, xi = d
                            yg, x = u // 2, 8 * (u % 2) + xi
                            d0 = (1 - yg) * 8
                            for jp in range(2):
                                lhs = Qs[:, jp, x * N + yg * P:x * N + yg * P + P]
                                rhs = ET[:, jp, :].rearrange("p (a b) -> p a b", a=31)[:, d0:d0 + DY, 15 - x:31 - x]
                                m = nc.tensor.matmul(bank[:, 0:DY * SIDE], lhs, rhs, start=jp == 0, stop=jp == 1)
                        elif kind == "K":
                            b, mc, nh = d
                            for jp in range(2):
                                rhs = Qs[:, jp, :].rearrange("p (x y g) -> p x y g", x=SIDE, y=SIDE)[
                                    :, 8 * nh:8 * nh + 8, :, HEADS0 * b:HEADS0 * b + HEADS0]
                                m = nc.tensor.matmul(bank, ks[:, b, jp, mc * P:mc * P + P], rhs,
                                                     start=jp == 0, stop=jp == 1)
                        elif kind == "A":
                            u, xg, mc = d
                            if xg == 0 and mc == 0:
                                pe.wait_ge(shifted[u], 128)
                            for xi in range(4):
                                m = nc.tensor.transpose(bank[:, xi * P:xi * P + P], A2[:, u, 4 * xg + xi, mc * P:mc * P + P], ident[:, :])
                        else:
                            b, vt, nh = d
                            if b == vt == nh == 0:
                                pe.wait_ge(dve_evac, 24 + 16)
                            for mc in range(2):
                                m = nc.tensor.matmul(bank, VT[:, mc, b * N + vt * P:b * N + vt * P + P],
                                                     AT[:, mc, b * C + nh * HALF:b * C + nh * HALF + HALF],
                                                     start=mc == 0, stop=mc == 1)
                        m.then_inc(pe_group, 1)
                        if kind == "Y" and i == len(groups) - 6:
                            norms[1].averages(0)
                        if kind == "Y" and i == len(groups) - 4:
                            norms[1].turn(0)


def layer12(nc, A, outer, g, layer):
    PS, xT, ident, identb, maskb, bias = (g[x] for x in ("PS", "xT", "ident", "identb", "maskb", "bias"))
    sem, sb, norms, w_used = (g[x] for x in ("sem", "sb", "norms", "w_used"))
    chunk_product, block_product, block_pair = g["chunk_product"], g["block_product"], g["block_pair"]
    norm = norms[layer]
    masked = layer == 1
    n0 = HB0 if masked else HB0 + HB1
    per_pass = 16 if masked else 8
    n1 = n0 + (HB1 if masked else HB2)
    PJ, S, PT, O = (0, 1), 2, 4, 6
    SCALE = 64 ** -0.5

    def q_block(j, second):
        return 6 * j + (n0 + 2 + (per_pass if second else 0))

    def spans(ahead):
        if not masked:
            return ((0, N), (0, N))
        return ((0, N), (P, N)) if ahead else ((0, P), (0, N))

    def tiles(ahead):
        at, r = 0, []
        for kt in range(2):
            for qt in range(2):
                lo, hi = spans(ahead)[qt]
                if lo <= kt * P < hi:
                    r.append((kt, qt, at))
                    at += P
        return r

    with ExitStack() as ctx:
        xh = sb(ctx, "xh", [P, CK, T], F32R)
        xl = sb(ctx, "xl", [P, CK, T], F32R)
        ytmp = sb(ctx, "ytmp", [P, 2, T])
        o_shape = [P, CK, HALF] if masked else [P, PAIRS // 2, T]
        oh = sb(ctx, "oh", o_shape, F32R)
        ol = sb(ctx, "ol", o_shape, F32R)
        vT = sb(ctx, "vT", [P, T])
        v = sb(ctx, "v", [P, CK, P])
        prob = sb(ctx, "prob", [P, 2, 2, N])
        probT = sb(ctx, "probT", [P, 4, HALF])
        nmax = sb(ctx, "nmax", [P, 2, 2])
        psum_ = sb(ctx, "psum", [P, 2, 2])
        prec = sb(ctx, "prec", [P, 2, 2])
        if masked:
            qh = sb(ctx, "qh", [P, 2, T], F32R)
            ql = sb(ctx, "ql", [P, 2, T], F32R)
            kh = sb(ctx, "kh", [P, T], F32R)
            kl = sb(ctx, "kl", [P, T], F32R)
        else:
            qp = sb(ctx, "qp", [P, T])
            q = sb(ctx, "qa", [KROWS, 2, T])
            k = sb(ctx, "ka", [KROWS, 2, T])
            rel = sb(ctx, "rel", [P, 2, 64])
            kb = sb(ctx, "kb", [P, PAIRS])

        v_evac = sem("v_evac")
        v_tr = sem("v_tr")
        v_ready = sem("v_ready")
        q_evac = sem("q_evac")
        qa_evac = sem("qa_evac")
        k_evac = sem("k_evac")
        k_half = sem("k_half")
        rel_done = sem("rel_done")
        split_done = sem("split_done")
        relh_evac = sem("relh_evac")
        relw_evac = sem("relw_evac")
        s_done = sem("s_done")
        p_max = sem("p_max")
        p_exp = sem("p_exp")
        p_rec = sem("p_rec")
        p_norm = sem("p_norm")
        t_done = sem("t_done")
        t_evac = sem("t_evac")
        o_done = sem("o_done")
        o_hi = sem("o_hi")
        o_ready = sem("o_ready")
        sum_done = sem("sum_done")
        tables_in = sem("tables_in")
        kb_ready = sem("kb_ready")
        zeroed = sem("zeroed")

        def pairs(eng, take_q, step, out_pass):
            take_q(0, n0 + 2)
            step(0, False, True)
            with eng.Fori(1, PAIRS // 2) as j:
                take_q(j, q_block(j, False))
                step(j, False, True)
            take_q(PAIRS // 2, q_block(PAIRS // 2, False))
            out_pass(0)
            step(PAIRS // 2, True, True)
            with eng.Fori(PAIRS // 2 + 1, PAIRS - 1) as j:
                take_q(j, q_block(j, True))
                step(j, True, True)
            take_q(PAIRS - 1, q_block(PAIRS - 1, True))
            step(PAIRS - 1, True, False)
            out_pass(1)

        def pass_block(half):
            return n0 + 2 + 24 + 2 if half == 0 else n1 - per_pass

        def k_banks(more):
            return (S, S + 1) if more else (S, 0)

        def k_products(eng, j, n, bank, more):
            if not more and not bank:
                eng.wait_ge(k_half, 1)
            elif not (more and bank):
                eng.wait_ge(w_used, n + 4)

        with nc.Block() as block:
            @block.sync
            def _(sp):
                if not masked:
                    sp.dma_start(rel[:, :, :], A["rel"].rearrange("a p n -> p a n")).then_inc(tables_in, 16)
                    for hh in range(2):
                        sp.dma_start(k[64:KROWS, hh, :], A["hot"]).then_inc(tables_in, 16)
                g["w_loads"](sp, n0 + 2, min(n1 + 2, HB_TOTAL))

            @block.gpsimd
            def _(pool):
                norm.power(1)
                g["w_splits"](pool, n0 + 2, n1)
                norms[layer + 1].power(0)
                if masked:
                    g["w_splits"](pool, n1, n1 + 2)

            @block.scalar
            def _(act):
                norm.on_scalar(xh, ytmp)

                def take_q(j, n):
                    both = PS[:, 0:2, :].rearrange("p a n -> p (a n)")
                    act.wait_ge(w_used, n + 2)
                    if masked:
                        for hh in range(2):
                            rows = slice(64 * hh, 64 * hh + 64)
                            last = nc.scalar.activation(qh[rows, hh, :], PS[rows, 0:2, :].rearrange("p a n -> p (a n)"), ACT.Copy)
                        last.then_inc(q_evac, 1)
                    else:
                        nc.scalar.activation(qp[:, :], both, ACT.Identity, bias=bias[:, bass.ds(j, 1)])\
                            .then_inc(q_evac, 1)

                def step(j, ahead, more):
                    n = q_block(j, ahead)
                    if not masked:
                        act.wait_ge(rel_done, j + 1)
                        for bank in range(2):
                            for hh in range(2):
                                src = PS[32 * hh:32 * hh + SIDE, O + bank, :].rearrange("p (h b w) -> p h b w", h=8, b=B)
                                dst = q[64:64 + SIDE, hh, :].rearrange("p (b h w) -> p h b w", b=B, h=SIDE)[
                                    :, 8 * bank:8 * bank + 8, :, :]
                                last = nc.scalar.activation(dst, src, ACT.Copy)
                        last.then_inc(relh_evac, 1)
                    def evac_k(half):
                        bank, part = k_banks(more)[half], slice(half * HALF, half * HALF + HALF)
                        k_products(act, j, n, half, more)
                        if masked:
                            last = nc.scalar.activation(kh[:, part], PS[:, bank, :], ACT.Copy, scale=SCALE)
                        else:
                            for hh in range(2):
                                rows = slice(64 * hh, 64 * hh + 64)
                                last = nc.scalar.activation(k[0:64, hh, part], PS[rows, bank, :], ACT.Identity,
                                                            bias=kb[rows, bass.ds(j, 1)], scale=SCALE)
                        last.then_inc(k_evac, 1)

                    evac_k(0)
                    if more:
                        evac_k(1)

                    def evac_t(u):
                        act.wait_ge(t_done, 8 * j + u + 1)
                        w = P * len(tiles(ahead))
                        nc.scalar.activation(probT[:, u % 4, 0:w], PS[:, PT + u % 2, 0:w], ACT.Copy).then_inc(t_evac, 1)

                    for u in range(UNITS):
                        if u == 3 and not more:
                            evac_k(1)
                        act.wait_ge(p_max, 8 * j + u + 1)
                        for qt, (lo, hi) in enumerate(spans(ahead)):
                            last = nc.scalar.activation(prob[:, u % 2, qt, lo:hi], PS[:, S + u % 2, qt * N + lo:qt * N + hi],
                                                        ACT.Exp, bias=nmax[:, u % 2, qt:qt + 1],
                                                        accum_out=psum_[:, u % 2, qt:qt + 1])
                        last.then_inc(p_exp, 1)
                        if u:
                            evac_t(u - 1)
                    evac_t(UNITS - 1)

                pairs(act, take_q, step, lambda half: None)

            @block.vector
            def _(dve):
                nc.vector.memset(nmax[:, :, :], 0.0).then_inc(sum_done, 2)
                nc.vector.memset(psum_[:, :, :], 0.0).then_inc(o_ready, 1)

                def after(c):
                    if c == 0 and not masked:
                        norm.chunk_stats(7).then_inc(norm.stats, 1)
                        norm.aggregate((6, 7), CK)
                    elif c == 0:
                        for k in (5, 7):
                            norm.chunk_stats(k, (B - 1,)).then_inc(norm.stats, 1)
                        norm.aggregate((5, 7), 32)
                    if c == 0:
                        norm.squares(1)
                    if c == 1:
                        norm.variances(1)
                    if c == 2:
                        norm.to_rows(1)
                    if c == 3:
                        norm.coefficients(1)

                norm.on_vector(xh, xl, ytmp, after)
                if masked:
                    for t in (qh, ql):
                        nc.vector.memset(t[64:P, 0, :].bitcast(F32), 0.0)
                        last = nc.vector.memset(t[0:64, 1, :].bitcast(F32), 0.0)
                    last.then_inc(zeroed, 1)
                else:
                    nc.vector.memset(q[64:96, :, :], 0.0).then_inc(zeroed, 1)
                    nc.vector.tensor_scalar(kb[:, :], bias[:, 8:16], SCALE, None, ALU.mult).then_inc(kb_ready, 1)

                def evac_v(j, used, bank):
                    dve.wait_ge(w_used, used)
                    both = PS[:, bank:bank + 2, :].rearrange("p a n -> p (a n)")
                    if masked:
                        ins = nc.vector.tensor_copy(vT[:, :], both)
                    else:
                        ins = nc.vector.tensor_scalar(vT[:, :], both, bias[:, bass.ds(j + 16, 1)], None, ALU.add)
                    ins.then_inc(v_evac, 1)

                def evac_o(j, half, grp):
                    dve.wait_ge(o_done, 2 * j + grp + 1)
                    jl = j - half * (PAIRS // 2)
                    src = PS[:, O + grp, :]
                    if masked:
                        src = src.rearrange("p (b r c) -> p b r c", b=2, c=CK)
                        hi, lo = (t[:, :, :].rearrange("p c (b j r) -> p b j r c", b=B, j=4)[
                            :, 2 * grp:2 * grp + 2, bass.ds(jl, 1), :, :].rearrange("p b j r c -> p b (j r) c") for t in (oh, ol))
                    else:
                        hi, lo = (t[:, bass.ds(jl, 1), HALF * grp:HALF * grp + HALF].rearrange("p a n -> p (a n)") for t in (oh, ol))
                    nc.vector.tensor_copy(hi, src).then_inc(o_hi, 1)
                    dve.wait_ge(o_hi, 2 * j + grp + 1)
                    nc.vector.tensor_tensor(lo, src, hi.bitcast(F32), ALU.subtract).then_inc(o_ready, 1)

                def take_q(j, n):
                    dve.wait_ge(q_evac, j + 1)
                    if masked:
                        for hh in range(2):
                            rows = slice(64 * hh, 64 * hh + 64)
                            last = nc.vector.tensor_tensor(ql[rows, hh, :], PS[rows, 0:2, :].rearrange("p a n -> p (a n)"),
                                                           qh[rows, hh, :].bitcast(F32), ALU.subtract)
                        last.then_inc(qa_evac, 1)
                    else:
                        for hh in range(2):
                            rows = slice(64 * hh, 64 * hh + 64)
                            last = nc.vector.tensor_scalar(q[0:64, hh, :], PS[rows, 0:2, :].rearrange("p a n -> p (a n)"),
                                                           bias[rows, bass.ds(j, 1)], None, ALU.add)
                        last.then_inc(qa_evac, 1)

                def step(j, ahead, more):
                    n = q_block(j, ahead)

                    def rest_of_k(half):
                        part = slice(half * HALF, half * HALF + HALF)
                        dve.wait_ge(k_evac, 2 * j + half + 1)
                        nc.vector.scalar_tensor_tensor(kl[:, part], PS[:, k_banks(more)[half], :], SCALE,
                                                       kh[:, part].bitcast(F32), ALU.mult, ALU.subtract).then_inc(split_done, 1)

                    dve.wait_ge(v_tr, j + 1)
                    nc.vector.tensor_copy(v[:, :, :].rearrange("p a n -> p (a n)"),
                                          PS[:, PT:PT + 2, :].rearrange("p a n -> p (a n)")).then_inc(v_ready, 1)
                    if masked:
                        rest_of_k(0)
                        if more:
                            rest_of_k(1)
                    else:
                        dve.wait_ge(rel_done, j + 1)
                        for bank in range(2):
                            for hh in range(2):
                                src = PS[64 + 32 * hh:64 + 32 * hh + SIDE, O + bank, :].rearrange("p (w b h) -> p w b h", w=8, b=B)
                                dst = q[96:96 + SIDE, hh, :].rearrange("p (b h w) -> p w b h", b=B, h=SIDE)[
                                    :, 8 * bank:8 * bank + 8, :, :]
                                last = nc.vector.tensor_copy(dst, src)
                        last.then_inc(relw_evac, 1)
                    for u in range(UNITS):
                        unit = 8 * j + u + 1
                        if masked and u == 3 and not more:
                            rest_of_k(1)
                        dve.wait_ge(s_done, unit)
                        if masked:
                            for qt, (lo, hi) in enumerate(spans(ahead)):
                                last = nc.vector.tensor_reduce(nmax[:, u % 2, qt:qt + 1], PS[:, S + u % 2, qt * N + lo:qt * N + hi],
                                                               AX, ALU.max, negate=True)
                        else:
                            last = nc.vector.tensor_reduce(nmax[:, u % 2, :], PS[:, S + u % 2, :].rearrange("p (a n) -> p a n", a=2),
                                                           AX, ALU.max, negate=True)
                        last.then_inc(p_max, 1)
                        dve.wait_ge(p_exp, unit)
                        nc.vector.reciprocal(prec[:, u % 2, :], psum_[:, u % 2, :]).then_inc(p_rec, 1)
                        dve.wait_ge(p_rec, unit)
                        for qt, (lo, hi) in enumerate(spans(ahead)):
                            last = nc.vector.tensor_scalar(prob[:, u % 2, qt, lo:hi], prob[:, u % 2, qt, lo:hi],
                                                           prec[:, u % 2, qt:qt + 1], None, ALU.mult)
                        last.then_inc(p_norm, 1)
                        if u == 5:
                            evac_o(j, int(ahead), 0)
                    if more:
                        evac_v(j + 1, n + 6, 0)
                    evac_o(j, int(ahead), 1)

                def out_pass(half):
                    base = 2 + CK * half
                    n = pass_block(half)

                    def sums(o, s):
                        x = xT[:, bass.ds(o, 1), :]
                        if masked:
                            dve.wait_ge(w_used, n + 2 * o + 2)
                            x = x.rearrange("p a (b r) -> p (a b) r", b=B)[:, :, half * P:half * P + P]
                            nc.vector.tensor_tensor(x, PS[:, s, :].rearrange("p (b r) -> p b r", b=B), x, ALU.add)\
                                .then_inc(sum_done, 1)
                        else:
                            dve.wait_ge(w_used, n + o + 1)
                            x = x.rearrange("p a n -> p (a n)")
                            src = PS[:, 2 * s:2 * s + 2, :].rearrange("p a n -> p (a n)")
                            if half:
                                ins = nc.vector.scalar_tensor_tensor(x, src, bias[:, bass.ds(o + 24, 1)], x, ALU.add, ALU.add)
                            else:
                                ins = nc.vector.tensor_tensor(x, src, x, ALU.add)
                            ins.then_inc(sum_done, 1)

                    def stats(o):
                        dve.wait_ge(sum_done, base + o + 1)
                        nxt.chunk_stats(o).then_inc(nxt.stats, 1)

                    nxt = norms[layer + 1]
                    if not half:
                        with dve.Fori(0, CK // 2) as i:
                            for s in range(2):
                                sums(2 * i + s, s)
                    else:
                        with dve.Fori(0, CK // 2 - 1) as i:
                            for s in range(2):
                                sums(2 * i + s, s)
                                stats(2 * i + s)
                        nxt.aggregate(range(6), 6)
                        nxt.squares(0)
                        sums(6, 0)
                        nxt.variances(0)
                        stats(6)
                        nxt.to_rows(0)
                        sums(7, 1)
                        nxt.coefficients(0)
                        dve.wait_ge(sum_done, base + CK)

                evac_v(0, n0 + 3, S)
                pairs(dve, take_q, step, out_pass)

            @block.tensor
            def _(pe):
                def before(c):
                    if c == 1:
                        norm.averages(1)
                    if c == 3:
                        norm.turn(1)

                block_pair(n0, xh, xl, (S, S + 1), PJ, norm.ready, before)
                if not masked:
                    pe.wait_ge(tables_in, 48)

                def scores(j, u, ahead):
                    b, hh = u // 2, u % 2
                    for qt, (lo, hi) in enumerate(spans(ahead)):
                        at = qt * N
                        qs, ks = slice(b * N + qt * P, b * N + qt * P + P), slice(b * N + lo, b * N + hi)
                        if not masked:
                            m = nc.tensor.matmul(PS[:, S + u % 2, at + lo:at + hi], q[:, hh, qs], k[:, hh, ks],
                                                 start=True, stop=True)
                        else:
                            for i, (x, y) in enumerate(((qh, kh), (qh, kl), (ql, kh))):
                                nc.tensor.matmul(PS[:, S + u % 2, at + lo:at + hi], x[:, hh, qs], y[:, ks],
                                                 start=i == 0, stop=False)
                            m = nc.tensor.matmul(PS[:, S + u % 2, at + qt * P:at + qt * P + P], identb[:, :],
                                                 maskb[:, int(ahead), :], start=False, stop=True)
                    m.then_inc(s_done, 1)

                def transposed(j, u, ahead):
                    pe.wait_ge(p_norm, 8 * j + u + 1)
                    for kt, qt, at in tiles(ahead):
                        m = nc.tensor.transpose(PS[:, PT + u % 2, at:at + P], prob[:, u % 2, qt, kt * P:kt * P + P], ident[:, :])
                    m.then_inc(t_done, 1)

                def outputs(j, u0, ahead):
                    b, bank = u0 // 2, O + u0 // 4
                    pe.wait_ge(t_evac, 8 * j + u0 + 2)
                    if not masked:
                        for kt in range(2):
                            for hh in range(2):
                                m = nc.tensor.matmul(PS[64 * hh:64 * hh + 64, bank, (b % 2) * N:(b % 2) * N + N],
                                                     v[:, 2 * b + kt, 64 * hh:64 * hh + 64],
                                                     probT[:, (u0 + hh) % 4, kt * N:kt * N + N],
                                                     start=kt == 0, stop=kt == 1)
                    else:
                        whole, part = (1, 0) if ahead else (0, 1)
                        w_at, p_at, p_col = (P, 0, 0) if ahead else (0, N, 64)
                        for u in (u0, u0 + 1):
                            hh, col = u % 2, (u % 4) * P
                            for kt, at, width, to in ((whole, w_at, N, col), (part, p_at, P, col + p_col)):
                                for r in range(2):
                                    m = nc.tensor.matmul(PS[64 * r:64 * r + 64, bank, to:to + width // 2],
                                                         v[:, 2 * b + kt, 64 * hh:64 * hh + 64],
                                                         probT[:, u % 4, at + r:at + width:2],
                                                         start=kt == whole, stop=kt == part)
                    if u0 % 4 == 2:
                        m.then_inc(o_done, 1)

                def take_q(j, n):
                    pe.wait_ge(v_evac, j + 1)
                    if not (isinstance(j, int) and j == 0):
                        block_product(n, xh, xl, PJ)

                def step(j, ahead, more):
                    n = q_block(j, ahead)
                    for tt in range(CK):
                        m = nc.tensor.transpose(PS[:, PT + tt // 4, (tt % 4) * P:(tt % 4) * P + P],
                                                vT[:, tt * P:tt * P + P], ident[:, :])
                    m.then_inc(v_tr, 1)
                    k_bank = (S, S + 1) if more else (S,)
                    block_product(n + 2, xh, xl, k_bank, range(4), used=more)
                    pe.wait_ge(q_evac, j + 1)
                    pe.wait_ge(qa_evac, j + 1)
                    if not masked:
                        pe.wait_ge(o_ready, 2 * j + 1)
                        for i in range(SIDE):
                            bank, cols = O + i // 8, slice((i % 8) * 64, (i % 8) * 64 + 64)
                            of_row = qp[:, :].rearrange("p (b h w) -> p h b w", b=B, h=SIDE)[:, i, :, :]
                            of_col = qp[:, :].rearrange("p (b h w) -> p w b h", b=B, h=SIDE)[:, i, :, :]
                            nc.tensor.matmul(PS[0:48, bank, cols], rel[:, 0, 15 - i:63 - i], of_row, start=True, stop=True)
                            m = nc.tensor.matmul(PS[64:112, bank, cols], rel[:, 1, 15 - i:63 - i], of_col, start=True, stop=True)
                        m.then_inc(rel_done, 1)
                    last = block_product(n + 2, xh, xl, k_bank, range(4, CK), used=more)
                    if not more:
                        last.then_inc(k_half, 1)

                    def next_v(c):
                        if more:
                            chunk_product(n + 4 + c // 4, c // 4, c % 4, c, xh, xl, PJ, c == 0, c == CK - 1)

                    def second_half(chunks):
                        if not more:
                            block_product(n + 2, xh[:, :, HALF:T], xl[:, :, HALF:T], (0,), chunks)

                    next_v(0)
                    if not masked:
                        pe.wait_ge(relh_evac, j + 1)
                        pe.wait_ge(relw_evac, j + 1)
                    for u in range(UNITS):
                        if u in ((0, 1) if more else (0, 4)):
                            half = int(u > 0)
                            pe.wait_ge(k_evac, 2 * j + half + 1)
                            if masked:
                                pe.wait_ge(split_done, 2 * j + half + 1)
                        scores(j, u, ahead)
                        if u < 3:
                            second_half(range(3 * u, min(3 * u + 3, CK)))
                        if u:
                            next_v(u)
                            if u == 1:
                                pe.wait_ge(v_ready, j + 1)
                            transposed(j, u - 1, ahead)
                        if u >= 3 and u % 2:
                            outputs(j, u - 3, ahead)
                    transposed(j, UNITS - 1, ahead)
                    outputs(j, UNITS - 2, ahead)

                def out_pass(half):
                    pe.wait_ge(o_ready, 8 * half + 9)
                    if half == 0:
                        pe.wait_ge(q_evac, PAIRS // 2 + 1)
                        pe.wait_ge(qa_evac, PAIRS // 2 + 1)
                    n = pass_block(half)

                    def out_block(o, s):
                        pe.wait_ge(sum_done, CK * half + o + 1)
                        if masked:
                            block_product(n + 2 * o, oh, ol, (s,))
                        else:
                            for c in range(4):
                                chunk_product(n + o, s, c, c, oh, ol, (2 * s, 2 * s + 1), c == 0, c == 3)

                    with pe.Fori(0, CK // 2 - half) as i:
                        for s in range(2):
                            out_block(2 * i + s, s)
                    if half:
                        out_block(6, 0)
                        norms[layer + 1].averages(0)
                        out_block(7, 1)
                        norms[layer + 1].turn(0)
                    if half == 0:
                        pe.wait_ge(sum_done, 2 + CK)

                pairs(pe, take_q, step, out_pass)


def layer3(nc, A, out, outer, g):
    PS, xT, bias, ttA, ttB = (g[x] for x in ("PS", "xT", "bias", "ttA", "ttB"))
    sem, sb, norms = (g[x] for x in ("sem", "sb", "norms"))
    norm = norms[3]
    O23, O01 = 32, 32
    QUART = 8
    with ExitStack() as ctx:
        xh = sb(ctx, "xh", [P, CK, T], F32R)
        xl = sb(ctx, "xl", [P, CK, T], F32R)
        ytmp = sb(ctx, "ytmp", [P, 2, T])
        Mh = sb(ctx, "Mh", [P, CK, C], F32R)
        Ml = sb(ctx, "Ml", [P, CK, C], F32R)
        BD = sb(ctx, "BD", [32, 2, QUART, P])
        U = sb(ctx, "U", [P, 2, 2, C])
        K = sb(ctx, "K", [P, 2, N])
        kt = sb(ctx, "kt", [P, 2, N])
        kx = sb(ctx, "kx", [P, 3, SIDE])
        kxt = sb(ctx, "kxt", [P, 3, SIDE])
        taps = sb(ctx, "taps", [P, 9])
        near_x = sb(ctx, "near_x", [P, 3, SIDE])
        near_y = sb(ctx, "near_y", [P, 3, 2, SIDE])
        r2c = sb(ctx, "r2c", [32, 4])
        act_out = ytmp[:, :, 0:2 * N].rearrange("p a (s n) -> p a s n", s=2)
        consts3 = sem("consts3")
        bd_ready = sem("bd_ready")
        m_done = sem("m_done")
        m_hi = sem("m_hi")
        m_lo = sem("m_lo")
        k_step = sem("k_step")
        k_ready = sem("k_ready")
        u_done = sem("u_done")
        u_act = sem("u_act")
        u_dve = sem("u_dve")
        f_done = sem("f_done")
        relu_done = sem("relu_done")
        x_final = sem("x_final")
        stored = sem("stored")

        with nc.Block() as block:
            @block.sync
            def _(sp):
                sp.dma_start(r2c[:, :], A["r2c"]).then_inc(consts3, 16)
                sp.dma_start(taps[:, :], A["taps"].partition_broadcast(P)).then_inc(consts3, 16)
                sp.dma_start(near_x[:, :, :].rearrange("p a b -> p (a b)"), A["near_x"]).then_inc(consts3, 16)
                sp.dma_start(near_y[:, :, :, :].rearrange("p a b c -> p (a b c)"), A["near_y"]).then_inc(consts3, 16)
                for b in range(B):
                    sp.wait_ge(x_final, 4 * b + 4)
                    sp.dma_start(out.rearrange("c p t -> p c t")[:, :, b * N:(b + 1) * N],
                                 xT[:, :, b * N:(b + 1) * N]).then_inc(stored, 16)
                sp.wait_ge(stored, 16 * B)

            @block.gpsimd
            def _(pool):
                pool.wait_ge(consts3, 64)

                def masked_factor(i):
                    if i >= 2:
                        pool.wait_ge(m_done, 4 * (i - 1))
                    o = BD[:, i % 2, :, :].rearrange("p o (a c) -> p o a c", a=4)
                    fac = ttB[:, i * 256:i * 256 + 256].rearrange("p (o a c) -> p o a c", o=QUART, a=1)\
                        .broadcast_to([32, QUART, 4, 32])
                    msk = r2c[:, :].rearrange("p (o a c) -> p o a c", o=1, c=1).broadcast_to([32, QUART, 4, 32])
                    nc.gpsimd.tensor_tensor(o, fac, msk, ALU.mult).then_inc(bd_ready, 1)

                masked_factor(0)
                norm.power(1)
                masked_factor(1)
                for i in range(2, 4):
                    masked_factor(i)
                step = Count(k_step)
                for dx in range(3):
                    to = kxt if dx else kx
                    t = taps[:, :].rearrange("p (a b c) -> p a b c", a=3, c=1)[:, :, dx, :].broadcast_to([P, 3, SIDE])
                    m = near_x[:, dx:dx + 1, :].broadcast_to([P, 3, SIDE])
                    step.up(nc.gpsimd.tensor_tensor(to[:, :, :], t, m, ALU.mult))
                    pool.wait_ge(k_step, step.n)
                    if dx:
                        step.up(nc.gpsimd.tensor_tensor(kx[:, :, :], kx[:, :, :], kxt[:, :, :], ALU.add))
                        pool.wait_ge(k_step, step.n)
                for dy in range(3):
                    to = (kt if dy else K)[:, :, :].rearrange("p t (y x) -> p t y x", y=SIDE)
                    a = near_y[:, dy, :, :].rearrange("p t (y x) -> p t y x", x=1).broadcast_to([P, 2, SIDE, SIDE])
                    b = kx[:, dy, :].rearrange("p (t y x) -> p t y x", t=1, y=1).broadcast_to([P, 2, SIDE, SIDE])
                    step.up(nc.gpsimd.tensor_tensor(to, a, b, ALU.mult))
                    pool.wait_ge(k_step, step.n)
                    if dy:
                        ins = nc.gpsimd.tensor_tensor(K[:, :, :], K[:, :, :], kt[:, :, :], ALU.add)
                        if dy == 2:
                            ins.then_inc(k_ready, 1)
                        else:
                            step.up(ins)
                            pool.wait_ge(k_step, step.n)

            def m_views(i):
                src = PS[:, i % 4, :].rearrange("p (b k a) -> p b k a", b=2, k=CK)
                return src, *(t[:, :, :].rearrange("p k (a b) -> p b k a", b=O23)[:, 2 * i:2 * i + 2, :, :] for t in (Mh, Ml))

            @block.scalar
            def _(act):
                def head_of_m(c):
                    for i in range(2 * c, 2 * c + 2):
                        act.wait_ge(m_done, i + 1)
                        src, hi, _ = m_views(i)
                        nc.scalar.activation(hi, src, ACT.Copy).then_inc(m_hi, 1)

                for c in range(CK):
                    head_of_m(c)
                norm.on_scalar(xh, ytmp)

                def relu(b):
                    for op in range(4):
                        i = 4 * b + op
                        act.wait_ge(f_done, i + 1)
                        if i >= 2:
                            act.wait_ge(x_final, i - 1)
                        for s in range(2):
                            o = 2 * op + s
                            last = nc.scalar.activation(act_out[:, i % 2, s, :], PS[:, 4 + i % 4, s * N:s * N + N],
                                                        ACT.Relu, bias=bias[:, 32 + o:33 + o])
                        last.then_inc(relu_done, 1)

                for b in range(B):
                    for tt in range(2):
                        act.wait_ge(u_done, 4 * b + 2 * tt + 1)
                        nc.scalar.activation(U[:, b % 2, tt, 0:HALF], PS[:, 2 * tt, :], ACT.Copy).then_inc(u_act, 1)
                    if b:
                        relu(b - 1)
                relu(B - 1)

            @block.vector
            def _(dve):
                def rest_of_m(c):
                    for i in range(2 * c, 2 * c + 2):
                        dve.wait_ge(m_hi, i + 1)
                        src, hi, lo = m_views(i)
                        nc.vector.tensor_tensor(lo, src, hi.bitcast(F32), ALU.subtract).then_inc(m_lo, 1)

                norm.chunk_stats(7).then_inc(norm.stats, 1)
                norm.aggregate((6, 7), CK)
                norm.squares(1)
                norm.variances(1)
                for c in range(CK):
                    rest_of_m(c)
                    if c == 0:
                        norm.to_rows(1)
                    if c == 1:
                        norm.coefficients(1)
                norm.on_vector(xh, xl, ytmp, lambda c: None)

                def add(b):
                    for op in range(4):
                        i = 4 * b + op
                        dve.wait_ge(relu_done, i + 1)
                        x = xT[:, 2 * op:2 * op + 2, b * N:(b + 1) * N]
                        nc.vector.tensor_tensor(x, act_out[:, i % 2, :, :], x, ALU.add).then_inc(x_final, 1)

                for b in range(B):
                    for tt in range(2):
                        dve.wait_ge(u_done, 4 * b + 2 * tt + 2)
                        nc.vector.tensor_copy(U[:, b % 2, tt, HALF:C], PS[:, 2 * tt + 1, :]).then_inc(u_dve, 1)
                    if b:
                        add(b - 1)
                add(B - 1)

            @block.tensor
            def _(pe):
                for i in range(16):
                    if i == 1:
                        norm.averages(1)
                    if i == 3:
                        norm.turn(1)
                    if i % 4 == 0:
                        pe.wait_ge(bd_ready, i // 4 + 1)
                    if i >= 4:
                        pe.wait_ge(m_lo, i - 3)
                    for s in range(2):
                        m = nc.tensor.matmul(PS[:, i % 4, s * 256:s * 256 + 256], BD[:, (i // 4) % 2, (2 * i + s) % QUART, :],
                                             ttA[:, :], start=True, stop=True)
                    m.then_inc(m_done, 1)
                pe.wait_ge(m_lo, 16)

                def channel_product(b):
                    if b == 0:
                        order = [(c, tt, oh) for c in range(CK) for tt in range(2) for oh in range(2)]
                    else:
                        order = [(c, tt, oh) for tt in range(2) for oh in range(2) for c in range(CK)]
                    for c, tt, oh in order:
                        bank = 2 * tt + oh
                        if b and c == 0:
                            pe.wait_ge(u_dve if oh else u_act, 2 * b - 1 + tt)
                        cols = slice((2 * b + tt) * P, (2 * b + tt) * P + P)
                        for k, (x, w) in enumerate(((xh, Mh), (xh, Ml), (xl, Mh))):
                            if b == tt == oh == 0 and k != 1:
                                norm.ready(c, k == 2)
                            m = nc.tensor.matmul(PS[:, bank, :], x[:, c, cols], w[:, c, oh * HALF:oh * HALF + HALF],
                                                 start=c == 0 and k == 0, stop=c == CK - 1 and k == 2)
                        if c == CK - 1:
                            m.then_inc(u_done, 1)

                def convolution(b):
                    for op in range(4):
                        i = 4 * b + op
                        if op == 0:
                            if b == 0:
                                pe.wait_ge(k_ready, 1)
                            pe.wait_ge(u_act, 2 * b + 2)
                            pe.wait_ge(u_dve, 2 * b + 2)
                        if i >= 4:
                            pe.wait_ge(relu_done, i - 3)
                        for s in range(2):
                            o = 2 * op + s
                            for tt in range(2):
                                m = nc.tensor.matmul(PS[:, 4 + i % 4, s * N:s * N + N], U[:, b % 2, tt, o * P:o * P + P],
                                                     K[:, tt, :], start=tt == 0, stop=tt == 1)
                        m.then_inc(f_done, 1)

                for b in range(B):
                    channel_product(b)
                    if b:
                        convolution(b - 1)
                convolution(B - 1)


def lay_out(v):
    def f(name):
        return np.asarray(v[name])

    def chunks(a):
        return a.T.reshape(CK, P, -1)

    def cols(a):
        return a.reshape(-1, P).T

    def block(w, d):
        return w[:, d:d + P].reshape(2, 4, P, P).transpose(0, 2, 1, 3).reshape(2, P, HALF)

    def rows(w):
        return w.reshape(-1, C).T

    def in_turns(a, b):
        return np.stack([a[0], b[0], a[1], b[1]])

    s0 = [in_turns(*(block(f("L0_conv_Wv"), P * i) for i in range(2)))] + [block(f("L0_conv_Wk"), P * i) for i in range(2)]
    s0 += [block(f("L0_conv_Wq"), P * i) for i in range(8)]

    def heads(q, k, w, out_blocks):
        s = [in_turns(block(w, 0), block(q, 0))]
        for j in range(PAIRS):
            s += [block(q, P * j)] if j not in (0, PAIRS // 2) else []
            s.append(block(k, P * j))
            if j + 1 < PAIRS:
                s.append(block(w, P * (j + 1)))
            if j == PAIRS // 2 - 1:
                s.append(block(q, P * (j + 1)))
            if j in (PAIRS // 2 - 1, PAIRS - 1):
                s += out_blocks(j // (PAIRS // 2))
        return s

    q1, k1, v1 = (np.concatenate([rows(f(f"L1_conv_W{x}_lb")), rows(f(f"L1_conv_W{x}_la"))], axis=1) for x in "qkv")
    wo = f("L1_conv_Wo").T
    s1 = heads(q1, k1, v1, lambda half: [block(wo, P * o) for o in range(CK)])
    q2, k2, v2 = np.split(f("L2_conv_qkv_w"), 3, axis=1)
    wp = f("L2_conv_proj_w")
    s2 = heads(q2, k2, v2, lambda half: [block(wp, P * o)[half:half + 1] for o in range(CK)])

    emb = f("L0_conv_rel_pos_emb")[..., 0].reshape(961, 64, 2, 2)
    rel = np.zeros((2, P, 64), np.float32)
    for i, name in enumerate(("L2_conv_rel_pos_h", "L2_conv_rel_pos_w")):
        table = f(name)[30::-1].T
        rel[i, 0:64, 0:31] = table
        rel[i, 64:128, 32:63] = table
    t = np.arange(N)
    hot = np.zeros((48, T), np.float32)
    hot[0:16] = np.tile(np.arange(16)[:, None] == t // SIDE, (1, B))
    hot[32:48] = np.tile(np.arange(16)[:, None] == t % SIDE, (1, B))
    i, j = np.arange(P)[:, None], np.arange(P)[None, :]
    mask = np.zeros((2, P, P), np.float32)
    mask[0][j > i] = -1e30
    mask[1][j < i] = -1e30
    c1 = f("L3_conv_core1").reshape(8, 8, 8, 2, 4)
    c2 = f("L3_conv_core2").reshape(8, 8, 8, 8)
    x = np.arange(P) % SIDE
    y = np.arange(P)[:, None] // SIDE + np.array([0, P // SIDE])
    d3 = np.arange(3)
    near_x = (x[:, None, None] - np.arange(16)[None, None] == d3[None, :, None] - 1).astype(np.float32)
    near_y = (y[:, None, :, None] - np.arange(16) == d3[None, :, None, None] - 1).astype(np.float32)
    bn = [np.concatenate([cols(f(f"L0_conv_q_{x}")), cols(f(f"L0_conv_v_{x}"))], axis=1)
          for x in ("gamma", "beta", "mean", "var")]
    return {
        "x": chunks(f("x").reshape(T, C)),
        "w": np.concatenate(s0 + s1 + s2),
        "ident": np.eye(P, dtype=np.float32),
        "gmat": np.kron(np.eye(P // GROUP), np.full((GROUP, GROUP), 1.0 / GROUP)).astype(np.float32),
        "mask": mask,
        "bn": np.concatenate(bn, axis=1),
        "bias": np.concatenate([cols(f("L2_conv_qkv_b")), cols(f("L2_conv_proj_b")), cols(f("L3_conv_bias"))], axis=1),
        "emb": emb.transpose(3, 1, 2, 0).reshape(P, 2, 961),
        "rel": rel,
        "hot": hot,
        "c0": f("L3_conv_core0").reshape(4, 8, 4).transpose(1, 2, 0).reshape(P),
        "c1": c1.transpose(1, 4, 2, 3, 0).reshape(32, P),
        "c2": c2.transpose(2, 1, 0, 3).reshape(8, HALF),
        "c3": f("L3_conv_core3").reshape(4, 8, 4).transpose(1, 0, 2).reshape(P),
        "taps": f("L3_conv_filters").reshape(9),
        "near_x": near_x.reshape(P, 48),
        "near_y": near_y.reshape(P, 96),
        "r2c": (np.arange(32)[:, None] % 4 == np.arange(4)[None]).astype(np.float32),
    }


def kernel(**inputs):
    import concourse.bacc as _bacc
    from concourse.bass_utils import run_bass_kernel_spmd as _run

    nc = _bacc.Bacc("TRN2", target_bir_lowering=False, num_devices=1)
    arrays, args = {}, {}
    for name, a in lay_out(inputs).items():
        a = np.ascontiguousarray(a)
        arrays[f"in_{name}"] = a
        args[name] = nc.dram_tensor(f"in_{name}", a.shape, mybir.dt.from_np(a.dtype), kind="ExternalInput").ap()
    out = nc.dram_tensor("out_x", (CK, P, T), F32, kind="ExternalOutput").ap()
    build(nc, args, out)
    r = _run(nc, [arrays], core_ids=[0])
    return np.ascontiguousarray(r.results[0]["out_x"].reshape(C, T).T).reshape(B, SIDE, SIDE, C)
```

```python
from contextlib import ExitStack

import numpy as np
import concourse.bass as bass
from concourse import mybir

F32 = mybir.dt.float32
F32R = mybir.dt.float32r
BF16 = mybir.dt.bfloat16
ALU = mybir.AluOpType
ACT = mybir.ActivationFunctionType
AX = mybir.AxisListType.X

P = 128
B = 4
SIDE = 16
N = SIDE * SIDE
T = B * N
C = 1024
CK = C // P
HALF = 512
PAIRS = 8
UNITS = 8
HEADS0 = 4
GROUP = 32
GN_EPS = 1e-5
BN_EPS = 1e-3
OUT_MODES = (4, 8, 8, 4)
RANK = 8
TT = 3 * 32
DY = 23
KROWS = 112

HB0 = 2 * 12
HB1 = 2 + 4 * 6 + 16 + 3 * 6 + 4 + 16
HB2 = 2 + 4 * 6 + 8 + 3 * 6 + 4 + 8
HB_TOTAL = HB0 + HB1 + HB2


class Count:

    def __init__(self, sem):
        self.sem, self.n = sem, 0

    def up(self, ins, k=1):
        self.n += k
        ins.then_inc(self.sem, k)
        return self.n


def build(nc, A, out):
    outer = ExitStack()
    with outer:
        names = [0]

        def sem(name):
            names[0] += 1
            return outer.enter_context(nc.semaphore(f"{name}_{names[0]}"))

        def sb(ctx, name, shape, dt=F32):
            names[0] += 1
            return ctx.enter_context(nc.sbuf_tensor(f"{name}_{names[0]}", shape, dt))

        PS = outer.enter_context(nc.psum_tensor("PS", [P, 8, HALF], F32))
        xT = sb(outer, "xT", [P, CK, T])
        ident = sb(outer, "ident", [P, P])
        gmat = sb(outer, "gmat", [P, P])
        identb = sb(outer, "identb", [P, P], BF16)
        maskb = sb(outer, "maskb", [P, 2, P], BF16)
        bn = sb(outer, "bn", [P, 40])
        bias = sb(outer, "bias", [P, 40])
        bst = sb(outer, "bst", [P, CK * B, 6])
        mv = sb(outer, "mv", [P, CK * B, 2])
        sq = sb(outer, "sq", [P, CK * B])
        gn = sb(outer, "gn", [CK * B, 4, P // GROUP])
        gn_row = sb(outer, "gn_row", [CK * B, 2, P])
        coef = sb(outer, "coef", [P, 2, CK * B])
        neghalf = sb(outer, "neghalf", [P, 32])
        ttA = sb(outer, "ttA", [TT, 256], F32R)
        ttB = sb(outer, "ttB", [TT, 1024], F32R)
        r2c = sb(outer, "r2c", [TT, 4])
        weights = outer.enter_context(ExitStack())
        w_raw = sb(weights, "w_raw", [P, 2, HALF])
        w_hi = sb(weights, "w_hi", [P, 2, HALF], F32R)
        w_lo = sb(weights, "w_lo", [P, 2, HALF], F32R)
        zeros = sb(weights, "zeros", [P, HALF])

        w_landed = [sem("w_landed0"), sem("w_landed1")]
        w_hi_done = sem("w_hi_done")
        w_ready = sem("w_ready")
        w_used = sem("w_used")
        consts_in = sem("consts_in")
        x_in = [sem(f"x_in{c}") for c in range(CK)]

        def w_load(sp, n, s, waits):
            if waits:
                sp.wait_ge(w_ready, n - 1)
            src = A["w"][n] if isinstance(n, int) else A["w"][bass.ds(n, 1)].rearrange("a p n -> p (a n)")
            sp.dma_start(w_raw[:, s, :], src).then_inc(w_landed[s], 16)

        def w_loads(sp, n0, n1):
            with sp.Fori(n0 // 2, n1 // 2) as i:
                for s in range(2):
                    w_load(sp, 2 * i + s, s, True)

        def w_split(pool, i, s, waits):
            n = 2 * i + s
            pool.wait_ge(w_landed[s], 16 * i + 16)
            if waits:
                pool.wait_ge(w_used, n - 1)
            pool.tensor_tensor(w_hi[:, s, :], w_raw[:, s, :], zeros[:, :], ALU.add).then_inc(w_hi_done, 1)
            pool.wait_ge(w_hi_done, n + 1)
            pool.tensor_tensor(w_lo[:, s, :], w_raw[:, s, :], w_hi[:, s, :].bitcast(F32),
                               ALU.subtract).then_inc(w_ready, 1)

        def w_splits(pool, n0, n1):
            with pool.Fori(n0 // 2, n1 // 2) as i:
                for s in range(2):
                    w_split(pool, i, s, True)

        def chunk_product(n, slot, cc, c, rhs_hi, rhs_lo, banks, first, last, ready=None, used=True,
                          first_bank=None):
            if cc == 0:
                nc.tensor.wait_ge(w_ready, n + 1)
            w = slice(cc * P, cc * P + P)
            passes = [(k, h) for k in range(3) for h in range(len(banks))]
            if first_bank is not None:
                passes.sort(key=lambda p: p[1])
            for k, h in passes:
                wt, x = ((w_hi, rhs_hi), (w_lo, rhs_hi), (w_hi, rhs_lo))[k]
                if ready and h == 0 and k != 1:
                    ready(c, k == 2)
                m = nc.tensor.matmul(PS[:, banks[h], :], wt[:, slot, w], x[:, c, h * HALF:h * HALF + HALF],
                                     start=first and k == 0, stop=last and k == 2)
                if first_bank is not None and (k, h) == (2, 0):
                    m.then_inc(first_bank, 1)
            if cc == 3 and used:
                m.then_inc(w_used, 1)
            return m

        def block_product(n, rhs_hi, rhs_lo, banks, chunks=range(CK), used=True, first_bank=None):
            for c in chunks:
                m = chunk_product(n + c // 4, c // 4, c % 4, c, rhs_hi, rhs_lo, banks, c == 0, c == CK - 1, used=used,
                                  first_bank=first_bank if c == CK - 1 else None)
            return m

        def block_pair(n, rhs_hi, rhs_lo, banks_a, banks_b, ready, before, early=True):
            order = [(c, slot) for c in range(CK) for slot in range(2)]
            if early:
                for i in (5, 9):
                    order[i], order[i + 1] = order[i + 1], order[i]
            for c, slot in order:
                before(c, slot)
                chunk_product(n + slot + 2 * (c // 4), slot, c % 4, c, rhs_hi, rhs_lo, (banks_a, banks_b)[slot],
                              c == 0, c == CK - 1, ready=None if slot else ready)

        class Norm:

            def __init__(self, batches):
                self.batches = batches
                self.stats = sem("gn_stats")
                self.aggr = sem("gn_aggr")
                self.step = sem("gn_step")
                self.grouped = sem("gn_grouped")
                self.rstd = sem("gn_rstd")
                self.rows = sem("gn_rows")
                self.turned = sem("gn_turned")
                self.coef = sem("gn_coef")
                self.y_dve = sem("gn_y_dve")
                self.y_act = sem("gn_y_act")
                self.hi = sem("xh_ready")
                self.lo = sem("xl_ready")
                self.steps = Count(self.step)

            def chunk_stats(self, c, images=range(B)):
                for b in images:
                    src = xT[:, bass.ds(c, 1), b * N:(b + 1) * N].rearrange("p a n -> p (a n)")
                    dst = bst[:, bass.ds(c * B + b, 1), :].rearrange("p a n -> p (a n)")
                    last = nc.vector.bn_stats(dst, src)
                return last

            def aggregate(self, chunks, stats):
                nc.vector.wait_ge(self.stats, stats)
                for c in chunks:
                    for k in range(c * B, c * B + B):
                        last = nc.vector.bn_aggr(mv[:, k, :], bst[:, k, :])
                last.then_inc(self.aggr, len(chunks))

            def size(self, i):
                c0, c1 = self.batches[i]
                return (c1 - c0) * B, slice(c0 * B, c1 * B)

            def squares(self, i):
                n, ks = self.size(i)
                nc.vector.wait_ge(self.aggr, self.batches[i][1])
                self.steps.up(nc.vector.tensor_tensor(sq[:, ks], mv[:, ks, 0], mv[:, ks, 0], ALU.mult))

            def variances(self, i):
                v, steps = nc.vector, self.steps
                n, ks = self.size(i)
                v.wait_ge(self.grouped, i + 1)
                steps.up(v.tensor_copy(gn[0:n, 0, :], PS[0:n, 6, 0:4]))
                v.wait_ge(self.step, steps.n)
                steps.up(v.tensor_tensor(gn[0:n, 1, :], gn[0:n, 0, :], gn[0:n, 0, :], ALU.mult))
                v.wait_ge(self.step, steps.n)
                steps.up(v.tensor_tensor(gn[0:n, 2, :], PS[0:n, 6, 4:8], gn[0:n, 1, :], ALU.subtract))
                v.wait_ge(self.step, steps.n)
                steps.up(v.tensor_scalar(gn[0:n, 2, :], gn[0:n, 2, :], 0.0, GN_EPS, ALU.max, ALU.add))

            def to_rows(self, i):
                n, ks = self.size(i)
                nc.vector.wait_ge(self.rstd, i + 1)
                mean, rstd = (gn[0:n, k, :].rearrange("p (g q) -> p g q", q=1).broadcast_to([n, 4, GROUP]) for k in (0, 3))
                nc.vector.tensor_copy(gn_row[0:n, 0, :].rearrange("p (g q) -> p g q", g=4), rstd)
                nc.vector.scalar_tensor_tensor(gn_row[0:n, 1, :].rearrange("p (g q) -> p g q", g=4), mean, -1.0, rstd,
                                               ALU.mult, ALU.mult).then_inc(self.rows, 1)

            def coefficients(self, i):
                n, ks = self.size(i)
                nc.vector.wait_ge(self.turned, i + 1)
                nc.vector.tensor_copy(coef[:, :, ks], PS[:, 6, 8:8 + 2 * n].rearrange("p (a k) -> p a k", a=2))\
                    .then_inc(self.coef, 1)

            def y(self, eng, c, images, ytmp, done):
                i = next(i for i, (c0, c1) in enumerate(self.batches) if c0 <= c < c1)
                eng.wait_ge(self.coef, i + 1)
                if c >= 2:
                    eng.wait_ge(self.hi, c - 1)
                    eng.wait_ge(self.lo, c - 1)
                for b in images:
                    k = c * B + b
                    dst, src = ytmp[:, c % 2, b * N:(b + 1) * N], xT[:, c, b * N:(b + 1) * N]
                    scale, shift = coef[:, 0, k:k + 1], coef[:, 1, k:k + 1]
                    if eng is nc.scalar:
                        last = nc.scalar.activation(dst, src, ACT.Identity, bias=shift, scale=scale)
                    else:
                        last = nc.vector.tensor_scalar(dst, src, scale, shift, ALU.mult, ALU.add)
                last.then_inc(done, 1)

            def on_vector(self, xh, xl, ytmp, after, flush=(), begin=0, wait_for_first=None):
                for c in range(begin, CK):
                    self.y(nc.vector, c, (0, 1), ytmp, self.y_dve)
                    if c == 0 and wait_for_first:
                        wait_for_first()
                    if c > begin and c - 1 not in flush:
                        self.rest(c - 1, xh, xl, ytmp)
                    if c in flush or c == CK - 1:
                        self.rest(c, xh, xl, ytmp)
                    after(c)

            def rest(self, c, xh, xl, ytmp):
                nc.vector.wait_ge(self.y_dve, c + 1)
                nc.vector.wait_ge(self.hi, c + 1)
                nc.vector.tensor_tensor(xl[:, c, :], ytmp[:, c % 2, :], xh[:, c, :].bitcast(F32),
                                        ALU.subtract).then_inc(self.lo, 1)

            def head(self, c, xh, ytmp):
                nc.scalar.wait_ge(self.y_dve, c + 1)
                nc.scalar.wait_ge(self.y_act, c + 1)
                nc.scalar.activation(xh[:, c, :], ytmp[:, c % 2, :], ACT.Copy).then_inc(self.hi, 1)

            def on_scalar(self, xh, ytmp, begin=0):
                for c0, c1 in self.batches:
                    for c in range(max(c0, begin), c1):
                        self.y(nc.scalar, c, (2, 3), ytmp, self.y_act)
                        if c > max(c0, begin, 1):
                            self.head(c - 1, xh, ytmp)
                        if c == 0 or c == c1 - 1:
                            self.head(c, xh, ytmp)

            def averages(self, i):
                n, ks = self.size(i)
                groups = gmat[:, 0:P:GROUP]
                nc.tensor.wait_ge(self.step, 5 * i + 1)
                nc.tensor.matmul(PS[0:n, 6, 0:4], mv[:, ks, 0], groups, start=True, stop=True)
                nc.tensor.matmul(PS[0:n, 6, 4:8], mv[:, ks, 1], groups, start=True, stop=False)
                nc.tensor.matmul(PS[0:n, 6, 4:8], sq[:, ks], groups, start=False, stop=True).then_inc(self.grouped, 1)

            def turn(self, i):
                n, ks = self.size(i)
                nc.tensor.wait_ge(self.rows, i + 1)
                for a in range(2):
                    m = nc.tensor.transpose(PS[:, 6, 8 + a * n:8 + a * n + n], gn_row[0:n, a, :], ident[0:n, 0:n])
                m.then_inc(self.turned, 1)

            def power(self, i):
                n, ks = self.size(i)
                nc.gpsimd.wait_ge(self.step, 5 * i + 5)
                nc.gpsimd.tensor_tensor(gn[0:n, 3, :], gn[0:n, 2, :], neghalf[0:n, 0:4], ALU.pow).then_inc(self.rstd, 1)

            def ready(self, c, lo):
                if lo:
                    nc.tensor.wait_ge(self.lo, c + 1)
                else:
                    nc.tensor.wait_ge(self.hi, c + 1)

        norms = [Norm(((0, 4), (4, 8))), Norm(((0, 4), (4, 8))), Norm(((0, 6), (6, 8))), Norm(((0, 6), (6, 8)))]

        layer0(nc, A, outer, locals())
        layer12(nc, A, outer, locals(), 1)
        layer12(nc, A, outer, locals(), 2)
        weights.close()
        layer3(nc, A, out, outer, locals())


def layer0(nc, A, outer, g):
    PS, xT, zeros, ident, gmat, identb, maskb = (g[x] for x in ("PS", "xT", "zeros", "ident", "gmat", "identb", "maskb"))
    bn, bias, neghalf, ttA, ttB, r2c = (g[x] for x in ("bn", "bias", "neghalf", "ttA", "ttB", "r2c"))
    sem, sb, norms, consts_in, x_in = (g[x] for x in ("sem", "sb", "norms", "consts_in", "x_in"))
    block_product, block_pair, w_used = g["block_product"], g["block_pair"], g["w_used"]
    norm = norms[0]
    with ExitStack() as keep:
        Qs = sb(keep, "Qs", [P, 2, B * HEADS0 * N])
        VT = sb(keep, "VT", [P, 2, T])
        ks = sb(keep, "ks", [P, B, 2, N])

        ET = sb(keep, "ET", [P, 2, 961])
        et_in = sem("et_in")

        with ExitStack() as ctx:
            xh = sb(ctx, "xh", [P, CK, T], F32R)
            xl = sb(ctx, "xl", [P, CK, T], F32R)
            ytmp = sb(ctx, "ytmp", [P, 2, T])
            qT = sb(ctx, "qT", [P, 2, T])
            KT = sb(ctx, "KT", [P, 2, T])
            bns = sb(ctx, "bns", [P, 4, 10])
            kmax = sb(ctx, "kmax", [P, B, 2])
            ksum = sb(ctx, "ksum", [P, B, 2])
            krec = sb(ctx, "krec", [P, B, 2])
            maskf = sb(ctx, "maskf", [P, 2, P])
            memset_done = sem("memset_done")
            gn_consts = sem("gn_consts")
            bn_step = sem("bn_step")
            bn_pow = sem("bn_pow")
            vk_evac = sem("vk_evac")
            q_evac = sem("q_evac")
            q_tr = sem("q_tr")
            q_placed = sem("q_placed")
            k_tr = sem("k_tr")
            k_max = sem("k_max")
            k_exp = sem("k_exp")
            k_rec = sem("k_rec")
            k_soft = sem("k_soft")

            with nc.Block() as block:
                @block.sync
                def _(sp):
                    for c in (0, 2):
                        sp.dma_start(xT[:, c, :], A["x"][c]).then_inc(x_in[c], 16)
                    for s in range(2):
                        g["w_load"](sp, s, s, False)
                    for c in (4, 6):
                        sp.dma_start(xT[:, c, :], A["x"][c]).then_inc(x_in[c], 16)
                    g["w_loads"](sp, 2, HB0 + 2)

                @block.gpsimd
                def _(pool):
                    nc.gpsimd.memset(zeros[:, :], 0.0).then_inc(memset_done, 1)
                    nc.gpsimd.memset(neghalf[:, :], -0.5).then_inc(memset_done, 1)
                    pool.wait_ge(memset_done, 2)
                    for s in range(2):
                        g["w_split"](pool, 0, s, False)
                    norm.power(0)
                    pool.wait_ge(bn_step, 1)
                    nc.gpsimd.tensor_tensor(bns[:, 1, :], bns[:, 0, :], neghalf[:, 0:10], ALU.pow).then_inc(bn_pow, 1)
                    norm.power(1)
                    g["w_splits"](pool, 2, HB0)

                @block.vector
                def _(dve):
                    def stats(c):
                        dve.wait_ge(x_in[c], 16)
                        norm.chunk_stats(c).then_inc(norm.stats, 1)

                    def after(c):
                        if c == 0:
                            dve.wait_ge(consts_in, 16 * 3)
                            dve.wait_ge(gn_consts, 16 * 2)
                            nc.vector.tensor_copy(identb[:, :], ident[:, :]).then_inc(q_placed, 1)
                            nc.vector.tensor_copy(maskb[:, :, :], maskf[:, :, :])
                            nc.vector.tensor_scalar(bns[:, 0, :], bn[:, 30:40], BN_EPS, None, ALU.add).then_inc(bn_step, 1)
                        if c < 4:
                            stats(c + 4)
                        if c == 3:
                            norm.aggregate(range(4, CK), CK)
                            norm.squares(1)
                            norm.variances(1)
                            norm.to_rows(1)
                            norm.coefficients(1)
                        if c == 4:
                            dve.wait_ge(bn_pow, 1)
                            nc.vector.tensor_tensor(bns[:, 2, :], bns[:, 1, :], bn[:, 0:10], ALU.mult).then_inc(bn_step, 1)
                        if c == 5:
                            dve.wait_ge(bn_step, 2)
                            nc.vector.tensor_tensor(bns[:, 3, :], bn[:, 20:30], bns[:, 2, :], ALU.mult).then_inc(bn_step, 1)
                        if c == 6:
                            dve.wait_ge(bn_step, 3)
                            nc.vector.tensor_tensor(bns[:, 3, :], bn[:, 10:20], bns[:, 3, :], ALU.subtract).then_inc(bn_step, 1)

                    for c in range(4):
                        stats(c)
                    norm.aggregate(range(4), 4)
                    norm.squares(0)
                    norm.variances(0)
                    norm.to_rows(0)
                    norm.coefficients(0)
                    norm.on_vector(xh, xl, ytmp, after, flush=(3,))

                    def soft_k(b):
                        dve.wait_ge(k_tr, b + 1)
                        nc.vector.tensor_reduce(kmax[:, b, :], PS[:, 6 + b % 2, :].rearrange("p (j m) -> p j m", j=2),
                                                AX, ALU.max, negate=True).then_inc(k_max, 1)
                        dve.wait_ge(k_exp, b + 1)
                        nc.vector.reciprocal(krec[:, b, :], ksum[:, b, :]).then_inc(k_rec, 1)
                        dve.wait_ge(k_rec, b + 1)
                        for jp in range(2):
                            last = nc.vector.tensor_scalar(ks[:, b, jp, :], ks[:, b, jp, :], krec[:, b, jp:jp + 1],
                                                           None, ALU.mult)
                        last.then_inc(k_soft, 1)

                    def place_q(jp):
                        for k in range(4):
                            j2, ph = k // 2, k % 2
                            dve.wait_ge(q_tr, 4 * jp + k + 1)
                            for bank in range(2):
                                for h2 in range(2):
                                    src = PS[64 * h2:64 * h2 + 64, 4 + bank, :].rearrange("p (c y x) -> p c y x", c=4, x=SIDE)
                                    dst = Qs[64 * j2:64 * j2 + 64, bass.ds(jp, 1), :]\
                                        .rearrange("p a (x y g h) -> p (a g) y x h", x=SIDE, y=SIDE, h=2)[
                                            :, 4 * bank:4 * bank + 4, 8 * ph:8 * ph + 8, :, h2]
                                    last = nc.vector.tensor_copy(dst, src)
                            last.then_inc(q_placed, 1)

                    for jp in range(2):
                        for b in (2 * jp, 2 * jp + 1):
                            soft_k(b)
                        place_q(jp)

                @block.scalar
                def _(act):
                    for c in (1, 3):
                        act.dma_start(xT[:, c, :], A["x"][c]).then_inc(x_in[c], 16)
                    act.dma_start(ident[:, :], A["ident"]).then_inc(gn_consts, 16)
                    act.dma_start(gmat[:, :], A["gmat"]).then_inc(gn_consts, 16)
                    for c in (5, 7):
                        act.dma_start(xT[:, c, :], A["x"][c]).then_inc(x_in[c], 16)
                    act.dma_start(maskf[:, :, :], A["mask"].rearrange("a p n -> p a n")).then_inc(consts_in, 16)
                    act.dma_start(bn[:, :], A["bn"]).then_inc(consts_in, 16)
                    act.dma_start(bias[:, :], A["bias"]).then_inc(consts_in, 16)
                    act.dma_start(ET[:, :, :], A["emb"]).then_inc(et_in, 16)
                    norm.on_scalar(xh, ytmp)
                    act.wait_ge(bn_step, 4)
                    for i, (dst, at) in enumerate(((VT[:, 0, :], 0), (VT[:, 1, :], 2), (KT[:, 0, :], 0), (KT[:, 1, :], 2))):
                        act.wait_ge(w_used, (3, 4, 6, 8)[i])
                        src = PS[:, at:at + 2, :].rearrange("p a n -> p (a n)")
                        if i < 2:
                            ins = nc.scalar.activation(dst, src, ACT.Identity, bias=bns[:, 3, 8 + i:9 + i],
                                                       scale=bns[:, 2, 8 + i:9 + i])
                        else:
                            dst = dst.rearrange("p (b j t) -> p b t j", b=B, j=4)
                            src = src.rearrange("p (b t j) -> p b t j", b=B, j=4)
                            ins = nc.scalar.activation(dst, src, ACT.Copy)
                        ins.then_inc(vk_evac, 1)

                    def exp_k(b):
                        act.wait_ge(k_max, b + 1)
                        for jp in range(2):
                            last = nc.scalar.activation(ks[:, b, jp, :], PS[:, 6 + b % 2, jp * N:jp * N + N], ACT.Exp,
                                                        bias=kmax[:, b, jp:jp + 1], accum_out=ksum[:, b, jp:jp + 1])
                        last.then_inc(k_exp, 1)

                    def evac_q(jp):
                        for k in range(4):
                            n = 4 * jp + k
                            at = 2 * (k % 2)
                            act.wait_ge(w_used, 2 * n + 10)
                            nc.scalar.activation(qT[:, k % 2, :], PS[:, at:at + 2, :].rearrange("p a n -> p (a n)"),
                                                 ACT.Identity, bias=bns[:, 3, bass.ds(n, 1)],
                                                 scale=bns[:, 2, bass.ds(n, 1)]).then_inc(q_evac, 1)

                    for jp in range(2):
                        for b in (2 * jp, 2 * jp + 1):
                            exp_k(b)
                        evac_q(jp)

                @block.tensor
                def _(pe):
                    def before(c, slot):
                        if (c, slot) == (4, 0):
                            norm.averages(1)
                            norm.turn(1)

                    pe.wait_ge(gn_consts, 16 * 2)
                    norm.averages(0)
                    norm.turn(0)
                    block_pair(0, xh, xl, (0, 1), (2, 3), norm.ready, before, early=False)
                    for i in range(2, 4):
                        pe.wait_ge(vk_evac, i - 1)
                        block_product(2 * i, xh, xl, (2 * (i % 2), 2 * (i % 2) + 1))

                    def transpose_k(b):
                        for jp in range(2):
                            for mc in range(2):
                                src = KT[:, mc, b * N + jp * P:b * N + jp * P + P]
                                m = nc.tensor.transpose(PS[:, 6 + b % 2, jp * N + mc * P:jp * N + mc * P + P], src, ident[:, :])
                        m.then_inc(k_tr, 1)

                    def transpose_q(n, k):
                        pe.wait_ge(q_evac, n + 1)
                        pe.wait_ge(q_placed, n + 1)
                        for tt in range(8):
                            m = nc.tensor.transpose(PS[:, 4 + tt // 4, (tt % 4) * P:(tt % 4) * P + P],
                                                    qT[:, k % 2, tt * P:tt * P + P], ident[:, :])
                        m.then_inc(q_tr, 1)

                    pe.wait_ge(vk_evac, 4)
                    for jp in range(2):
                        if jp:
                            pe.wait_ge(k_exp, 2)
                        for b in (2 * jp, 2 * jp + 1):
                            transpose_k(b)
                        for k in range(4):
                            n = 4 * jp + k
                            if n >= 2:
                                pe.wait_ge(q_evac, n - 1)
                            block_product(8 + 2 * n, xh, xl, (2 * (k % 2), 2 * (k % 2) + 1))
                            if n >= 1:
                                transpose_q(n - 1, (k - 1) % 4)
                    transpose_q(7, 3)

        with ExitStack() as ctx:
            AT = sb(ctx, "AT", [P, 2, B * HEADS0 * N])
            G = sb(ctx, "G", [P, 2, 8, DY * SIDE])
            A2 = sb(ctx, "A2", [P, 4, 8, N])
            c0 = sb(ctx, "c0", [TT, 8, 4, 4])
            c1 = sb(ctx, "c1", [TT, 8, 2, 8])
            c2 = sb(ctx, "c2", [TT, 8, 8, 8])
            c3 = sb(ctx, "c3", [TT, 8, 4, 4])
            term = sb(ctx, "term", [TT, HALF])
            total = sb(ctx, "total", [TT, HALF])
            cores_in = sem("cores_in")
            mul_done = sem("mul_done")
            add_done = sem("add_done")
            shifted = [sem(f"shifted{u}") for u in range(4)]
            pe_group = sem("pe_group")
            act_evac = sem("act_evac")
            dve_evac = sem("dve_evac")
            x_sum = sem("x_sum")

            groups = []
            for u in range(4):
                for xi in range(8):
                    groups.append(("G", (u, xi), "act" if xi % 2 else "dve"))
            for b in range(B):
                for mc in range(2):
                    for nh in range(2):
                        groups.append(("K", (b, mc, nh), "act" if nh else "dve"))
            for u in range(4):
                for xg in range(2):
                    for mc in range(2):
                        groups.append(("A", (u, xg, mc), "dve"))
            for nh in range(2):
                for vt in range(2):
                    for b in range(B):
                        groups.append(("Y", (b, vt, nh), "dve"))
            seen = {"act": 0, "dve": 0}
            evac_at = []
            for _, _, e in groups:
                seen[e] += 1
                evac_at.append((e, seen[e]))
            bank_of = [i % 8 if kind != "Y" else (0, 1, 2, 3, 4, 5, 7)[i % 7] for i, (kind, _, _) in enumerate(groups)]
            before_it = [max((k for k in range(i) if bank_of[k] == bank_of[i]), default=None) for i in range(len(groups))]
            evac_sem = {"act": act_evac, "dve": dve_evac}

            def evacuated(eng, i):
                e, k = evac_at[i]
                eng.wait_ge(evac_sem[e], k)

            def a_view(mc, u, xg):
                yg, x0 = u // 2, 8 * (u % 2) + 4 * xg
                v = AT[:, mc, :].rearrange("p (g y x) -> p x y g", y=SIDE, x=SIDE)
                return v[:, x0:x0 + 4, 8 * yg:8 * yg + 8, :]

            def next_stats(eng, i):
                b, vt, nh = groups[i][1]
                evacuated(eng, i)
                chunks = (4 * nh + vt, 4 * nh + 2 + vt)
                for c in chunks:
                    norms[1].chunk_stats(c, (b,)).then_inc(norms[1].stats, 1)
                if b == B - 1:
                    norms[1].aggregate(chunks, 8 * (2 * nh + vt + 1))
                k = i - (len(groups) - 16)
                if k == 7:
                    norms[1].squares(0)
                if k == 9:
                    norms[1].variances(0)
                if k == 10:
                    norms[1].to_rows(0)
                if k == 12:
                    norms[1].coefficients(0)

            def read_out(eng, name):
                for i, (kind, d, e) in enumerate(groups):
                    if e != name:
                        continue
                    bank = PS[:, bank_of[i], :]
                    eng.wait_ge(pe_group, i + 1)
                    if kind == "G":
                        u, xi = d
                        if u >= 2:
                            eng.wait_ge(shifted[u - 2], 128)
                        dst, src = G[:, u % 2, xi, :], bank[:, 0:DY * SIDE]
                    elif kind == "K":
                        b, mc, nh = d
                        dst = AT[:, mc, b * C:b * C + C].rearrange("p (h y x) -> p x y h", y=SIDE, x=SIDE)[
                            :, 8 * nh:8 * nh + 8, :, :]
                        src = bank.rearrange("p (x y h) -> p x y h", x=8, y=SIDE)
                    if kind in "GK":
                        ins = nc.scalar.activation(dst, src, ACT.Copy) if name == "act" else nc.vector.tensor_copy(dst, src)
                    elif kind == "A":
                        u, xg, mc = d
                        if (u, xg, mc) == (0, 0, 0):
                            eng.wait_ge(act_evac, 24)
                            eng.wait_ge(dve_evac, 24)
                        v = a_view(mc, u, xg)
                        ins = nc.vector.tensor_tensor(v, bank.rearrange("p (x y g) -> p x y g", x=4, y=8), v, ALU.add)
                    else:
                        b, vt, nh = d
                        v = xT[:, :, b * N:(b + 1) * N].rearrange("p (h v) n -> p v h n", v=2)[:, vt, 2 * nh:2 * nh + 2, :]
                        ins = nc.vector.tensor_tensor(v, bank.rearrange("p (h n) -> p h n", h=2), v, ALU.add)
                    ins.then_inc(evac_sem[name], 1)
                    if kind == "Y" and d != (0, 0, 0):
                        next_stats(eng, i - 1)

            def shift(eng, u, ys):
                for i in range(8 * u, 8 * u + 8):
                    evacuated(eng, i)
                for y in ys:
                    rows = slice(16 * y, 16 * y + 16)
                    eng.dma_start(A2[rows, u, :, :], G[rows, u % 2, :, (7 - y) * SIDE:(7 - y) * SIDE + N])\
                        .then_inc(shifted[u], 16)

            with nc.Block() as block:
                @block.sync
                def _(sp):
                    sp.dma_start(c0[:, :, :, :].rearrange("p a b c -> p (a b c)"), A["c0"].partition_broadcast(TT)).then_inc(cores_in, 16)
                    sp.dma_start(c3[:, :, :, :].rearrange("p a b c -> p (a b c)"), A["c3"].partition_broadcast(TT)).then_inc(cores_in, 16)
                    sp.dma_start(c1[:, :, :, :].rearrange("p a b c -> p (a b c)"), A["c1"]).then_inc(cores_in, 16)
                    sp.dma_start(c2[:, :, :, :].rearrange("p a b c -> p (a b c)"), A["c2"]).then_inc(cores_in, 16)
                    sp.dma_start(r2c[:, :], A["r2c"]).then_inc(cores_in, 16)
                    for u in range(4):
                        shift(sp, u, range(8))

                @block.gpsimd
                def _(pool):
                    g["w_splits"](pool, HB0, HB0 + 2)
                    pool.wait_ge(cores_in, 16 * 5)
                    muls, adds = Count(mul_done), Count(add_done)

                    def term_of_a(r, to):
                        for a in range(4):
                            o = to[:, 64 * a:64 * a + 64].rearrange("p (h o q) -> p h o q", h=2, o=4)
                            i0 = c0[:, r, a, :].rearrange("p (h o q) -> p h o q", h=1, q=1).broadcast_to([TT, 2, 4, 8])
                            i1 = c1[:, r, :, :].rearrange("p h (o q) -> p h o q", o=1).broadcast_to([TT, 2, 4, 8])
                            last = nc.gpsimd.tensor_tensor(o, i0, i1, ALU.mult)
                        return last

                    def term_of_b(half):
                        def term_of(r, to):
                            for o2 in range(4):
                                o = to[:, 128 * o2:128 * o2 + 128].rearrange("p (o c q) -> p o c q", o=4, c=8)
                                i0 = c2[:, r, 4 * half + o2, :].rearrange("p (o c q) -> p o c q", o=1, q=1).broadcast_to([TT, 4, 8, 4])
                                i1 = c3[:, r, :, :].rearrange("p o (c q) -> p o c q", c=1).broadcast_to([TT, 4, 8, 4])
                                last = nc.gpsimd.tensor_tensor(o, i0, i1, ALU.mult)
                            return last
                        return term_of

                    def factor(term_of, n, split, lo):
                        for r in range(RANK):
                            muls.up(term_of(r, term if r else total))
                            pool.wait_ge(mul_done, muls.n)
                            if r:
                                adds.up(nc.gpsimd.tensor_tensor(total[:, 0:n], total[:, 0:n], term[:, 0:n], ALU.add))
                                pool.wait_ge(add_done, adds.n)
                        muls.up(nc.gpsimd.tensor_tensor(split, total[:, 0:n], zeros[0:TT, 0:n], ALU.add))
                        pool.wait_ge(mul_done, muls.n)
                        adds.up(nc.gpsimd.tensor_tensor(split[lo, :], total[lo, 0:n], split[lo, :].bitcast(F32), ALU.subtract))
                        pool.wait_ge(add_done, adds.n)

                    factor(term_of_a, 256, ttA[:, :], slice(64, 96))
                    for half in range(2):
                        factor(term_of_b(half), HALF, ttB[:, half * HALF:half * HALF + HALF], slice(32, 64))
                    norms[1].power(0)

                @block.scalar
                def _(act):
                    read_out(act, "act")

                @block.vector
                def _(dve):
                    read_out(dve, "dve")
                    evacuated(dve, len(groups) - 1)

                @block.tensor
                def _(pe):
                    pe.wait_ge(et_in, 16)
                    for i, (kind, d, _) in enumerate(groups):
                        bank = PS[:, bank_of[i], :]
                        if before_it[i] is not None:
                            evacuated(pe, before_it[i])
                        if kind == "G":
                            u, xi = d
                            yg, x = u // 2, 8 * (u % 2) + xi
                            d0 = (1 - yg) * 8
                            for jp in range(2):
                                lhs = Qs[:, jp, x * N + yg * P:x * N + yg * P + P]
                                rhs = ET[:, jp, :].rearrange("p (a b) -> p a b", a=31)[:, d0:d0 + DY, 15 - x:31 - x]
                                m = nc.tensor.matmul(bank[:, 0:DY * SIDE], lhs, rhs, start=jp == 0, stop=jp == 1)
                        elif kind == "K":
                            b, mc, nh = d
                            for jp in range(2):
                                rhs = Qs[:, jp, :].rearrange("p (x y g) -> p x y g", x=SIDE, y=SIDE)[
                                    :, 8 * nh:8 * nh + 8, :, HEADS0 * b:HEADS0 * b + HEADS0]
                                m = nc.tensor.matmul(bank, ks[:, b, jp, mc * P:mc * P + P], rhs,
                                                     start=jp == 0, stop=jp == 1)
                        elif kind == "A":
                            u, xg, mc = d
                            if xg == 0 and mc == 0:
                                pe.wait_ge(shifted[u], 128)
                            for xi in range(4):
                                m = nc.tensor.transpose(bank[:, xi * P:xi * P + P], A2[:, u, 4 * xg + xi, mc * P:mc * P + P], ident[:, :])
                        else:
                            b, vt, nh = d
                            if b == vt == nh == 0:
                                pe.wait_ge(dve_evac, 24 + 16)
                            for mc in range(2):
                                m = nc.tensor.matmul(bank, VT[:, mc, b * N + vt * P:b * N + vt * P + P],
                                                     AT[:, mc, b * C + nh * HALF:b * C + nh * HALF + HALF],
                                                     start=mc == 0, stop=mc == 1)
                        m.then_inc(pe_group, 1)
                        if kind == "Y" and i == len(groups) - 6:
                            norms[1].averages(0)
                        if kind == "Y" and i == len(groups) - 4:
                            norms[1].turn(0)


def layer12(nc, A, outer, g, layer):
    PS, xT, ident, identb, maskb, bias = (g[x] for x in ("PS", "xT", "ident", "identb", "maskb", "bias"))
    sem, sb, norms, w_used = (g[x] for x in ("sem", "sb", "norms", "w_used"))
    chunk_product, block_product, block_pair = g["chunk_product"], g["block_product"], g["block_pair"]
    norm = norms[layer]
    masked = layer == 1
    n0 = HB0 if masked else HB0 + HB1
    per_pass = 16 if masked else 8
    n1 = n0 + (HB1 if masked else HB2)
    PJ, S, PT, O = (0, 1), 2, 4, 6
    SCALE = 64 ** -0.5

    def q_block(j, second):
        return 6 * j + (n0 + 2 + (per_pass if second else 0))

    def spans(ahead):
        if not masked:
            return ((0, N), (0, N))
        return ((0, N), (P, N)) if ahead else ((0, P), (0, N))

    def tiles(ahead):
        at, r = 0, []
        for kt in range(2):
            for qt in range(2):
                lo, hi = spans(ahead)[qt]
                if lo <= kt * P < hi:
                    r.append((kt, qt, at))
                    at += P
        return r

    with ExitStack() as ctx:
        xh = sb(ctx, "xh", [P, CK, T], F32R)
        xl = sb(ctx, "xl", [P, CK, T], F32R)
        ytmp = sb(ctx, "ytmp", [P, 2, T])
        o_shape = [P, CK, HALF] if masked else [P, PAIRS // 2, T]
        oh = sb(ctx, "oh", o_shape, F32R)
        ol = sb(ctx, "ol", o_shape, F32R)
        vT = sb(ctx, "vT", [P, T])
        v = sb(ctx, "v", [P, CK, P])
        prob = sb(ctx, "prob", [P, 2, 2, N])
        probT = sb(ctx, "probT", [P, 4, HALF])
        nmax = sb(ctx, "nmax", [P, 2, 2])
        psum_ = sb(ctx, "psum", [P, 2, 2])
        prec = sb(ctx, "prec", [P, 2, 2])
        if masked:
            qh = sb(ctx, "qh", [P, 2, T], F32R)
            ql = sb(ctx, "ql", [P, 2, T], F32R)
            kh = sb(ctx, "kh", [P, T], F32R)
            kl = sb(ctx, "kl", [P, T], F32R)
        else:
            qp = sb(ctx, "qp", [P, T])
            q = sb(ctx, "qa", [KROWS, 2, T])
            k = sb(ctx, "ka", [KROWS, 2, T])
            rel = sb(ctx, "rel", [P, 2, 64])
            kb = sb(ctx, "kb", [P, PAIRS])

        v_evac = sem("v_evac")
        v_tr = sem("v_tr")
        v_ready = sem("v_ready")
        q_evac = sem("q_evac")
        qa_evac = sem("qa_evac")
        k_evac = sem("k_evac")
        v_half = sem("v_half")
        k_half = sem("k_half")
        k_first = sem("k_first")
        rel_done = sem("rel_done")
        split_done = sem("split_done")
        relh_evac = sem("relh_evac")
        relw_evac = sem("relw_evac")
        s_done = sem("s_done")
        p_max = sem("p_max")
        p_exp = sem("p_exp")
        p_rec = sem("p_rec")
        p_norm = sem("p_norm")
        t_done = sem("t_done")
        t_evac = sem("t_evac")
        o_done = sem("o_done")
        o_hi = sem("o_hi")
        o_ready = sem("o_ready")
        sum_done = sem("sum_done")
        tables_in = sem("tables_in")
        kb_ready = sem("kb_ready")
        zeroed = sem("zeroed")

        def pairs(eng, take_q, step, out_pass):
            take_q(0, n0 + 2)
            step(0, False, True)
            with eng.Fori(1, PAIRS // 2) as j:
                take_q(j, q_block(j, False), False)
                step(j, False, True)
            take_q(PAIRS // 2, q_block(PAIRS // 2, False), False)
            out_pass(0)
            step(PAIRS // 2, True, True)
            with eng.Fori(PAIRS // 2 + 1, PAIRS - 1) as j:
                take_q(j, q_block(j, True), True)
                step(j, True, True)
            take_q(PAIRS - 1, q_block(PAIRS - 1, True), True)
            step(PAIRS - 1, True, False)
            out_pass(1)

        def sum_banks(half, s):
            if masked:
                return (s if half else S + s,)
            s = s if half else 1 - s
            return (2 * s, 2 * s + 1)

        def pass_block(half):
            return n0 + 2 + 24 + 2 if half == 0 else n1 - per_pass

        def k_banks(more):
            return (S, S + 1) if more else (S, 0)

        with nc.Block() as block:
            @block.sync
            def _(sp):
                if not masked:
                    sp.dma_start(rel[:, :, :], A["rel"].rearrange("a p n -> p a n")).then_inc(tables_in, 16)
                    for hh in range(2):
                        sp.dma_start(k[64:KROWS, hh, :], A["hot"]).then_inc(tables_in, 16)
                g["w_loads"](sp, n0 + 2, min(n1 + 2, HB_TOTAL))

            @block.gpsimd
            def _(pool):
                if not masked:
                    g["w_splits"](pool, n0, n0 + 2)
                    pool.wait_ge(g["w_ready"], n0 + 2)
                    nc.gpsimd.memset(q[64:96, :, :], 0.0).then_inc(zeroed, 1)
                    pool.wait_ge(zeroed, 1)
                norm.power(1)
                g["w_splits"](pool, n0 + 2, n1)
                norms[layer + 1].power(0)

            @block.scalar
            def _(act):
                norm.on_scalar(xh, ytmp)
                if not masked:
                    act.wait_ge(zeroed, 1)

                def take_q(j, n, ahead=None):
                    both = PS[:, 0:2, :].rearrange("p a n -> p (a n)")
                    act.wait_ge(w_used, n + 2)
                    if masked:
                        for hh in range(2):
                            rows = slice(64 * hh, 64 * hh + 64)
                            last = nc.scalar.activation(qh[rows, hh, :], PS[rows, 0:2, :].rearrange("p a n -> p (a n)"), ACT.Copy)
                        last.then_inc(q_evac, 1)
                    else:
                        nc.scalar.activation(qp[:, :], both, ACT.Identity, bias=bias[:, bass.ds(j, 1)])\
                            .then_inc(q_evac, 1)

                def step(j, ahead, more):
                    n = q_block(j, ahead)
                    if not masked:
                        act.wait_ge(rel_done, j + 1)
                        for bank in range(2):
                            for hh in range(2):
                                src = PS[32 * hh:32 * hh + SIDE, O + bank, :].rearrange("p (h b w) -> p h b w", h=8, b=B)
                                dst = q[64:64 + SIDE, hh, :].rearrange("p (b h w) -> p h b w", b=B, h=SIDE)[
                                    :, 8 * bank:8 * bank + 8, :, :]
                                last = nc.scalar.activation(dst, src, ACT.Copy)
                        last.then_inc(relh_evac, 1)
                    def evac_k(half):
                        bank, part = k_banks(more)[half], slice(half * HALF, half * HALF + HALF)
                        if half:
                            act.wait_ge(w_used, n + 4)
                        else:
                            act.wait_ge(k_half, j + 1)
                        if masked:
                            last = nc.scalar.activation(kh[:, part], PS[:, bank, :], ACT.Copy, scale=SCALE)
                        else:
                            for hh in range(2):
                                rows = slice(64 * hh, 64 * hh + 64)
                                last = nc.scalar.activation(k[0:64, hh, part], PS[rows, bank, :], ACT.Identity,
                                                            bias=kb[rows, bass.ds(j, 1)], scale=SCALE)
                        last.then_inc(k_evac, 1)

                    if masked:
                        evac_k(0)
                    if more:
                        evac_k(1)

                    def evac_t(u):
                        act.wait_ge(t_done, 8 * j + u + 1)
                        w = P * len(tiles(ahead))
                        nc.scalar.activation(probT[:, u % 4, 0:w], PS[:, PT + u % 2, 0:w], ACT.Copy).then_inc(t_evac, 1)

                    for u in range(UNITS):
                        if u == 3 and not more:
                            evac_k(1)
                        act.wait_ge(p_max, 8 * j + u + 1)
                        for qt, (lo, hi) in enumerate(spans(ahead)):
                            last = nc.scalar.activation(prob[:, u % 2, qt, lo:hi], PS[:, S + u % 2, qt * N + lo:qt * N + hi],
                                                        ACT.Exp, bias=nmax[:, u % 2, qt:qt + 1],
                                                        accum_out=psum_[:, u % 2, qt:qt + 1])
                        last.then_inc(p_exp, 1)
                        if u:
                            evac_t(u - 1)
                    evac_t(UNITS - 1)

                pairs(act, take_q, step, lambda half: None)

            @block.vector
            def _(dve):
                nc.vector.memset(nmax[:, :, :], 0.0).then_inc(sum_done, 2)
                nc.vector.memset(psum_[:, :, :], 0.0).then_inc(o_ready, 1)

                def last_stats():
                    if masked:
                        for c in (5, 7):
                            norm.chunk_stats(c, (B - 1,)).then_inc(norm.stats, 1)
                    else:
                        norm.chunk_stats(7).then_inc(norm.stats, 1)

                def after(c):
                    if c == 0:
                        norm.aggregate(*(((5, 7), 32) if masked else ((6, 7), CK)))
                        norm.squares(1)
                    if c == 1:
                        norm.variances(1)
                    if c == 2:
                        norm.to_rows(1)
                    if c == 3:
                        norm.coefficients(1)
                    if c in (4, 5) and masked:
                        t = (qh, ql)[c - 4]
                        nc.vector.memset(t[64:P, 0, :].bitcast(F32), 0.0)
                        nc.vector.memset(t[0:64, 1, :].bitcast(F32), 0.0).then_inc(zeroed, 1)

                norm.on_vector(xh, xl, ytmp, after, flush=(0,), wait_for_first=last_stats)
                if not masked:
                    dve.wait_ge(zeroed, 1)
                    nc.vector.tensor_scalar(kb[:, :], bias[:, 8:16], SCALE, None, ALU.mult).then_inc(kb_ready, 1)

                def evac_v(j, used, bank):
                    for half in range(2):
                        part = slice(half * HALF, half * HALF + HALF)
                        if bank == 0 and half == 0:
                            dve.wait_ge(v_half, j)
                        else:
                            dve.wait_ge(w_used, used)
                        if masked:
                            ins = nc.vector.tensor_copy(vT[:, part], PS[:, bank + half, :])
                        else:
                            ins = nc.vector.tensor_scalar(vT[:, part], PS[:, bank + half, :], bias[:, bass.ds(j + 16, 1)],
                                                          None, ALU.add)
                    ins.then_inc(v_evac, 1)

                def evac_o(j, half, grp):
                    dve.wait_ge(o_done, 2 * j + grp + 1)
                    jl = j - half * (PAIRS // 2)
                    src = PS[:, O + grp, :]
                    if masked:
                        src = src.rearrange("p (b r c) -> p b r c", b=2, c=CK)
                        hi, lo = (t[:, :, :].rearrange("p c (b j r) -> p b j r c", b=B, j=4)[
                            :, 2 * grp:2 * grp + 2, bass.ds(jl, 1), :, :].rearrange("p b j r c -> p b (j r) c") for t in (oh, ol))
                    else:
                        hi, lo = (t[:, bass.ds(jl, 1), HALF * grp:HALF * grp + HALF].rearrange("p a n -> p (a n)") for t in (oh, ol))
                    nc.vector.tensor_copy(hi, src).then_inc(o_hi, 1)
                    dve.wait_ge(o_hi, 2 * j + grp + 1)
                    nc.vector.tensor_tensor(lo, src, hi.bitcast(F32), ALU.subtract).then_inc(o_ready, 1)

                def take_q(j, n, ahead=None):
                    dve.wait_ge(q_evac, j + 1)
                    if masked:
                        for hh in range(2):
                            rows = slice(64 * hh, 64 * hh + 64)
                            last = nc.vector.tensor_tensor(ql[rows, hh, :], PS[rows, 0:2, :].rearrange("p a n -> p (a n)"),
                                                           qh[rows, hh, :].bitcast(F32), ALU.subtract)
                        last.then_inc(qa_evac, 1)
                    else:
                        for hh in range(2):
                            rows = slice(64 * hh, 64 * hh + 64)
                            last = nc.vector.tensor_scalar(q[0:64, hh, :], PS[rows, 0:2, :].rearrange("p a n -> p (a n)"),
                                                           bias[rows, bass.ds(j, 1)], None, ALU.add)
                        last.then_inc(qa_evac, 1)

                def step(j, ahead, more):
                    n = q_block(j, ahead)

                    def rest_of_k(half):
                        part = slice(half * HALF, half * HALF + HALF)
                        dve.wait_ge(k_evac, 2 * j + half + 1)
                        nc.vector.scalar_tensor_tensor(kl[:, part], PS[:, k_banks(more)[half], :], SCALE,
                                                       kh[:, part].bitcast(F32), ALU.mult, ALU.subtract).then_inc(split_done, 1)

                    dve.wait_ge(v_tr, j + 1)
                    nc.vector.tensor_copy(v[:, :, :].rearrange("p a n -> p (a n)"),
                                          PS[:, PT:PT + 2, :].rearrange("p a n -> p (a n)")).then_inc(v_ready, 1)
                    if masked:
                        rest_of_k(0)
                        if more:
                            rest_of_k(1)
                    else:
                        dve.wait_ge(rel_done, j + 1)
                        for bank in range(2):
                            for hh in range(2):
                                src = PS[64 + 32 * hh:64 + 32 * hh + SIDE, O + bank, :].rearrange("p (w b h) -> p w b h", w=8, b=B)
                                dst = q[96:96 + SIDE, hh, :].rearrange("p (b h w) -> p w b h", b=B, h=SIDE)[
                                    :, 8 * bank:8 * bank + 8, :, :]
                                last = nc.vector.tensor_copy(dst, src)
                        last.then_inc(relw_evac, 1)
                        dve.wait_ge(k_half, j + 1)
                        for hh in range(2):
                            rows = slice(64 * hh, 64 * hh + 64)
                            last = nc.vector.tensor_scalar(k[0:64, hh, 0:HALF], PS[rows, S, :], SCALE, kb[rows, bass.ds(j, 1)],
                                                           ALU.mult, ALU.add)
                        last.then_inc(k_first, 1)
                    for u in range(UNITS):
                        unit = 8 * j + u + 1
                        if masked and u == 3 and not more:
                            rest_of_k(1)
                        dve.wait_ge(s_done, unit)
                        if masked:
                            for qt, (lo, hi) in enumerate(spans(ahead)):
                                last = nc.vector.tensor_reduce(nmax[:, u % 2, qt:qt + 1], PS[:, S + u % 2, qt * N + lo:qt * N + hi],
                                                               AX, ALU.max, negate=True)
                        else:
                            last = nc.vector.tensor_reduce(nmax[:, u % 2, :], PS[:, S + u % 2, :].rearrange("p (a n) -> p a n", a=2),
                                                           AX, ALU.max, negate=True)
                        last.then_inc(p_max, 1)
                        if more and u == UNITS - 2:
                            evac_v(j + 1, n + 6, 0)
                        dve.wait_ge(p_exp, unit)
                        nc.vector.reciprocal(prec[:, u % 2, :], psum_[:, u % 2, :]).then_inc(p_rec, 1)
                        dve.wait_ge(p_rec, unit)
                        for qt, (lo, hi) in enumerate(spans(ahead)):
                            last = nc.vector.tensor_scalar(prob[:, u % 2, qt, lo:hi], prob[:, u % 2, qt, lo:hi],
                                                           prec[:, u % 2, qt:qt + 1], None, ALU.mult)
                        last.then_inc(p_norm, 1)
                        if u == 5:
                            evac_o(j, int(ahead), 0)
                    evac_o(j, int(ahead), 1)

                def out_pass(half):
                    base = 2 + CK * half
                    n = pass_block(half)

                    def sums(o, s):
                        x = xT[:, bass.ds(o, 1), :]
                        if masked:
                            dve.wait_ge(w_used, n + 2 * o + 2)
                            x = x.rearrange("p a (b r) -> p (a b) r", b=B)[:, :, half * P:half * P + P]
                            nc.vector.tensor_tensor(x, PS[:, sum_banks(half, s)[0], :].rearrange("p (b r) -> p b r", b=B), x, ALU.add)\
                                .then_inc(sum_done, 1)
                        else:
                            dve.wait_ge(w_used, n + o + 1)
                            x = x.rearrange("p a n -> p (a n)")
                            src = PS[:, sum_banks(half, s)[0]:sum_banks(half, s)[1] + 1, :].rearrange("p a n -> p (a n)")
                            if half:
                                ins = nc.vector.scalar_tensor_tensor(x, src, bias[:, bass.ds(o + 24, 1)], x, ALU.add, ALU.add)
                            else:
                                ins = nc.vector.tensor_tensor(x, src, x, ALU.add)
                            ins.then_inc(sum_done, 1)

                    def stats(o):
                        dve.wait_ge(sum_done, base + o + 1)
                        nxt.chunk_stats(o).then_inc(nxt.stats, 1)

                    nxt = norms[layer + 1]
                    if not half:
                        with dve.Fori(0, CK // 2) as i:
                            for s in range(2):
                                sums(2 * i + s, s)
                    else:
                        with dve.Fori(0, CK // 2 - 1) as i:
                            for s in range(2):
                                sums(2 * i + s, s)
                                stats(2 * i + s)
                        nxt.aggregate(range(6), 6)
                        nxt.squares(0)
                        sums(6, 0)
                        nxt.variances(0)
                        stats(6)
                        nxt.to_rows(0)
                        sums(7, 1)
                        nxt.coefficients(0)
                        dve.wait_ge(sum_done, base + CK)

                evac_v(0, n0 + 3, S)
                pairs(dve, take_q, step, out_pass)

            @block.tensor
            def _(pe):
                def before(c, slot):
                    if (c, slot) == (0, 1):
                        norm.averages(1)
                    if (c, slot) == (3, 0):
                        norm.turn(1)

                block_pair(n0, xh, xl, (S, S + 1), PJ, norm.ready, before)
                if not masked:
                    pe.wait_ge(tables_in, 48)

                def scores(j, u, ahead):
                    b, hh = u // 2, u % 2
                    for qt, (lo, hi) in enumerate(spans(ahead)):
                        at = qt * N
                        qs, ks = slice(b * N + qt * P, b * N + qt * P + P), slice(b * N + lo, b * N + hi)
                        if not masked:
                            m = nc.tensor.matmul(PS[:, S + u % 2, at + lo:at + hi], q[:, hh, qs], k[:, hh, ks],
                                                 start=True, stop=True)
                        else:
                            for i, (x, y) in enumerate(((qh, kh), (qh, kl), (ql, kh))):
                                nc.tensor.matmul(PS[:, S + u % 2, at + lo:at + hi], x[:, hh, qs], y[:, ks],
                                                 start=i == 0, stop=False)
                            m = nc.tensor.matmul(PS[:, S + u % 2, at + qt * P:at + qt * P + P], identb[:, :],
                                                 maskb[:, int(ahead), :], start=False, stop=True)
                    m.then_inc(s_done, 1)

                def transposed(j, u, ahead):
                    pe.wait_ge(p_norm, 8 * j + u + 1)
                    for kt, qt, at in tiles(ahead):
                        m = nc.tensor.transpose(PS[:, PT + u % 2, at:at + P], prob[:, u % 2, qt, kt * P:kt * P + P], ident[:, :])
                    m.then_inc(t_done, 1)

                def outputs(j, u0, ahead):
                    b, bank = u0 // 2, O + u0 // 4
                    pe.wait_ge(t_evac, 8 * j + u0 + 2)
                    if not masked:
                        for kt in range(2):
                            for hh in range(2):
                                m = nc.tensor.matmul(PS[64 * hh:64 * hh + 64, bank, (b % 2) * N:(b % 2) * N + N],
                                                     v[:, 2 * b + kt, 64 * hh:64 * hh + 64],
                                                     probT[:, (u0 + hh) % 4, kt * N:kt * N + N],
                                                     start=kt == 0, stop=kt == 1)
                    else:
                        whole, part = (1, 0) if ahead else (0, 1)
                        w_at, p_at, p_col = (P, 0, 0) if ahead else (0, N, 64)
                        for u in (u0, u0 + 1):
                            hh, col = u % 2, (u % 4) * P
                            for kt, at, width, to in ((whole, w_at, N, col), (part, p_at, P, col + p_col)):
                                for r in range(2):
                                    m = nc.tensor.matmul(PS[64 * r:64 * r + 64, bank, to:to + width // 2],
                                                         v[:, 2 * b + kt, 64 * hh:64 * hh + 64],
                                                         probT[:, u % 4, at + r:at + width:2],
                                                         start=kt == whole, stop=kt == part)
                    if u0 % 4 == 2:
                        m.then_inc(o_done, 1)

                def take_q(j, n, ahead=None):
                    pe.wait_ge(v_evac, j + 1)
                    if ahead is None:
                        return
                    block_product(n, xh, xl, PJ, range(0, 1))
                    transposed(j - 1, UNITS - 2, ahead)
                    outputs(j - 1, UNITS - 4, ahead)
                    block_product(n, xh, xl, PJ, range(1, 2))
                    transposed(j - 1, UNITS - 1, ahead)
                    block_product(n, xh, xl, PJ, range(2, 3))
                    outputs(j - 1, UNITS - 2, ahead)
                    block_product(n, xh, xl, PJ, range(3, CK))

                def step(j, ahead, more):
                    n = q_block(j, ahead)
                    for tt in range(CK):
                        m = nc.tensor.transpose(PS[:, PT + tt // 4, (tt % 4) * P:(tt % 4) * P + P],
                                                vT[:, tt * P:tt * P + P], ident[:, :])
                    m.then_inc(v_tr, 1)
                    k_bank = (S, S + 1) if more else (S,)
                    block_product(n + 2, xh, xl, k_bank, range(4), used=more)
                    pe.wait_ge(q_evac, j + 1)
                    pe.wait_ge(qa_evac, j + 1)
                    if not masked:
                        pe.wait_ge(o_ready, 2 * j + 1)
                        for i in range(SIDE):
                            bank, cols = O + i // 8, slice((i % 8) * 64, (i % 8) * 64 + 64)
                            of_row = qp[:, :].rearrange("p (b h w) -> p h b w", b=B, h=SIDE)[:, i, :, :]
                            of_col = qp[:, :].rearrange("p (b h w) -> p w b h", b=B, h=SIDE)[:, i, :, :]
                            nc.tensor.matmul(PS[0:48, bank, cols], rel[:, 0, 15 - i:63 - i], of_row, start=True, stop=True)
                            m = nc.tensor.matmul(PS[64:112, bank, cols], rel[:, 1, 15 - i:63 - i], of_col, start=True, stop=True)
                        m.then_inc(rel_done, 1)
                    block_product(n + 2, xh, xl, k_bank, range(4, CK), used=more, first_bank=k_half)

                    def next_v(c):
                        if more:
                            chunk_product(n + 4 + c // 4, c // 4, c % 4, c, xh, xl, PJ, c == 0, c == CK - 1,
                                          first_bank=v_half if c == CK - 1 else None)

                    def second_half(chunks):
                        if not more:
                            block_product(n + 2, xh[:, :, HALF:T], xl[:, :, HALF:T], (0,), chunks)

                    next_v(0)
                    if not masked:
                        pe.wait_ge(relh_evac, j + 1)
                        pe.wait_ge(relw_evac, j + 1)
                    for u in range(UNITS):
                        if u in ((0, 1) if more else (0, 4)):
                            half = int(u > 0)
                            if masked:
                                pe.wait_ge(k_evac, 2 * j + half + 1)
                                pe.wait_ge(split_done, 2 * j + half + 1)
                            else:
                                pe.wait_ge(k_evac if half else k_first, j + 1)
                        scores(j, u, ahead)
                        if u < 3:
                            second_half(range(3 * u, min(3 * u + 3, CK)))
                        if u:
                            if u == 1:
                                next_v(1)
                            if u < UNITS - 1:
                                next_v(u + 1)
                            if u == 1:
                                pe.wait_ge(v_ready, j + 1)
                            if not more or u < UNITS - 1:
                                transposed(j, u - 1, ahead)
                        if u in ((3, 5) if more else (3, 5, 7)):
                            outputs(j, u - 3, ahead)
                    if not more:
                        first_out_block(range(0, 2))
                        transposed(j, UNITS - 1, ahead)
                        first_out_block(range(2, 3))
                        outputs(j, UNITS - 2, ahead)

                def first_out_block(chunks):
                    if not masked:
                        for c in chunks:
                            chunk_product(pass_block(1), 0, c, c, oh, ol, sum_banks(1, 0), c == 0, c == 3)

                def out_pass(half):
                    pe.wait_ge(o_ready, 8 * half + 9)
                    n = pass_block(half)

                    def out_block(o, s, begin=0):
                        pe.wait_ge(sum_done, CK * half + o + 1)
                        if half == 0 and 0 in sum_banks(half, s):
                            pe.wait_ge(q_evac, PAIRS // 2 + 1)
                            pe.wait_ge(qa_evac, PAIRS // 2 + 1)
                        if masked:
                            block_product(n + 2 * o, oh, ol, sum_banks(half, s))
                        else:
                            for c in range(begin, 4):
                                chunk_product(n + o, s, c, c, oh, ol, sum_banks(half, s), c == 0, c == 3)

                    if half:
                        out_block(0, 0, begin=0 if masked else 3)
                        out_block(1, 1)
                    with pe.Fori(half, CK // 2 - half) as i:
                        for s in range(2):
                            out_block(2 * i + s, s)
                    if half:
                        out_block(6, 0)
                        norms[layer + 1].averages(0)
                        out_block(7, 1)
                        norms[layer + 1].turn(0)
                    if half == 0:
                        pe.wait_ge(sum_done, 2 + CK)

                pairs(pe, take_q, step, out_pass)


def layer3(nc, A, out, outer, g):
    PS, xT, bias, ttA, ttB, r2c = (g[x] for x in ("PS", "xT", "bias", "ttA", "ttB", "r2c"))
    sem, sb, norms = (g[x] for x in ("sem", "sb", "norms"))
    norm = norms[3]
    O23, O01 = 32, 32
    STORES = 4
    QUART = 8
    with ExitStack() as ctx:
        xh = sb(ctx, "xh", [P, CK, T], F32R)
        xl = sb(ctx, "xl", [P, CK, T], F32R)
        ytmp = sb(ctx, "ytmp", [P, 2, T])
        Mh = sb(ctx, "Mh", [P, CK, C], F32R)
        Ml = sb(ctx, "Ml", [P, CK, C], F32R)
        BD = sb(ctx, "BD", [TT, 2, QUART, P], F32R)
        K = sb(ctx, "K", [P, 2, N])
        Kh = sb(ctx, "Kh", [P, 2, N], F32R)
        Kl = sb(ctx, "Kl", [P, 2, N], F32R)
        kt = sb(ctx, "kt", [P, 2, N])
        kx = sb(ctx, "kx", [P, 3, SIDE])
        kxt = sb(ctx, "kxt", [P, 3, SIDE])
        taps = sb(ctx, "taps", [P, 9])
        near_x = sb(ctx, "near_x", [P, 3, SIDE])
        near_y = sb(ctx, "near_y", [P, 3, 2, SIDE])
        act_out = ytmp[:, :, 0:2 * N].rearrange("p a (s n) -> p a s n", s=2)
        consts3 = sem("consts3")
        bd_ready = sem("bd_ready")
        m_done = sem("m_done")
        m_hi = sem("m_hi")
        m_lo = sem("m_lo")
        k_step = sem("k_step")
        k_ready = sem("k_ready")
        u_done = sem("u_done")
        u_hi = sem("u_hi")
        u_lo = sem("u_lo")
        f_done = sem("f_done")
        relu_done = sem("relu_done")
        x_final = sem("x_final")
        stored = sem("stored")

        with nc.Block() as block:
            @block.sync
            def _(sp):
                sp.dma_start(taps[:, :], A["taps"].partition_broadcast(P)).then_inc(consts3, 16)
                sp.dma_start(near_x[:, :, :].rearrange("p a b -> p (a b)"), A["near_x"]).then_inc(consts3, 16)
                sp.dma_start(near_y[:, :, :, :].rearrange("p a b c -> p (a b c)"), A["near_y"]).then_inc(consts3, 16)
                for b in range(B):
                    for i in range(STORES):
                        sp.wait_ge(x_final, 4 * b + 4 // STORES * (i + 1))
                        cs = slice(CK // STORES * i, CK // STORES * (i + 1))
                        sp.dma_start(out.rearrange("c p t -> p c t")[:, cs, b * N:(b + 1) * N],
                                     xT[:, cs, b * N:(b + 1) * N]).then_inc(stored, 16)
                sp.wait_ge(stored, 16 * B * STORES)

            @block.gpsimd
            def _(pool):
                def masked_factor(i):
                    if i >= 2:
                        pool.wait_ge(m_done, 4 * (i - 1))
                    o = BD[:, i % 2, :, :].rearrange("p o (a c) -> p o a c", a=4)
                    fac = ttB[:, i * 256:i * 256 + 256].bitcast(F32).rearrange("p (o a c) -> p o a c", o=QUART, a=1)\
                        .broadcast_to([TT, QUART, 4, 32])
                    msk = r2c[:, :].rearrange("p (o a c) -> p o a c", o=1, c=1).broadcast_to([TT, QUART, 4, 32])
                    nc.gpsimd.tensor_tensor(o, fac, msk, ALU.mult).then_inc(bd_ready, 1)

                masked_factor(0)
                masked_factor(1)
                norm.power(1)
                for i in range(2, 4):
                    masked_factor(i)
                pool.wait_ge(consts3, 48)
                step = Count(k_step)
                for dx in range(3):
                    to = kxt if dx else kx
                    t = taps[:, :].rearrange("p (a b c) -> p a b c", a=3, c=1)[:, :, dx, :].broadcast_to([P, 3, SIDE])
                    m = near_x[:, dx:dx + 1, :].broadcast_to([P, 3, SIDE])
                    step.up(nc.gpsimd.tensor_tensor(to[:, :, :], t, m, ALU.mult))
                    pool.wait_ge(k_step, step.n)
                    if dx:
                        step.up(nc.gpsimd.tensor_tensor(kx[:, :, :], kx[:, :, :], kxt[:, :, :], ALU.add))
                        pool.wait_ge(k_step, step.n)
                for dy in range(3):
                    to = (kt if dy else K)[:, :, :].rearrange("p t (y x) -> p t y x", y=SIDE)
                    a = near_y[:, dy, :, :].rearrange("p t (y x) -> p t y x", x=1).broadcast_to([P, 2, SIDE, SIDE])
                    b = kx[:, dy, :].rearrange("p (t y x) -> p t y x", t=1, y=1).broadcast_to([P, 2, SIDE, SIDE])
                    step.up(nc.gpsimd.tensor_tensor(to, a, b, ALU.mult))
                    pool.wait_ge(k_step, step.n)
                    if dy:
                        ins = nc.gpsimd.tensor_tensor(K[:, :, :], K[:, :, :], kt[:, :, :], ALU.add)
                        step.up(ins)
                        pool.wait_ge(k_step, step.n)
                step.up(nc.gpsimd.tensor_copy(Kh[:, :, :], K[:, :, :]))
                pool.wait_ge(k_step, step.n)
                nc.gpsimd.tensor_tensor(Kl[:, :, :], K[:, :, :], Kh[:, :, :].bitcast(F32), ALU.subtract).then_inc(k_ready, 1)

            def u_view(t, b, tt, oh):
                return t[:, 4 * oh:4 * oh + 4, (2 * b + tt) * P:(2 * b + tt) * P + P]

            def m_views(i):
                src = PS[:, i % 4, :].rearrange("p (b k a) -> p b k a", b=2, k=CK)
                return src, *(t[:, :, :].rearrange("p k (a b) -> p b k a", b=O23)[:, 2 * i:2 * i + 2, :, :] for t in (Mh, Ml))

            @block.scalar
            def _(act):
                def head_of_m(c):
                    for i in range(2 * c, 2 * c + 2):
                        act.wait_ge(m_done, i + 1)
                        src, hi, _ = m_views(i)
                        nc.scalar.activation(hi, src, ACT.Copy).then_inc(m_hi, 1)

                for c in range(CK - 1):
                    head_of_m(c)
                norm.y(nc.scalar, 0, (2, 3), ytmp, norm.y_act)
                head_of_m(CK - 1)
                norm.head(0, xh, ytmp)
                norm.on_scalar(xh, ytmp, begin=1)

                def relu(b):
                    for op in range(4):
                        i = 4 * b + op
                        act.wait_ge(f_done, i + 1)
                        if i >= 2:
                            act.wait_ge(x_final, i - 1)
                        for s in range(2):
                            o = 2 * op + s
                            last = nc.scalar.activation(act_out[:, i % 2, s, :], PS[:, 4 + i % 4, s * N:s * N + N],
                                                        ACT.Relu, bias=bias[:, 32 + o:33 + o])
                        last.then_inc(relu_done, 1)

                for b in range(B):
                    for tt in range(2):
                        act.wait_ge(u_done, 4 * b + 2 * tt + 2)
                        for oh in range(2):
                            nc.scalar.activation(u_view(xh, b, tt, oh), PS[:, 2 * tt + oh, :].rearrange("p (c n) -> p c n", c=4),
                                                 ACT.Copy).then_inc(u_hi, 1)
                    if b:
                        relu(b - 1)
                relu(B - 1)

            @block.vector
            def _(dve):
                def rest_of_m(c):
                    for i in range(2 * c, 2 * c + 2):
                        dve.wait_ge(m_hi, i + 1)
                        src, hi, lo = m_views(i)
                        nc.vector.tensor_tensor(lo, src, hi.bitcast(F32), ALU.subtract).then_inc(m_lo, 1)

                norm.chunk_stats(7).then_inc(norm.stats, 1)
                norm.aggregate((6, 7), CK)
                norm.squares(1)
                for c in range(CK):
                    if c == CK - 1:
                        norm.y(nc.vector, 0, (0, 1), ytmp, norm.y_dve)
                    rest_of_m(c)
                    if c == 0:
                        norm.variances(1)
                    if c == 1:
                        norm.to_rows(1)
                    if c == 3:
                        norm.coefficients(1)
                norm.rest(0, xh, xl, ytmp)
                norm.on_vector(xh, xl, ytmp, lambda c: None, begin=1)

                def add(b):
                    for op in range(4):
                        i = 4 * b + op
                        dve.wait_ge(relu_done, i + 1)
                        x = xT[:, 2 * op:2 * op + 2, b * N:(b + 1) * N]
                        nc.vector.tensor_tensor(x, act_out[:, i % 2, :, :], x, ALU.add).then_inc(x_final, 1)

                for b in range(B):
                    for i in range(4):
                        tt, oh = i // 2, i % 2
                        dve.wait_ge(u_hi, 4 * b + i + 1)
                        nc.vector.tensor_tensor(u_view(xl, b, tt, oh), PS[:, i, :].rearrange("p (c n) -> p c n", c=4),
                                                u_view(xh, b, tt, oh).bitcast(F32), ALU.subtract).then_inc(u_lo, 1)
                    if b:
                        add(b - 1)
                add(B - 1)

            @block.tensor
            def _(pe):
                for i in range(16):
                    if i == 1:
                        norm.averages(1)
                    if i == 6:
                        norm.turn(1)
                    if i % 4 == 0:
                        pe.wait_ge(bd_ready, i // 4 + 1)
                    if i >= 4:
                        pe.wait_ge(m_lo, i - 3)
                    for s in range(2):
                        m = nc.tensor.matmul(PS[:, i % 4, s * 256:s * 256 + 256], BD[:, (i // 4) % 2, (2 * i + s) % QUART, :],
                                             ttA[:, :], start=True, stop=True)
                    m.then_inc(m_done, 1)
                pe.wait_ge(m_lo, 16)

                def channel_product(b):
                    if b == 0:
                        order = [(c, tt, oh) for c in range(CK) for tt in range(2) for oh in range(2)]
                    else:
                        order = [(c, tt, oh) for tt in range(2) for oh in range(2) for c in range(CK)]
                    for c, tt, oh in order:
                        bank = 2 * tt + oh
                        if b and c == 0:
                            pe.wait_ge(u_lo, 4 * (b - 1) + bank + 1)
                        cols = slice((2 * b + tt) * P, (2 * b + tt) * P + P)
                        for k, (x, w) in enumerate(((xh, Mh), (xh, Ml), (xl, Mh))):
                            if b == tt == oh == 0 and k != 1:
                                norm.ready(c, k == 2)
                            m = nc.tensor.matmul(PS[:, bank, :], x[:, c, cols], w[:, c, oh * HALF:oh * HALF + HALF],
                                                 start=c == 0 and k == 0, stop=c == CK - 1 and k == 2)
                        if c == CK - 1:
                            m.then_inc(u_done, 1)

                def convolution(b):
                    for op in range(4):
                        i = 4 * b + op
                        if op == 0:
                            if b == 0:
                                pe.wait_ge(k_ready, 1)
                            pe.wait_ge(u_lo, 4 * b + 4)
                        if i >= 4:
                            pe.wait_ge(relu_done, i - 3)
                        for s in range(2):
                            o = 2 * op + s
                            for tt in range(2):
                                cols = slice((2 * b + tt) * P, (2 * b + tt) * P + P)
                                for k, (u, w) in enumerate(((xh, Kh), (xl, Kh), (xh, Kl))):
                                    m = nc.tensor.matmul(PS[:, 4 + i % 4, s * N:s * N + N], u[:, o, cols], w[:, tt, :],
                                                         start=tt == 0 and k == 0, stop=tt == 1 and k == 2)
                        m.then_inc(f_done, 1)

                for b in range(B):
                    channel_product(b)
                    if b:
                        convolution(b - 1)
                convolution(B - 1)


def lay_out(v):
    def f(name):
        return np.asarray(v[name])

    def chunks(a):
        return a.T.reshape(CK, P, -1)

    def cols(a):
        return a.reshape(-1, P).T

    def block(w, d):
        return w[:, d:d + P].reshape(2, 4, P, P).transpose(0, 2, 1, 3).reshape(2, P, HALF)

    def rows(w):
        return w.reshape(-1, C).T

    def in_turns(a, b):
        return np.stack([a[0], b[0], a[1], b[1]])

    s0 = [in_turns(*(block(f("L0_conv_Wv"), P * i) for i in range(2)))] + [block(f("L0_conv_Wk"), P * i) for i in range(2)]
    s0 += [block(f("L0_conv_Wq"), P * i) for i in range(8)]

    def heads(q, k, w, out_blocks):
        s = [in_turns(block(w, 0), block(q, 0))]
        for j in range(PAIRS):
            s += [block(q, P * j)] if j not in (0, PAIRS // 2) else []
            s.append(block(k, P * j))
            if j + 1 < PAIRS:
                s.append(block(w, P * (j + 1)))
            if j == PAIRS // 2 - 1:
                s.append(block(q, P * (j + 1)))
            if j in (PAIRS // 2 - 1, PAIRS - 1):
                s += out_blocks(j // (PAIRS // 2))
        return s

    q1, k1, v1 = (np.concatenate([rows(f(f"L1_conv_W{x}_lb")), rows(f(f"L1_conv_W{x}_la"))], axis=1) for x in "qkv")
    wo = f("L1_conv_Wo").T
    s1 = heads(q1, k1, v1, lambda half: [block(wo, P * o) for o in range(CK)])
    q2, k2, v2 = np.split(f("L2_conv_qkv_w"), 3, axis=1)
    wp = f("L2_conv_proj_w")
    s2 = heads(q2, k2, v2, lambda half: [block(wp, P * o)[half:half + 1] for o in range(CK)])

    emb = f("L0_conv_rel_pos_emb")[..., 0].reshape(961, 64, 2, 2)
    rel = np.zeros((2, P, 64), np.float32)
    for i, name in enumerate(("L2_conv_rel_pos_h", "L2_conv_rel_pos_w")):
        table = f(name)[30::-1].T
        rel[i, 0:64, 0:31] = table
        rel[i, 64:128, 32:63] = table
    t = np.arange(N)
    hot = np.zeros((48, T), np.float32)
    hot[0:16] = np.tile(np.arange(16)[:, None] == t // SIDE, (1, B))
    hot[32:48] = np.tile(np.arange(16)[:, None] == t % SIDE, (1, B))
    i, j = np.arange(P)[:, None], np.arange(P)[None, :]
    mask = np.zeros((2, P, P), np.float32)
    mask[0][j > i] = -1e30
    mask[1][j < i] = -1e30
    c1 = f("L3_conv_core1").reshape(8, 8, 8, 2, 4)
    c2 = f("L3_conv_core2").reshape(8, 8, 8, 8)
    x = np.arange(P) % SIDE
    y = np.arange(P)[:, None] // SIDE + np.array([0, P // SIDE])
    d3 = np.arange(3)
    near_x = (x[:, None, None] - np.arange(16)[None, None] == d3[None, :, None] - 1).astype(np.float32)
    near_y = (y[:, None, :, None] - np.arange(16) == d3[None, :, None, None] - 1).astype(np.float32)
    bn = [np.concatenate([cols(f(f"L0_conv_q_{x}")), cols(f(f"L0_conv_v_{x}"))], axis=1)
          for x in ("gamma", "beta", "mean", "var")]
    return {
        "x": chunks(f("x").reshape(T, C)),
        "w": np.concatenate(s0 + s1 + s2),
        "ident": np.eye(P, dtype=np.float32),
        "gmat": np.kron(np.eye(P // GROUP), np.full((GROUP, GROUP), 1.0 / GROUP)).astype(np.float32),
        "mask": mask,
        "bn": np.concatenate(bn, axis=1),
        "bias": np.concatenate([cols(f("L2_conv_qkv_b")), cols(f("L2_conv_proj_b")), cols(f("L3_conv_bias"))], axis=1),
        "emb": emb.transpose(3, 1, 2, 0).reshape(P, 2, 961),
        "rel": rel,
        "hot": hot,
        "c0": f("L3_conv_core0").reshape(4, 8, 4).transpose(1, 2, 0).reshape(P),
        "c1": np.tile(c1.transpose(1, 4, 2, 3, 0).reshape(32, P), (3, 1)),
        "c2": np.tile(np.repeat(c2.transpose(2, 1, 0, 3).reshape(8, HALF), 4, axis=0), (3, 1)),
        "c3": f("L3_conv_core3").reshape(4, 8, 4).transpose(1, 0, 2).reshape(P),
        "taps": f("L3_conv_filters").reshape(9),
        "near_x": near_x.reshape(P, 48),
        "near_y": near_y.reshape(P, 96),
        "r2c": (np.arange(TT)[:, None] % 4 == np.arange(4)[None]).astype(np.float32),
    }


def kernel(**inputs):
    import concourse.bacc as _bacc
    from concourse.bass_utils import run_bass_kernel_spmd as _run

    nc = _bacc.Bacc("TRN2", target_bir_lowering=False, num_devices=1)
    arrays, args = {}, {}
    for name, a in lay_out(inputs).items():
        a = np.ascontiguousarray(a)
        arrays[f"in_{name}"] = a
        args[name] = nc.dram_tensor(f"in_{name}", a.shape, mybir.dt.from_np(a.dtype), kind="ExternalInput").ap()
    out = nc.dram_tensor("out_x", (CK, P, T), F32, kind="ExternalOutput").ap()
    build(nc, args, out)
    r = _run(nc, [arrays], core_ids=[0])
    return np.ascontiguousarray(r.results[0]["out_x"].reshape(C, T).T).reshape(B, SIDE, SIDE, C)
```
